# Optimizing a Trainium2 kernel written in Bass

```python
import numpy as np
import jax
import jax.numpy as jnp

def _softmax(x, axis=-1):
    return jax.nn.softmax(x, axis=axis)

def _gelu(x):
    return jax.nn.gelu(x, approximate=True)

def _silu(x):
    return jax.nn.silu(x)

def _sigmoid(x):
    return jax.nn.sigmoid(x)

def _layernorm(x, axis=-1, eps=1e-05):
    m = jnp.mean(x, axis=axis, keepdims=True)
    v = jnp.var(x, axis=axis, keepdims=True)
    return (x - m) / jnp.sqrt(v + eps)

def _scatter_add(tgt, idx, src, axis=0):
    return tgt.at[idx].add(src)

def _segment_sum(src, seg, n):
    return jax.ops.segment_sum(src, seg, n)
kernel_name = 'mk_adaln_d1_jaxref_r4_43a07d'

def setup_inputs(seed: int=0):
    np.random.seed(seed)
    _w = jnp.asarray

    def _L0_attn_setup():
        import jax, jax.numpy as jnp
        import numpy as np
        from jax.scipy.linalg import solve_triangular
        B, L, HID, NH = (2, 256, 256, 4)
        DK = DV = 64
        CONV_K, CHUNK, FIR_S_K, FIR_L_K = (4, 32, 3, 31)
        GATE_IN = HID + 3 * DV * 4 + DV * 4
        GATE_H = 2 * DV

        def _l2norm(x):
            return x * jax.lax.rsqrt(jnp.sum(x * x, -1, keepdims=True) + 1e-06)

        def _short_conv(x, w):
            c, k = w.shape
            y = jax.lax.conv_general_dilated(x.transpose(0, 2, 1), w[:, None, :], (1,), [(k - 1, 0)], feature_group_count=c)
            return jax.nn.silu(y.transpose(0, 2, 1))

        def _fir(x, f):
            b, l, h, d = x.shape
            k = f.shape[-1]
            xf = x.transpose(0, 2, 3, 1).reshape(b, h * d, l)
            y = jax.lax.conv_general_dilated(xf, f.reshape(h * d, 1, k), (1,), [(k - 1, 0)], feature_group_count=h * d)
            return y.reshape(b, h, d, l).transpose(0, 3, 1, 2)

        def _delta_rule(q, k, v, beta, chunk=CHUNK):
            b, h, l, dk = q.shape
            dv = v.shape[-1]
            n = l // chunk
            q = _l2norm(q)
            k = _l2norm(k)
            v = v * beta[..., None]
            kb = k * beta[..., None]
            rs = lambda t: t.reshape(b, h, n, chunk, -1)
            q, k, v, kb = map(rs, (q, k, v, kb))
            A = -jnp.tril(jnp.einsum('bhncd,bhned->bhnce', kb, k), -1)
            eye = jnp.eye(chunk, dtype=q.dtype)
            T = solve_triangular(eye - A, jnp.broadcast_to(eye, A.shape), lower=True)
            u = T @ v
            w = T @ kb
            mov = lambda t: jnp.moveaxis(t, 2, 0)

            def step(S, inp):
                qi, ki, ui, wi = inp
                attn = jnp.tril(qi @ ki.transpose(0, 1, 3, 2))
                u_i = ui - wi @ S
                o_i = qi @ S + attn @ u_i
                return (S + ki.transpose(0, 1, 3, 2) @ u_i, o_i)
            S0 = jnp.zeros((b, h, dk, dv), dtype=q.dtype)
            S, o = jax.lax.scan(step, S0, (mov(q), mov(k), mov(u), mov(w)))
            o = jnp.moveaxis(o, 0, 2).reshape(b, h, l, dv)
            return (o, S)

        def _gate(hidden, branches, W1, b1, W2, b2, temp, eps_floor):

            def stats(p):
                m = p.mean(-1, keepdims=True)
                r = jnp.sqrt(jnp.clip((p * p).mean(-1, keepdims=True), 1e-08))
                mx = p.max(-1, keepdims=True)
                return jnp.concatenate([jnp.broadcast_to(m, p.shape), jnp.broadcast_to(r, p.shape), jnp.broadcast_to(mx, p.shape)], -1)
            b, l, h, d = branches[0].shape
            hb = jnp.broadcast_to(hidden[:, :, None, :], (b, l, h, hidden.shape[-1]))
            head_in = jnp.concatenate([hb] + [stats(p) for p in branches] + list(branches), -1)
            hmid = jax.nn.gelu(head_in @ W1 + b1, approximate=False)
            logits = hmid @ W2 + b2
            t = jnp.clip(temp, 0.2, 10.0)[None, None, :, None]
            w = jax.nn.softmax(logits / t, -1)
            floor = jnp.clip(eps_floor, 1e-07, 0.1)[None, None]
            w = jnp.maximum(w, floor)
            return w / w.sum(-1, keepdims=True)
        key = jax.random.key(seed)
        ks = jax.random.split(key, 16)
        s = 0.02
        inp = {'x': jax.random.normal(ks[0], (B, L, HID), jnp.float32), 'Wq': jax.random.normal(ks[1], (HID, NH * DK), jnp.float32) * s, 'Wk': jax.random.normal(ks[2], (HID, NH * DK), jnp.float32) * s, 'Wv': jax.random.normal(ks[3], (HID, NH * DV), jnp.float32) * s, 'Wb': jax.random.normal(ks[4], (HID, NH), jnp.float32) * s, 'qc_w': jax.random.normal(ks[5], (NH * DK, CONV_K), jnp.float32) * 0.5, 'kc_w': jax.random.normal(ks[6], (NH * DK, CONV_K), jnp.float32) * 0.5, 'vc_w': jax.random.normal(ks[7], (NH * DV, CONV_K), jnp.float32) * 0.5, 'gW1': jax.random.normal(ks[10], (GATE_IN, GATE_H), jnp.float32) * s, 'gb1': jnp.zeros((GATE_H,), jnp.float32), 'gW2': jax.random.normal(ks[11], (GATE_H, 4), jnp.float32) * s, 'gb2': jnp.zeros((4,), jnp.float32), 'temp': jnp.ones((NH,), jnp.float32), 'eps_floor': jnp.full((NH, 4), 0.01, jnp.float32), 'onorm_w': jnp.ones((DV,), jnp.float32), 'Wo': jax.random.normal(ks[12], (NH * DV, HID), jnp.float32) * s}
        fs = jnp.zeros((NH, DV, FIR_S_K)).at[..., -1].set(1.0)
        fl = jnp.zeros((NH, DV, FIR_L_K)).at[..., -1].set(1.0)
        inp['fir_s'] = fs + s * jax.random.normal(ks[8], fs.shape, jnp.float32)
        inp['fir_l'] = fl + s * jax.random.normal(ks[9], fl.shape, jnp.float32)
        return inp
    _L0_attn_in = _L0_attn_setup()

    def _L0_ffn_setup():
        import jax, jax.numpy as jnp
        import numpy as np
        from jax.scipy.special import logsumexp
        EPS = 1e-06
        SINKHORN_ITERS = 8
        TEMPERATURE = 1.0

        def sinkhorn(logits):
            t = jnp.log(jnp.clip(logits, EPS)) / TEMPERATURE
            for _ in range(SINKHORN_ITERS):
                t = t - logsumexp(t, axis=-2, keepdims=True)
                t = t - logsumexp(t, axis=-1, keepdims=True)
            return jnp.exp(t)
        key = jax.random.key(seed)
        k1, k2, k3 = jax.random.split(key, 3)
        b, n, d, e, h = (4, 1024, 256, 8, 1)
        x = jax.random.normal(k1, (b, n, d), dtype=jnp.float32)
        gate_w = jax.random.normal(k2, (h, d, e), dtype=jnp.float32)
        experts = jax.random.normal(k3, (e, d, d), dtype=jnp.float32) * 0.02
        return {'x': x, 'gate_w': gate_w, 'experts': experts}
    _L0_ffn_in = _L0_ffn_setup()
    _L0_c = _w((lambda *s: np.random.randn(*s).astype(np.float32) * 0.05)(4, 256))
    _L0_wmod = _w((lambda *s: np.random.randn(*s).astype(np.float32) * 0.05)(256, 6 * 256) * 256 ** (-0.5))
    _d = {'L0_attn_x': _L0_attn_in['x'], 'L0_attn_Wq': _L0_attn_in['Wq'], 'L0_attn_Wk': _L0_attn_in['Wk'], 'L0_attn_Wv': _L0_attn_in['Wv'], 'L0_attn_Wb': _L0_attn_in['Wb'], 'L0_attn_qc_w': _L0_attn_in['qc_w'], 'L0_attn_kc_w': _L0_attn_in['kc_w'], 'L0_attn_vc_w': _L0_attn_in['vc_w'], 'L0_attn_fir_s': _L0_attn_in['fir_s'], 'L0_attn_fir_l': _L0_attn_in['fir_l'], 'L0_attn_gW1': _L0_attn_in['gW1'], 'L0_attn_gb1': _L0_attn_in['gb1'], 'L0_attn_gW2': _L0_attn_in['gW2'], 'L0_attn_gb2': _L0_attn_in['gb2'], 'L0_attn_temp': _L0_attn_in['temp'], 'L0_attn_eps_floor': _L0_attn_in['eps_floor'], 'L0_attn_onorm_w': _L0_attn_in['onorm_w'], 'L0_attn_Wo': _L0_attn_in['Wo'], 'L0_ffn_gate_w': _L0_ffn_in['gate_w'], 'L0_ffn_experts': _L0_ffn_in['experts'], 'L0_c': _L0_c, 'L0_wmod': _L0_wmod}
    _x0 = _d['L0_attn_x']
    _d['L0_attn_x'] = jax.random.normal(jax.random.fold_in(jax.random.key(seed), 1), (4, 2048, 256), dtype=_x0.dtype)
    del _x0
    return _d

def reference(L0_attn_x, L0_attn_Wq, L0_attn_Wk, L0_attn_Wv, L0_attn_Wb, L0_attn_qc_w, L0_attn_kc_w, L0_attn_vc_w, L0_attn_fir_s, L0_attn_fir_l, L0_attn_gW1, L0_attn_gb1, L0_attn_gW2, L0_attn_gb2, L0_attn_temp, L0_attn_eps_floor, L0_attn_onorm_w, L0_attn_Wo, L0_ffn_gate_w, L0_ffn_experts, L0_c, L0_wmod):

    def _L0_attn_ref(x, Wq, Wk, Wv, Wb, qc_w, kc_w, vc_w, fir_s, fir_l, gW1, gb1, gW2, gb2, temp, eps_floor, onorm_w, Wo):
        import jax, jax.numpy as jnp
        import numpy as np
        from jax.scipy.linalg import solve_triangular
        B, L, HID, NH = (2, 256, 256, 4)
        DK = DV = 64
        CONV_K, CHUNK, FIR_S_K, FIR_L_K = (4, 32, 3, 31)
        GATE_IN = HID + 3 * DV * 4 + DV * 4
        GATE_H = 2 * DV

        def _l2norm(x):
            return x * jax.lax.rsqrt(jnp.sum(x * x, -1, keepdims=True) + 1e-06)

        def _short_conv(x, w):
            c, k = w.shape
            y = jax.lax.conv_general_dilated(x.transpose(0, 2, 1), w[:, None, :], (1,), [(k - 1, 0)], feature_group_count=c)
            return jax.nn.silu(y.transpose(0, 2, 1))

        def _fir(x, f):
            b, l, h, d = x.shape
            k = f.shape[-1]
            xf = x.transpose(0, 2, 3, 1).reshape(b, h * d, l)
            y = jax.lax.conv_general_dilated(xf, f.reshape(h * d, 1, k), (1,), [(k - 1, 0)], feature_group_count=h * d)
            return y.reshape(b, h, d, l).transpose(0, 3, 1, 2)

        def _delta_rule(q, k, v, beta, chunk=CHUNK):
            b, h, l, dk = q.shape
            dv = v.shape[-1]
            n = l // chunk
            q = _l2norm(q)
            k = _l2norm(k)
            v = v * beta[..., None]
            kb = k * beta[..., None]
            rs = lambda t: t.reshape(b, h, n, chunk, -1)
            q, k, v, kb = map(rs, (q, k, v, kb))
            A = -jnp.tril(jnp.einsum('bhncd,bhned->bhnce', kb, k), -1)
            eye = jnp.eye(chunk, dtype=q.dtype)
            T = solve_triangular(eye - A, jnp.broadcast_to(eye, A.shape), lower=True)
            u = T @ v
            w = T @ kb
            mov = lambda t: jnp.moveaxis(t, 2, 0)

            def step(S, inp):
                qi, ki, ui, wi = inp
                attn = jnp.tril(qi @ ki.transpose(0, 1, 3, 2))
                u_i = ui - wi @ S
                o_i = qi @ S + attn @ u_i
                return (S + ki.transpose(0, 1, 3, 2) @ u_i, o_i)
            S0 = jnp.zeros((b, h, dk, dv), dtype=q.dtype)
            S, o = jax.lax.scan(step, S0, (mov(q), mov(k), mov(u), mov(w)))
            o = jnp.moveaxis(o, 0, 2).reshape(b, h, l, dv)
            return (o, S)

        def _gate(hidden, branches, W1, b1, W2, b2, temp, eps_floor):

            def stats(p):
                m = p.mean(-1, keepdims=True)
                r = jnp.sqrt(jnp.clip((p * p).mean(-1, keepdims=True), 1e-08))
                mx = p.max(-1, keepdims=True)
                return jnp.concatenate([jnp.broadcast_to(m, p.shape), jnp.broadcast_to(r, p.shape), jnp.broadcast_to(mx, p.shape)], -1)
            b, l, h, d = branches[0].shape
            hb = jnp.broadcast_to(hidden[:, :, None, :], (b, l, h, hidden.shape[-1]))
            head_in = jnp.concatenate([hb] + [stats(p) for p in branches] + list(branches), -1)
            hmid = jax.nn.gelu(head_in @ W1 + b1, approximate=False)
            logits = hmid @ W2 + b2
            t = jnp.clip(temp, 0.2, 10.0)[None, None, :, None]
            w = jax.nn.softmax(logits / t, -1)
            floor = jnp.clip(eps_floor, 1e-07, 0.1)[None, None]
            w = jnp.maximum(w, floor)
            return w / w.sum(-1, keepdims=True)
        b, l, _ = x.shape
        q = _short_conv(x @ Wq, qc_w).reshape(b, l, NH, DK)
        k = _short_conv(x @ Wk, kc_w).reshape(b, l, NH, DK)
        v = _short_conv(x @ Wv, vc_w).reshape(b, l, NH, DV)
        beta = jax.nn.sigmoid(x @ Wb)
        tr = lambda t: t.transpose(0, 2, 1, 3)
        delta_o, _ = _delta_rule(tr(q), tr(k), tr(v), beta.transpose(0, 2, 1))
        delta_o = tr(delta_o)
        branches = [_fir(v, fir_s), _fir(v, fir_l), delta_o, v]
        w = _gate(x, branches, gW1, gb1, gW2, gb2, temp, eps_floor)
        o = sum((w[..., i:i + 1] * branches[i] for i in range(4)))
        o = o * jax.lax.rsqrt((o * o).mean(-1, keepdims=True) + 1e-05) * onorm_w
        return o.reshape(b, l, NH * DV) @ Wo

    def _L0_ffn_ref(x, gate_w, experts):
        import jax, jax.numpy as jnp
        import numpy as np
        from jax.scipy.special import logsumexp
        EPS = 1e-06
        SINKHORN_ITERS = 8
        TEMPERATURE = 1.0

        def sinkhorn(logits):
            t = jnp.log(jnp.clip(logits, EPS)) / TEMPERATURE
            for _ in range(SINKHORN_ITERS):
                t = t - logsumexp(t, axis=-2, keepdims=True)
                t = t - logsumexp(t, axis=-1, keepdims=True)
            return jnp.exp(t)
        b, n, d = x.shape
        h, _, e = gate_w.shape
        m = n // e
        xh = x[:, None]
        gate_logits = jnp.einsum('bhnd,hde->bhne', xh, gate_w)
        gates = sinkhorn(gate_logits)
        g = jnp.swapaxes(gates, -1, -2)
        gv, idx = jax.lax.top_k(g, m)
        gate_values = jnp.swapaxes(gv, -1, -2)
        routed_indices = jnp.swapaxes(idx, -1, -2)
        hard_gates = (gate_values > 0.5).astype(x.dtype)
        bi = jnp.arange(b)[:, None, None, None]
        hi = jnp.arange(h)[None, :, None, None]
        routed = xh[bi, hi, routed_indices]
        experts4 = experts[:, None, :, :]
        out = jnp.einsum('bhmei,ehio->bhmeo', routed, experts4)
        out = out * hard_gates[..., None]
        y = jnp.zeros_like(xh).at[bi, hi, routed_indices].set(out)
        return y[:, 0]
    x = L0_attn_x
    mod = (_silu(L0_c) @ L0_wmod).reshape(L0_c.shape[0], 6, 1, -1)
    sa, ca, ga, sb, cb, gb = (mod[:, 0], mod[:, 1], mod[:, 2], mod[:, 3], mod[:, 4], mod[:, 5])
    ga = (2 * (ga >= 0) - 1) * jnp.maximum(jnp.abs(ga), 0.25)
    gb = (2 * (gb >= 0) - 1) * jnp.maximum(jnp.abs(gb), 0.25)
    h = _layernorm(x, axis=-1) * (1 + ca) + sa
    x = x + ga * _L0_attn_ref(h, L0_attn_Wq, L0_attn_Wk, L0_attn_Wv, L0_attn_Wb, L0_attn_qc_w, L0_attn_kc_w, L0_attn_vc_w, L0_attn_fir_s, L0_attn_fir_l, L0_attn_gW1, L0_attn_gb1, L0_attn_gW2, L0_attn_gb2, L0_attn_temp, L0_attn_eps_floor, L0_attn_onorm_w, L0_attn_Wo)
    h = _layernorm(x, axis=-1) * (1 + cb) + sb
    x = x + gb * _L0_ffn_ref(h, L0_ffn_gate_w, L0_ffn_experts)
    return x

_drawn_inputs = setup_inputs


def setup_inputs(seed=0):
    import zlib

    import numpy as np

    out = dict(_drawn_inputs(seed))
    spreads = {'L0_attn_gb1': (0.0, 0.8),
     'L0_attn_gb2': (0.0, 0.8),
     'L0_attn_temp': (1.0, 0.6),
     'L0_attn_eps_floor': (0.009999999776482582, 0.2),
     'L0_attn_onorm_w': (1.0, 0.6)}
    factors = {'L0_attn_Wq': 3.758,
     'L0_attn_Wk': 3.733,
     'L0_attn_Wb': 8.0,
     'L0_attn_qc_w': 3.682,
     'L0_attn_kc_w': 3.685,
     'L0_attn_gW1': 8.0,
     'L0_attn_gW2': 8.0}
    for name, (base, spread) in spreads.items():
        noise = np.random.default_rng([zlib.crc32(name.encode()), seed]).standard_normal(out[name].shape)
        drawn = base * np.exp(spread * noise) if base else spread * noise
        out[name] = jnp.asarray(drawn.astype(out[name].dtype))
    for name, factor in factors.items():
        out[name] = (out[name] * factor).astype(out[name].dtype)
    return out
```

```python
from contextlib import ExitStack

import concourse.bass as bass
from concourse import mybir

ALU = mybir.AluOpType
ACT = mybir.ActivationFunctionType
F32 = mybir.dt.float32
U32 = mybir.dt.uint32
AX = mybir.AxisListType.X
ENG = mybir.EngineType

P = 128
B, L, C, H = 4, 2048, 256, 4
D = C // H
TOK = B * L
TILES = TOK // P
CH = 32
TPB = TILES // B
UNITS = TOK // CH
CPB = L // CH
KT = C // P
WIN = 512
TAPS, FIRL, FIRS = 4, 31, 3
BLK = 64
NBLK = TOK // BLK
SPAN = BLK + FIRL - 1
RW = SPAN + BLK
NBR = 4
NE = 8
CAP = L // NE
EPS_LN, EPS_L2, EPS_RMS = 1e-5, 1e-6, 1e-5


class Sems:

    def __init__(self, nc, n):
        self.plain = (nc.sync, nc.gpsimd)
        self.free = [[nc.alloc_semaphore(f"s{i}"), 1] for i in range(n)]
        engines = (nc.sync, nc.scalar, nc.tensor, nc.vector, nc.gpsimd)
        for i, (sem, _) in enumerate(self.free):
            engines[i % 5].sem_inc(sem, 1)
        nc.all_engine_barrier()
        self.soft = [[nc.alloc_semaphore(f"pool_dma{i}"), 0] for i in range(8)]

    def loop(self, turns):
        return Loop(self, turns)


class Loop:

    def __init__(self, sems, turns):
        self.sems, self.turns, self.it, self.steps = sems, turns, 0, []

    def step(self, per_turn=1):
        s = Step(self, self.sems.free.pop(0), per_turn)
        self.steps.append(s)
        return s

    def dma(self, n=1):
        s = self.step(16 * n)
        s.unit = 16
        return s

    def pool_dma(self, n=1):
        s = Step(self, self.sems.soft.pop(0), 16 * n)
        s.unit = 16
        return s

    def close(self):
        for s in self.steps:
            s.slot[1] += s.per_turn * self.turns
            self.sems.free.append(s.slot)


class Pair:

    def __init__(self, sems, turns, n=1, pool=False):
        self.loop = sems.loop(turns // 2)
        make = self.loop.pool_dma if pool else self.loop.dma
        self.of = [make(n), make(n)]

    def by(self, instruction, par):
        return self.of[par].by(instruction)

    def wait(self, engine, par, half):
        self.of[par].wait(engine, t=half)

    def free(self, engine, par, half):
        self.of[par].back(engine, half, 1)

    def wait_all(self, engine):
        for s in self.of:
            s.wait_all(engine)

    def close(self):
        self.loop.close()


class Step:
    def __init__(self, loop, slot, per_turn):
        self.loop, self.slot, self.per_turn, self.unit = loop, slot, per_turn, 1
        self.sem, self.base = slot

    def by(self, instruction):
        return instruction.then_inc(self.sem, self.unit)

    def until(self, engine, t, k, alone=False):
        count = t * self.per_turn + (self.base + k)
        if not isinstance(t, int) and (alone or engine in self.loop.sems.plain):
            count = engine.snap(engine.to_reg(count))
            engine.wait_ge(self.sem, self.base + max(k, 0))
        engine.wait_ge(self.sem, count)

    def wait(self, engine, k=None, t=None, alone=False):
        self.until(engine, self.loop.it if t is None else t, self.per_turn if k is None else k, alone)

    def wait_last(self, engine):
        self.back(engine, self.loop.it, 1)

    def back(self, engine, t, n, alone=False):
        if not isinstance(t, int) or t >= n:
            self.until(engine, t, (1 - n) * self.per_turn, alone)

    def wait_all(self, engine):
        engine.wait_ge(self.sem, self.base + self.per_turn * self.loop.turns)


def weave(*stages):
    stages = list(stages)
    while stages:
        for s in list(stages):
            if next(s, stages) is stages:
                stages.remove(s)


def pipeline(nc, turns, first, second):
    weave(first(0, 0, 0))
    weave(second(0, 0, 0), first(1, 1, 0))
    with nc.Fori(1, turns // 2) as i:
        weave(second(i * 2 - 1, 1, i - 1), first(i * 2, 0, i))
        weave(second(i * 2, 0, i), first(i * 2 + 1, 1, i))
    weave(second(turns - 1, 1, turns // 2 - 1))


def build(nc, a, out, dbg=()):
    pe, dve, act, pool, sp = nc.tensor, nc.vector, nc.scalar, nc.gpsimd, nc.sync
    sems = Sems(nc, 90)
    whole = ExitStack()

    def dram(name, shape, dt=F32):
        kind = "ExternalOutput" if name in dbg else "Internal"
        return nc.dram_tensor(name, list(shape), dt, kind=kind).ap()

    hT_d = dram("hT_d", [KT, P, TOK])
    qkv_d = dram("qkv_d", [3, TOK, C])
    beta_d = dram("beta_d", [H, TOK])
    taps_d = dram("taps_d", [C, 2, RW])
    fir_d = dram("fir_d", [2, TOK, C])
    gram_d = dram("gram_d", [UNITS, P, CH])
    tinv_d = dram("tinv_d", [UNITS, P, CH])
    delta_d = dram("delta_d", [TOK, C])
    x2_d = dram("x2_d", [TOK, C])
    h2_d = dram("h2_d", [TOK, C])
    key_d = dram("key_d", [TOK * NE, 1])
    routed_d = dram("routed_d", [B * CAP * NE, C])

    def sb(stack, name, shape, dt=F32):
        return stack.enter_context(nc.sbuf_tensor(name, list(shape), dt))

    def ps(stack, name, shape):
        return stack.enter_context(nc.psum_tensor(name, list(shape), F32))

    def barrier():
        nc.all_engine_barrier()

    ident = sb(whole, "ident", [P, P])
    ones = sb(whole, "ones", [P, P])
    blockdiag = sb(whole, "blockdiag", [P, P])
    causal = sb(whole, "causal", [P, P])
    parity = sb(whole, "parity", [P, 2])
    rows = sb(whole, "rows", [P, 4, B, C])
    scT = sb(whole, "scT", [P, B, 2, KT])
    mean = sb(whole, "mean", [P, TILES])
    rstd = sb(whole, "rstd", [P, TILES])
    gates = sb(whole, "gates", [P, TPB, B, NE])

    with ExitStack() as st:
        p = sems.loop(1)
        cT = sb(st, "cT", [P, KT, B])
        cs = sb(st, "cs", [P, KT, B])
        crep = sb(st, "crep", [P, KT, B, P])
        wmod = sb(st, "wmod", [P, KT, 6 * C])
        xs = sb(st, "xs", [P, TILES, C])
        bst = sb(st, "bst", [P, TILES, 6])
        ta = sb(st, "ta", [P, TILES])
        tb = sb(st, "tb", [P, TILES])
        sgn = sb(st, "sgn", [P, 2, B, C])
        mag = sb(st, "mag", [P, 2, B, C])
        tapr = sb(st, "tapr", [P, KT, 2, RW])
        pcol = ps(st, "pcol", [P, 2, KT, B])
        prow = ps(st, "prow", [P, 2, 512])

        s_c, s_x, s_tap, s_tapz, s_tapo = p.dma(2), p.dma(4), p.dma(2 * KT), p.step(), p.dma()
        for src, n in ((a["cT"], 0), (a["wmod"], 1)):
            s_c.by(sp.dma_start((cT if n == 0 else wmod)[:, :, :], src.rearrange("(k p) n -> p k n", p=P)))
        for b in range(4):
            nt = TILES // 4
            s_x.by(sp.dma_start(xs[:, nt * b:nt * (b + 1), :],
                                a["x"][b * nt * P:(b + 1) * nt * P, :].rearrange("(t p) c -> p t c", p=P)))
        s_tapz.by(dve.memset(tapr[:, :, :, :], 0.0))
        s_tapz.wait(act)
        for k in range(KT):
            s_tap.by(act.dma_start(tapr[:, k, 0, BLK - 1:BLK - 1 + FIRL], a["fir_l"][k * P:(k + 1) * P, :]))
            s_tap.by(act.dma_start(tapr[:, k, 1, BLK - 1 + FIRL - FIRS:BLK - 1 + FIRL], a["fir_s"][k * P:(k + 1) * P, :]))
        s_tap.wait(act)
        s_tapo.by(act.dma_start(taps_d.rearrange("(k p) f w -> p k f w", p=P), tapr[:, :, :, :]))

        s_sel = p.step(4 + 3 * H)
        n_sel = 0

        def in_order(ins):
            nonlocal n_sel
            n_sel += 1
            s_sel.by(ins)
            s_sel.wait(pool, n_sel)

        in_order(pool.memset(ones[:, :], 1.0))
        in_order(pool.affine_select(out=ident[:, :], in_=ones[:, :], pattern=[[-1, P]], compare_op=ALU.is_equal,
                                    fill=0.0, base=0, channel_multiplier=1))
        in_order(pool.memset(parity[:, :], 0.0))
        in_order(pool.memset(blockdiag[:, :], 0.0))
        pool.wait_ge(s_sel.sem, s_sel.base + n_sel)
        causal_z = p.step()
        causal_z.by(pool.memset(causal[:, :], 0.0))
        causal_z.wait(pool)
        for h in range(H):
            r = slice(CH * h, CH * (h + 1))
            in_order(pool.memset(parity[r, h % 2:h % 2 + 1], 1.0))
            in_order(pool.memset(blockdiag[r, r], 1.0))
            in_order(pool.affine_select(out=causal[r, r], in_=ones[r, 0:CH], pattern=[[1, CH]],
                                        compare_op=ALU.is_ge, fill=0.0, base=0, channel_multiplier=-1))

        s_silu, s_rep, s_col, s_cole = p.step(), p.step(), p.step(), p.step(2)
        s_c.wait(act)
        s_silu.by(act.activation(cs[:, :, :], cT[:, :, :], ACT.Silu))
        s_silu.wait(dve)
        s_rep.by(dve.tensor_copy(crep[:, :, :, :], cs[:, :, :].unsqueeze(3).broadcast_to([P, KT, B, P])))
        s_c.wait(pe)
        s_silu.wait(pe)
        for w in range(2):
            for m in range(KT):
                for k in range(KT):
                    i = pe.matmul(pcol[:, w, m, :], wmod[:, k, w * C + m * P:w * C + (m + 1) * P], cs[:, k, :],
                                  start=(k == 0), stop=(k == KT - 1))
        s_col.by(i)
        s_col.wait(dve)
        for w in range(2):
            s_cole.by(dve.tensor_scalar(scT[:, :, w, :], pcol[:, w, :, :].rearrange("p m b -> p b m"),
                                        float(w), None, ALU.add))
        s_rep.wait(pe)
        s_row, s_rowe = p.step(2 * B), p.step(2 * B)
        for b in range(B):
            for g in range(2):
                n = b * 2 + g
                if n >= 2:
                    s_rowe.wait(pe, n - 1)
                for k in range(KT):
                    i = pe.matmul(prow[:, n % 2, :], crep[:, k, b, :], wmod[:, k, 2 * C + g * 512:2 * C + (g + 1) * 512],
                                  start=(k == 0), stop=(k == KT - 1))
                s_row.by(i)
                s_row.wait(dve, n + 1)
                s_rowe.by(dve.tensor_copy(rows[:, 2 * g:2 * g + 2, b, :], prow[:, n % 2, :].rearrange("p (r c) -> p r c", r=2)))
        s_sg, s_ab, s_rfin = p.step(4), p.step(2), p.step(3)
        s_rowe.wait(dve)
        for n, r in enumerate((0, 3)):
            s_sg.by(dve.tensor_scalar(sgn[:, n, :, :], rows[:, r, :, :], 0.0, 2.0, ALU.is_ge, ALU.mult))
            g = rows[:, r, :, :].rearrange("p b c -> p (b c)")
            m = mag[:, n, :, :].rearrange("p b c -> p (b c)")
            s_sg.by(dve.scalar_tensor_tensor(m, g, -1.0, g, ALU.mult, ALU.max))
        s_sg.wait(dve)
        for n in range(2):
            s_ab.by(dve.tensor_scalar(mag[:, n, :, :], mag[:, n, :, :], 0.25, None, ALU.max))
        s_ab.wait(dve)
        for n, r in enumerate((0, 3)):
            s_rfin.by(dve.scalar_tensor_tensor(rows[:, r, :, :].rearrange("p b c -> p (b c)"),
                                               sgn[:, n, :, :].rearrange("p b c -> p (b c)"), 1.0,
                                               mag[:, n, :, :].rearrange("p b c -> p (b c)"), ALU.subtract, ALU.mult))
        s_rfin.by(dve.tensor_scalar(rows[:, 2, :, :], rows[:, 2, :, :], 1.0, None, ALU.add))

        s_x.wait(dve)
        q = sems.loop(TILES // 4)
        s_b = q.step()
        with nc.Fori(0, TILES // 4, engines=[ENG.DVE]) as i:
            for n in range(4):
                last = dve.bn_stats(bst[:, bass.ds(i * 4 + n, 1), :].rearrange("p a s -> p (a s)"),
                                    xs[:, bass.ds(i * 4 + n, 1), :].rearrange("p a c -> p (a c)"))
            s_b.by(last)
        s_b.wait_all(dve)
        s_v = p.step(7)
        v = 0

        def chain(ins):
            nonlocal v
            v += 1
            s_v.by(ins)
            s_v.wait(dve, v)

        chain(dve.tensor_tensor(mean[:, :], bst[:, :, 1], bst[:, :, 4], ALU.add))
        chain(dve.tensor_tensor(ta[:, :], bst[:, :, 1], bst[:, :, 4], ALU.subtract))
        chain(dve.tensor_tensor(tb[:, :], bst[:, :, 2], bst[:, :, 5], ALU.add))
        chain(dve.tensor_tensor(ta[:, :], ta[:, :], ta[:, :], ALU.mult))
        chain(dve.tensor_scalar(tb[:, :], tb[:, :], 1.0 / C, EPS_LN, ALU.mult, ALU.add))
        chain(dve.scalar_tensor_tensor(tb[:, :], ta[:, :], 0.25, tb[:, :], ALU.mult, ALU.add))
        chain(dve.tensor_scalar(mean[:, :], mean[:, :], -0.5, None, ALU.mult))
        s_sq, s_rs = p.step(), p.step()
        s_v.wait(act)
        s_sq.by(act.activation(ta[:, :], tb[:, :], ACT.Sqrt))
        s_sq.wait(dve)
        s_rs.by(dve.reciprocal(rstd[:, :], ta[:, :]))
        s_tapo.wait(act)
        barrier()
        q.close()
        p.close()

    with ExitStack() as st:
        wqkv = sb(st, "wqkv", [P, KT, 3, C])
        wb = sb(st, "wb", [P, KT, H])
        cw = sb(st, "cw", [P, 6, TAPS])
        proj = sb(st, "proj", [P, 6, TAPS - 1 + L])
        xw = sb(st, "xw", [P, 2, WIN // P, C])
        xn = sb(st, "xn", [P, 2, WIN // P, C])
        cur = sb(st, "cur", [P, 2, KT])
        hT = sb(st, "hT", [P, KT, WIN])
        acc = sb(st, "acc", [P, 2, WIN])
        sil = sb(st, "sil", [P, 3, WIN])
        tm = sb(st, "tm", [P, WIN // P, 3, C])
        bT = sb(st, "bT", [H, WIN])
        pT = ps(st, "pT", [P, KT, WIN])
        pP = ps(st, "pP", [P, 3, WIN])
        pB = ps(st, "pB", [P, WIN])
        pK = ps(st, "pK", [P, 2, WIN])
        NM = 6

        p = sems.loop(1)
        s_w, s_z = p.dma(7), p.step()
        for n, w in enumerate(("Wq", "Wk", "Wv")):
            s_w.by(sp.dma_start(wqkv[:, :, n, :], a[w].rearrange("(k p) n -> p k n", p=P)))
        s_w.by(sp.dma_start(wb[:, :, :], a["Wb"].rearrange("(k p) n -> p k n", p=P)))
        for n, w in enumerate(("qc", "kc", "vc")):
            s_w.by(sp.dma_start(cw[:, 2 * n:2 * n + 2, :], a[w].rearrange("(k p) n -> p k n", p=P)))
        s_z.by(dve.memset(proj[:, :, 0:TAPS - 1], 0.0))
        for e in (pe, act, dve):
            s_w.wait(e)
        s_z.wait(dve)

        q = sems.loop(TOK // WIN)
        NW = L // WIN
        s_ld, s_cur, s_ln = q.dma(), q.step(), q.step(4)
        s_tr, s_ht, s_hto = q.step(), q.step(2), q.dma()
        s_pr, s_bt, s_be, s_bo = q.step(NM), q.step(), q.step(), q.dma()
        s_ev, s_cv, s_si, s_tt, s_te, s_tmo = (q.step(NM), q.step(3 * NM), q.step(NM), q.step(NM), q.step(NM), q.dma(3))
        with nc.Fori(0, B) as b, nc.Fori(0, NW) as j:
            q.it = b * NW + j
            s_ln.wait_last(sp)
            s_ld.by(sp.dma_start(xw[:, 0, :, :], a["x"][bass.ds(q.it * WIN, WIN), :].rearrange("(t p) c -> p t c", p=P)))
            s_ht.wait_last(dve)
            s_cur.by(dve.tensor_copy(cur[:, :, :], scT[:, bass.ds(b, 1), :, :].rearrange("p a w k -> p (a w) k")))
            s_ld.wait(dve)
            s_tr.wait_last(dve)
            for t in range(4):
                s_ln.by(dve.tensor_scalar(xn[:, 0, t, :], xw[:, 0, t, :], mean[:, bass.ds(q.it * 4 + t, 1)],
                                          rstd[:, bass.ds(q.it * 4 + t, 1)], ALU.add, ALU.mult))
            s_ln.wait(pe)
            s_ht.wait_last(pe)
            for k in range(KT):
                for t in range(4):
                    i = pe.transpose(pT[:, k, t * P:(t + 1) * P], xn[:, 0, t, k * P:(k + 1) * P], ident[:, :])
            s_tr.by(i)
            s_tr.wait(act)
            s_cur.wait(act)
            s_hto.wait_last(act)
            s_pr.wait_last(act)
            s_bt.wait_last(act)
            for k in range(KT):
                s_ht.by(act.activation(hT[:, k, :], pT[:, k, :], ACT.Identity, bias=cur[:, 0, k:k + 1], scale=cur[:, 1, k:k + 1]))
            s_ht.wait(sp)
            s_hto.by(sp.dma_start(hT_d.rearrange("k p t -> p k t")[:, :, bass.ds(q.it * WIN, WIN)], hT[:, :, :]))
            s_ht.wait(pe)

            def project(m):
                if m >= 3:
                    s_ev.wait(pe, m - 2)
                else:
                    s_ev.wait_last(pe)
                for k in range(KT):
                    i = pe.matmul(pP[:, m % 3, :], wqkv[:, k, m // 2, (m % 2) * P:(m % 2 + 1) * P], hT[:, k, :],
                                  start=(k == 0), stop=(k == KT - 1))
                s_pr.by(i)

            def convolve(m):
                s_pr.wait(act, m + 1)
                if m >= 2:
                    s_si.wait(act, m - 1)
                act.activation(proj[:, m, bass.ds(j * WIN + TAPS - 1, WIN)], pP[:, m % 3, :], ACT.Copy)
                s_ev.by(act.activation(acc[:, m % 2, :], pP[:, m % 3, :], ACT.Copy, scale=cw[:, m, TAPS - 1:TAPS]))
                s_ev.wait(dve, m + 1)
                for n, tap in enumerate((2, 1, 0)):
                    if n:
                        s_cv.wait(dve, 3 * m + n)
                    s_cv.by(dve.scalar_tensor_tensor(acc[:, m % 2, :], proj[:, m, bass.ds(j * WIN + tap, WIN)],
                                                     cw[:, m, tap:tap + 1], acc[:, m % 2, :], ALU.mult, ALU.add))

            def silu(m):
                s_cv.wait(act, 3 * m + 3)
                if m >= 3:
                    s_tt.wait(act, m - 2)
                else:
                    s_tt.wait_last(act)
                s_si.by(act.activation(sil[:, m % 3, :], acc[:, m % 2, :], ACT.Silu))

            def to_tokens(m):
                s_si.wait(pe, m + 1)
                if m >= 2:
                    s_te.wait(pe, m - 1)
                else:
                    s_te.wait_last(pe)
                for t in range(4):
                    i = pe.transpose(pK[:, m % 2, t * P:(t + 1) * P], sil[:, m % 3, t * P:(t + 1) * P], ident[:, :])
                s_tt.by(i)

            def keep_tokens(m, e):
                s_tt.wait(e, m + 1)
                if m == 0:
                    s_tmo.wait_last(e)
                dst = tm[:, :, m // 2, (m % 2) * P:(m % 2 + 1) * P]
                src = pK[:, m % 2, :].rearrange("p (t c) -> p t c", t=4)
                s_te.by(e.tensor_copy(dst, src))

            for m in range(3):
                project(m)
            s_be.wait_last(pe)
            for k in range(KT):
                i = pe.matmul(pB[0:H, :], wb[:, k, :], hT[:, k, :], start=(k == 0), stop=(k == KT - 1))
            s_bt.by(i)
            for m in range(NM + 2):
                if m < NM:
                    convolve(m)
                if 1 <= m <= NM:
                    silu(m - 1)
                    if 3 <= m + 2 < NM:
                        project(m + 2)
                    to_tokens(m - 1)
                if m >= 2:
                    keep_tokens(m - 2, dve)
            s_bt.wait(act)
            s_bo.wait_last(act)
            s_be.by(act.activation(bT[:, :], pB[0:H, :], ACT.Copy))
            s_be.wait(act)
            s_bo.by(act.dma_start(beta_d[:, bass.ds(q.it * WIN, WIN)], bT[:, :]))
            for n in range(3):
                s_te.wait(sp, 2 * n + 2)
                s_tmo.by(sp.dma_start(qkv_d[n, bass.ds(q.it * WIN, WIN), :].rearrange("(t p) c -> p t c", p=P), tm[:, :, n, :]))
        for s in (s_hto, s_bo, s_tmo):
            s.wait_all(sp)
        barrier()
        q.close()
        p.close()
    hold = ExitStack()
    rnorm = sb(hold, "rnorm", [P, 2, UNITS])
    betac = sb(hold, "betac", [P, UNITS])
    with ExitStack() as st:
        NU = 8
        turns = UNITS // NU
        kq = sb(st, "kq", [P, 2, 2, NU, D])
        sqr = sb(st, "sqr", [P, 2, NU, D])
        ssum = sb(st, "ssum", [P, 2, NU])
        root = sb(st, "root", [P, 2, NU])
        kn = sb(st, "kn", [P, NU, D])
        kT2 = sb(st, "kT2", [D, NU, P])
        gr = sb(st, "gr", [P, 2, NU, CH])
        bu = sb(st, "bu", [P, 2, H, CH])
        pk2 = ps(st, "pk2", [P, NU, P])
        pg2 = ps(st, "pg2", [P, NU, P])

        p = sems.loop(1)
        s_bl, s_sg, s_bt, s_bc = p.dma(2 * H), p.step(), p.step(), p.step()
        for h in range(H):
            for w in range(2):
                s_bl.by(sp.dma_start(bu[:, w, h, :], beta_d[h, w * TOK // 2:(w + 1) * TOK // 2].rearrange("(u i) -> u i", i=CH)))
        s_bl.wait(act)
        s_sg.by(act.activation(bu[:, :, :, :], bu[:, :, :, :], ACT.Sigmoid))
        s_sg.wait(pe)
        for w in range(2):
            i = pe.transpose(pk2[:, w, :], bu[:, w, :, :].rearrange("p h i -> p (h i)"), ident[:, :])
        s_bt.by(i)
        s_bt.wait(dve)
        s_bc.by(dve.tensor_copy(betac[:, :], pk2[:, 0:2, :].rearrange("p w u -> p (w u)")))
        s_bc.wait(pe)

        q = sems.loop(turns)
        s_ld, s_go = Pair(sems, turns, 2 * H), Pair(sems, turns)
        s_n, s_rt, s_rn, s_kn = q.step(3), q.step(), q.step(), q.step()
        s_tr, s_kt, s_gm, s_ge = q.step(), q.step(2), q.step(), q.step(H)

        def norms(t, par, half):
            s_kn.back(sp, t, 2)
            for h in range(H):
                for n in range(2):
                    src = qkv_d[n, bass.ds(t * NU * CH, NU * CH), h * D:(h + 1) * D].rearrange("(u i) d -> i u d", i=CH)
                    s_ld.by(sp.dma_start(kq[h * CH:(h + 1) * CH, par, n, :, :], src), par)
            s_ld.wait(dve, par, half)
            s_n.by(dve.tensor_tensor(sqr[:, :, :, :], kq[:, par, :, :, :], kq[:, par, :, :, :], ALU.mult))
            s_n.wait(dve, 1, t=t)
            s_n.by(dve.tensor_reduce(ssum[:, :, :], sqr[:, :, :, :], AX, ALU.add))
            s_n.wait(dve, 2, t=t)
            s_n.by(dve.tensor_scalar(ssum[:, :, :], ssum[:, :, :], EPS_L2, None, ALU.add))
            yield
            s_n.wait(act, 3, t=t)
            s_rt.by(act.activation(root[:, :, :], ssum[:, :, :], ACT.Sqrt))
            s_rt.wait(dve, t=t)
            s_rn.by(dve.reciprocal(rnorm[:, :, bass.ds(t * NU, NU)], root[:, :, :]))
            s_rn.wait(dve, t=t)
            s_tr.back(dve, t, 1)
            s_kn.by(dve.tensor_tensor(kn[:, :, :], kq[:, par, 1, :, :],
                                      rnorm[:, 1, bass.ds(t * NU, NU)].unsqueeze(2).broadcast_to([P, NU, D]), ALU.mult))

        def gram(t, par, half):
            s_kt.back(pe, t, 1, alone=True)
            s_kn.wait(pe, t=t, alone=True)
            for u in range(NU):
                i = pe.transpose(pk2[0:D, u, :], kn[:, u, :], ident[:, :])
            s_tr.by(i)
            s_tr.wait(act, t=t)
            s_gm.back(act, t, 1)
            for w in range(2):
                s_kt.by(act.activation(kT2[:, 4 * w:4 * w + 4, :], pk2[0:D, 4 * w:4 * w + 4, :], ACT.Copy))
            yield
            s_kt.wait(pe, t=t)
            s_ge.back(pe, t, 1)
            for u in range(NU):
                i = pe.matmul(pg2[:, u, :], kT2[:, u, :], kT2[:, u, :], start=True, stop=True)
            s_gm.by(i)
            s_go.free(act, par, half)
            s_go.free(dve, par, half)
            for h in range(H):
                e = act if h % 2 else dve
                s_gm.wait(e, t=t)
                r = slice(h * CH, (h + 1) * CH)
                if h % 2:
                    s_ge.by(act.activation(gr[r, par, :, :], pg2[r, :, r], ACT.Copy))
                else:
                    s_ge.by(dve.tensor_copy(gr[r, par, :, :], pg2[r, :, r]))
            s_ge.wait(act, t=t)
            s_go.by(act.dma_start(gram_d[bass.ds(t * NU, NU)].rearrange("u p j -> p u j"), gr[:, par, :, :]), par)

        pipeline(nc, turns, norms, gram)
        s_go.wait_all(sp)
        barrier()
        s_go.close()
        s_ld.close()
        q.close()
        p.close()

    with ExitStack() as st:
        QC, G = 64, 4
        NS = UNITS * H // P
        vwin = sb(st, "vwin", [SPAN, NBLK, QC])
        band = sb(st, "band", [SPAN, 2, G, 2, BLK])
        vst = sb(st, "vst", [SPAN, 2, G, NBLK])
        fo = sb(st, "fo", [NBLK, 2, 2, BLK, QC])
        amat = sb(st, "amat", [P, NS, CH, CH])
        tinv = sb(st, "tinv", [P, NS, CH, CH])
        prod = sb(st, "prod", [P, NS, CH * CH // 4])
        bs = sb(st, "bs", [P, NS, CH])
        pf = ps(st, "pf", [NBLK, 2, G, 2, BLK])

        p = sems.loop(1)
        s_a, s_sg, s_i = p.dma(1 + H), p.step(), p.step(3)
        s_a.by(act.dma_start(amat[:, :, :, :].rearrange("p s i j -> p (s i j)"),
                             gram_d.rearrange("u (h i) j -> (u h i j)", h=H).rearrange("(p x) -> p x", p=P)))
        for h in range(H):
            s_a.by(act.dma_start(bs[:, :, :].rearrange("p (u h) i -> p u h i", h=H)[:, :, h, :],
                                 beta_d[h].rearrange("(p u i) -> p u i", p=P, i=CH)))
        s_i.by(dve.memset(tinv[:, :, :, :], 0.0))
        s_a.wait(act)
        s_sg.by(act.activation(bs[:, :, :], bs[:, :, :], ACT.Sigmoid))
        s_i.wait(dve, 1)
        s_i.by(dve.memset(tinv[:, :, :, :].rearrange("p s i j -> p s (i j)")[:, :, 0:CH * CH:CH + 1], 1.0))
        s_sg.wait(dve)
        s_i.by(dve.tensor_tensor(amat[:, :, :, :], amat[:, :, :, :],
                                 bs[:, :, :].unsqueeze(3).broadcast_to([P, NS, CH, CH]), ALU.mult))
        s_i.wait(dve)
        s_f = p.step(2 * (CH - 1))
        for j in range(CH - 1):
            nc_, ni = j + 1, CH - 1 - j
            col = amat[:, :, j + 1:, j].unsqueeze(2).broadcast_to([P, NS, nc_, ni])
            row = tinv[:, :, 0:nc_, j].unsqueeze(3).broadcast_to([P, NS, nc_, ni])
            tmp = prod[:, :, 0:nc_ * ni].rearrange("p s (c i) -> p s c i", c=nc_)
            s_f.by(dve.tensor_tensor(tmp, col, row, ALU.mult))
            s_f.wait(dve, 2 * j + 1)
            s_f.by(dve.tensor_tensor(tinv[:, :, 0:nc_, j + 1:], tinv[:, :, 0:nc_, j + 1:], tmp, ALU.subtract))
            s_f.wait(dve, 2 * j + 2)

        s_vz, s_v = p.step(B), p.dma(4 * (B + B))
        GT = QC // G
        q = sems.loop(4 * GT // 2)
        s_bd, s_cp, s_mm, s_ev = [[make() for _ in range(2)] for make in (q.dma, q.step, q.step, q.step)]
        s_fo = Pair(sems, 4, 2)
        for b in range(B):
            s_vz.by(pool.memset(vwin[0:FIRL - 1, b * (NBLK // B), :], 0.0))
        s_vz.wait(sp)
        s_vz.wait(pool)
        for c4 in range(C // QC):
            c0 = c4 * QC
            if c4:
                for par in range(2):
                    s_cp[par].wait(sp, t=c4 * GT // 2 - 1)
            for b in range(B):
                vb = qkv_d[2, b * L:(b + 1) * L, c0:c0 + QC]
                nb = NBLK // B
                wins = bass.AP(vb.tensor, vb.offset + (BLK - FIRL + 1) * C, [[C, SPAN], [BLK * C, nb - 1], [1, QC]])
                s_v.by(sp.dma_start(vwin[:, b * nb + 1:(b + 1) * nb, :], wins))
                s_v.by(sp.dma_start(vwin[FIRL - 1:SPAN, b * nb, :], vb[0:BLK, :]))
            s_v.wait(pool, 16 * 8 * (c4 + 1))
            s_fo.free(act, c4 % 2, c4 // 2)
            with nc.Fori(0, GT // 2, engines=[ENG.SP, ENG.PE, ENG.Activation, ENG.Pool]) as i:
                for par in range(2):
                    t2 = i + c4 * GT // 2
                    s_mm[par].back(sp, t2, 1)
                    cb = (i * (2 * G) + (c0 + par * G)) * (2 * RW)
                    src = bass.AP(taps_d.tensor, cb, [[1, SPAN], [RW, 2 * G], [1, BLK]])
                    s_bd[par].by(sp.dma_start(band[:, par, :, :, :].rearrange("p g f t -> p (g f) t"), src))
                    s_mm[par].back(pool, t2, 1)
                    s_cp[par].by(pool.tensor_copy(vst[:, par, :, :], vwin[:, :, bass.ds((i * 2 + par) * G, G)].rearrange("p n g -> p g n")))
                    s_cp[par].wait(pe, t=t2)
                    s_bd[par].wait(pe, t=t2)
                    s_ev[par].back(pe, t2, 1)
                    for g in range(G):
                        mm = pe.matmul(pf[:, par, g, :, :], vst[:, par, g, :], band[:, par, g, :, :], start=True, stop=True)
                    s_mm[par].by(mm)
                    s_mm[par].wait(act, t=t2)
                    s_ev[par].by(act.activation(fo[:, c4 % 2, :, :, bass.ds((i * 2 + par) * G, G)],
                                                pf[:, par, :, :, ::-1].rearrange("p g f t -> p f t g"), ACT.Copy))
            s_ev[0].wait(sp, t=(c4 + 1) * GT // 2 - 1)
            s_ev[1].wait(sp, t=(c4 + 1) * GT // 2 - 1)
            for f in range(2):
                dst = fir_d[f, :, c0:c0 + QC].rearrange("(n t) c -> n t c", t=BLK)
                s_fo.by(sp.dma_start(dst, fo[:, c4 % 2, f, :, :]), c4 % 2)
        s_to = p.dma()
        s_f.wait(sp)
        s_to.by(sp.dma_start(tinv_d.rearrange("u (h i) j -> (u h i j)", h=H).rearrange("(p x) -> p x", p=P),
                             tinv[:, :, :, :].rearrange("p s i j -> p (s i j)")))
        s_to.wait(sp)
        s_fo.wait_all(sp)
        barrier()
        s_fo.close()
        q.close()
        p.close()

    with ExitStack() as st:
        turns = CPB
        NP = H // 2
        rq = sb(st, "rq", [P, 2, 2, UNITS])
        kqv = sb(st, "kqv", [P, 2, 3, B, D])
        tc = sb(st, "tc", [P, 2, B, CH])
        kx = sb(st, "kx", [P, 2, B, P])
        qx = sb(st, "qx", [P, B, P])
        kbx = sb(st, "kbx", [P, B, P])
        vb = sb(st, "vb", [P, B, D])
        tx = sb(st, "tx", [P, B, P])
        kT = sb(st, "kT", [P, B, P])
        qT = sb(st, "qT", [P, 2, B, P])
        atT = sb(st, "atT", [P, 2, B, P])
        wT = sb(st, "wT", [P, 2, B, P])
        uu = sb(st, "uu", [P, 2, B, D])
        ui = sb(st, "ui", [P, B, D])
        state = sb(st, "state", [P, B, NP, D])
        do = sb(st, "do", [P, 2, B, D])
        pA = ps(st, "pA", [P, B, P])
        pBq = ps(st, "pBq", [P, B, P])
        pC = ps(st, "pC", [P, B, P])
        pD = ps(st, "pD", [P, B, P])
        pF = ps(st, "pF", [P, B, 2 * D])
        pG = ps(st, "pG", [P, B, 2 * D])
        pH = ps(st, "pH", [P, NP, 512])

        p = sems.loop(1)
        s_z, s_r = p.step(), p.step(4)
        s_z.by(dve.memset(state[:, :, :, :], 0.0))
        for s in range(2):
            for n in range(2):
                s_r.by(dve.tensor_scalar(rq[:, s, n, :], rnorm[:, n, :], parity[:, s:s + 1], None, ALU.mult))
        s_r.wait(pool)
        s_z.wait(pe)
        q = sems.loop(turns)
        s_ld, s_do = Pair(sems, turns, H + 1), Pair(sems, turns, H)
        s_kx, s_qx, s_kb, s_vb, s_tx = q.step(), q.step(), q.step(), q.step(), q.step()
        s_tk, s_tq, s_ek, s_eq = q.step(), q.step(), q.step(), q.step()
        s_at, s_ea, s_w, s_ew, s_u, s_eu = q.step(), q.step(), q.step(), q.step(), q.step(), q.step()
        s_ws, s_ui, s_qs, s_ku, s_st, s_o, s_eo = [q.step() for _ in range(7)]

        def unit_cols(ap2, t):
            return ap2.rearrange("p (b c) -> p b c", b=B)[:, :, bass.ds(t, 1)].rearrange("p b c -> p (b c)")

        def expand(t, dst, par, n, step):
            src = kqv[:, par, n, :, :].unsqueeze(2).broadcast_to([P, B, 2, D])
            sc = rq[:, :, n, :].rearrange("p s (b c) -> p b s c", b=B)[:, :, :, bass.ds(t, 1)].rearrange("p b s c -> p b (s c)")
            step.by(pool.tensor_tensor(dst.rearrange("p b (s d) -> p b s d", s=2), src,
                                       sc.unsqueeze(3).broadcast_to([P, B, 2, D]), ALU.mult))

        def prepare(t, par, half):
            for s in (s_kx, s_qx, s_vb, s_tx):
                s.back(sp, t, 2)
            for h in range(H):
                src = qkv_d[:, :, h * D:(h + 1) * D].rearrange("n (b c i) f -> c i n b f", b=B, i=CH)
                s_ld.by(sp.dma_start(kqv[h * CH:(h + 1) * CH, par, :, :, :],
                                     src[bass.ds(t, 1)].rearrange("o i n b f -> (o i) n b f")), par)
            s_ld.by(sp.dma_start(tc[:, par, :, :], tinv_d.rearrange("(b c) p i -> c p b i", b=B)[bass.ds(t, 1)]
                                 .rearrange("o p b i -> (o p) b i")), par)
            s_ld.wait(pool, par, half)
            s_ku.back(pool, t, 2)
            s_tk.back(pool, t, 2)
            expand(t, kx[:, par, :, :], par, 1, s_kx)
            s_tq.back(pool, t, 1)
            expand(t, qx[:, :, :], par, 0, s_qx)
            s_ld.wait(dve, par, half)
            s_u.back(dve, t, 1)
            s_w.back(dve, t, 1)
            s_tx.by(dve.tensor_tensor(tx[:, :, :].rearrange("p b (h i) -> p b h i", h=H),
                                      tc[:, par, :, :].unsqueeze(2).broadcast_to([P, B, H, CH]),
                                      blockdiag[:, :].rearrange("p (h i) -> p h i", h=H).unsqueeze(1).broadcast_to([P, B, H, CH]),
                                      ALU.mult))
            beta = unit_cols(betac[:, :], t)
            s_vb.by(dve.tensor_tensor(vb[:, :, :], kqv[:, par, 2, :, :], beta.unsqueeze(2).broadcast_to([P, B, D]), ALU.mult))
            yield
            s_kx.wait(pe, t=t)
            s_eu.back(pe, t, 1)
            for b in range(B):
                i = pe.transpose(pA[:, b, :], kx[:, par, b, :], ident[:, :])
            s_tk.by(i)
            s_qx.wait(pe, t=t)
            s_eq.back(pe, t, 1)
            for b in range(B):
                i = pe.transpose(pBq[:, b, :], qx[:, b, :], ident[:, :])
            s_tq.by(i)
            s_tk.wait(act, t=t)
            s_at.back(act, t, 1)
            s_ek.by(act.activation(kT[:, :, :], pA[:, :, :], ACT.Copy))
            s_tq.wait(act, t=t)
            s_o.back(act, t, 2)
            s_eq.by(act.activation(qT[:, par, :, :], pBq[:, :, :], ACT.Copy))
            s_kx.wait(dve, t=t)
            s_kb.by(dve.tensor_tensor(kbx[:, :, :], kx[:, par, :, :], beta.unsqueeze(2).broadcast_to([P, B, P]), ALU.mult))
            yield
            s_ek.wait(pe, t=t)
            s_eq.wait(pe, t=t)
            s_ea.back(pe, t, 1)
            for b in range(B):
                i = pe.matmul(pC[:, b, :], kT[:, b, :], qT[:, par, b, :], start=True, stop=True)
            s_at.by(i)
            s_at.wait(dve, t=t)
            s_o.back(dve, t, 2)
            s_ea.by(dve.tensor_tensor(atT[:, par, :, :], pC[:, :, :], causal[:, :].unsqueeze(1).broadcast_to([P, B, P]), ALU.mult))
            yield
            s_kb.wait(pe, t=t)
            s_tx.wait(pe, t=t)
            s_ew.back(pe, t, 1)
            for b in range(B):
                i = pe.matmul(pD[:, b, :], kbx[:, b, :], tx[:, b, :], start=True, stop=True)
            s_w.by(i)
            s_w.wait(act, t=t)
            s_ws.back(act, t, 2)
            s_ew.by(act.activation(wT[:, par, :, :], pD[:, :, :], ACT.Copy))
            s_vb.wait(pe, t=t)
            for b in range(B):
                i = pe.matmul(pA[:, b, 0:D], tx[:, b, :], vb[:, b, :], start=True, stop=True)
            s_u.by(i)
            s_u.wait(act, t=t)
            s_ui.back(act, t, 2)
            s_eu.by(act.activation(uu[:, par, :, :], pA[:, :, 0:D], ACT.Copy))

        def advance(t, par, half):
            s_st.back(pe, t, 1)
            s_ew.wait(pe, t=t)
            s_ui.back(pe, t, 1)
            for b in range(B):
                for n in range(NP):
                    r = slice(n * D, (n + 1) * D)
                    i = pe.matmul(pF[r, b, 0:D], wT[:, par, b, r], state[:, b, n, :], start=True, stop=True)
            s_ws.by(i)
            s_ws.wait(dve, t=t)
            s_eu.wait(dve, t=t)
            s_ku.back(dve, t, 1)
            s_o.back(dve, t, 1)
            s_ui.by(dve.tensor_tensor(ui[:, :, :], uu[:, par, :, :], pF[:, :, 0:D], ALU.subtract))
            s_eo.back(pe, t, 1)
            for b in range(B):
                for n in range(NP):
                    r = slice(n * D, (n + 1) * D)
                    i = pe.matmul(pG[r, b, 0:D], qT[:, par, b, r], state[:, b, n, :], start=(b == 0), stop=False,
                                  skip_group_check=True)
            s_qs.by(i)
            yield
            s_ui.wait(pe, t=t)
            for b in range(B):
                for n in range(NP):
                    r = slice(n * D, (n + 1) * D)
                    i = pe.matmul(pH[:, n, b * D:(b + 1) * D], kx[r, par, b, :], ui[r, b, :], start=True, stop=True)
            s_ku.by(i)
            s_ku.wait(dve, t=t)
            s_qs.wait(dve, t=t)
            s_st.by(dve.tensor_tensor(state[:, :, :, :], state[:, :, :, :], pH[:, :, 0:B * D].rearrange("p n (b d) -> p b n d", b=B), ALU.add))
            yield
            s_ea.wait(pe, t=t)
            for b in range(B):
                i = pe.matmul(pG[:, b, 0:D], atT[:, par, b, :], ui[:, b, :], start=False, stop=True, skip_group_check=True)
            s_o.by(i)
            s_o.wait(act, t=t)
            s_do.free(act, par, half)
            s_eo.by(act.activation(do[:, par, :, :], pG[:, :, 0:D], ACT.Copy))
            s_eo.wait(sp, t=t)
            for h in range(H):
                dst = delta_d[:, h * D:(h + 1) * D].rearrange("(b c i) f -> c i b f", b=B, i=CH)
                s_do.by(sp.dma_start(dst[bass.ds(t, 1)].rearrange("o i b f -> (o i) b f"), do[h * CH:(h + 1) * CH, par, :, :]), par)
            yield

        pipeline(nc, turns, prepare, advance)
        s_do.wait_all(sp)
        barrier()
        s_do.close()
        s_ld.close()
        q.close()
        p.close()
    hold.close()

    gate = ExitStack()
    weight = sb(gate, "weight", [P, TILES, H, NBR])
    BR = (("fir", 1), ("fir", 0), ("delta", 0), ("qkv", 2))

    def branch(n, t):
        kind, i = BR[n]
        src = {"fir": fir_d, "delta": None, "qkv": qkv_d}[kind]
        src = delta_d if src is None else src[i]
        return src[bass.ds(t * P, P), :]

    NG = H * NBR
    temp = sb(gate, "temp", [P, H])
    floor = sb(gate, "floor", [P, NG])
    onorm = sb(gate, "onorm", [P, 1])
    GW = P
    with ExitStack() as st:
        w1h = sb(st, "w1h", [P, KT, GW])
        w1b = sb(st, "w1b", [P, 2, GW])
        w1m = sb(st, "w1m", [P, 2, GW])
        w1s = sb(st, "w1s", [D, NBR, 2, GW])
        half = sb(st, "half", [P, P])
        pick = sb(st, "pick", [D, 4 * NG - 1])
        wst = sb(st, "wst", [2 * NG, H, GW])
        w2 = sb(st, "w2", [GW, NBR])
        b1 = sb(st, "b1", [GW, 1])
        b2 = sb(st, "b2", [P, NBR])
        br = sb(st, "br", [P, 2, 2, H, 2, D])
        ht = sb(st, "ht", [P, 2, KT, P])
        sq = sb(st, "sq", [P, NG, D])
        stt = sb(st, "stt", [P, 2, 2, NG])
        bT5 = sb(st, "bT5", [P, 2, 2, H, P])
        sT = sb(st, "sT", [2 * NG, 2, P])
        hm = sb(st, "hm", [P, 2, H, P])
        pX = ps(st, "pX", [P, 2, H, P])
        pS = ps(st, "pS", [P, 512])
        pM = ps(st, "pM", [P, 2, H, P])
        pL = ps(st, "pL", [P, 2, 512])

        p = sems.loop(1)
        s_w, s_c = p.dma(10 + 3 * NBR), p.step(3)
        s_w.by(sp.dma_start(w1h[:, :, :], a["gW1"][0:C, :].rearrange("(k p) n -> p k n", p=P)))
        s_w.by(sp.dma_start(w1b[:, :, :], a["gW1"][C + 3 * NBR * D:, :].rearrange("(k p) n -> p k n", p=P)))
        for n in range(NBR):
            r = C + 3 * D * n
            s_w.by(sp.dma_start(w1m[(n % 2) * D:(n % 2 + 1) * D, n // 2, :], a["gW1"][r:r + D, :]))
            for s in range(2):
                s_w.by(sp.dma_start(w1s[:, n, s, :], a["gW1"][r + (s + 1) * D:r + (s + 2) * D, :]))
        s_w.by(sp.dma_start(w2[:, :], a["gW2"]))
        s_w.by(sp.dma_start(b1[:, :], a["gb1"]))
        s_w.by(sp.dma_start(b2[:, :], a["gb2"][0].partition_broadcast(P)))
        s_w.by(sp.dma_start(temp[:, :], a["temp"][0].partition_broadcast(P)))
        s_w.by(sp.dma_start(floor[:, :], a["floor"][0].partition_broadcast(P)))
        for n in range(2):
            s_w.by(sp.dma_start(onorm[n * D:(n + 1) * D, :], a["onorm"].rearrange("o d -> d o")))
        s_w.by(sp.dma_start(sT[:, 0, :], a["gW1"][0:2 * NG, :]))
        s_c.by(dve.memset(half[:, :], 0.0))
        s_c.by(dve.memset(pick[:, :], 0.0))
        s_c.wait(dve, 2)
        dve.memset(half[0:D, 0:D], 1.0 / D)
        dve.memset(half[D:P, D:P], 1.0 / D)
        s_c.by(dve.memset(pick[:, 2 * NG - 1:2 * NG], 1.0))
        s_c.wait(pe)
        s_w.wait(pe)
        s_m, s_ma = p.step(1 + H), p.step(1 + H)
        for k in range(2):
            i = pe.matmul(pX[:, 0, k, :], half[:, :], w1m[:, k, :], start=True, stop=True)
        s_m.by(i)
        s_m.wait(dve, 1)
        s_w.wait(dve)
        s_ma.by(dve.tensor_tensor(w1b[:, :, :], w1b[:, :, :], pX[:, 0, 0:2, :], ALU.add))
        for h in range(H):
            if h:
                s_ma.wait(pe, h + 1)
            for n in range(NBR):
                for s in range(2):
                    c = s * NG + (n // 2) * 2 * H + h * 2 + n % 2
                    i = pe.matmul(pS[0:2 * NG, 0:GW], pick[:, 2 * NG - 1 - c:4 * NG - 1 - c], w1s[:, n, s, :],
                                  start=(n + s == 0), stop=(n == NBR - 1 and s == 1))
            s_m.by(i)
            s_m.wait(dve, h + 2)
            s_ma.by(dve.tensor_copy(wst[:, h, :], pS[0:2 * NG, 0:GW]))
        s_ma.wait(pe)
        s_w.wait(act)

        q = sems.loop(TILES)
        s_ld = Pair(sems, TILES, NBR + 1)
        s_sq, s_v, s_rt, s_tx, s_ex, s_ts, s_es = q.step(), q.step(3), q.step(), q.step(2), q.step(2), q.step(), q.step()
        s_m1, s_ge, s_l, s_lo = q.step(), q.step(), q.step(), q.step()

        def features(t, par, hf):
            s_tx.back(sp, t, 2)
            s_sq.back(sp, t, 2)
            s_v.back(sp, t, 2)
            s_m1.back(sp, t, 2)
            for n in range(NBR):
                s_ld.by(sp.dma_start(br[:, par, n // 2, :, n % 2, :], branch(n, t).rearrange("p (h d) -> p h d", h=H)), par)
            s_ld.by(sp.dma_start(ht[:, par, :, :], hT_d.rearrange("k p t -> p k t")[:, :, bass.ds(t * P, P)]), par)
            s_ld.wait(act, par, hf)
            s_v.back(act, t, 1)
            s_sq.by(act.activation(sq[:, :, :], br[:, par, :, :, :, :].rearrange("p k h n d -> p (k h n) d"), ACT.Square))
            s_ld.wait(dve, par, hf)
            s_ts.back(dve, t, 2)
            s_v.by(dve.tensor_reduce(stt[:, par, 1, :], br[:, par, :, :, :, :].rearrange("p k h n d -> p (k h n) d"), AX, ALU.max))
            s_ld.wait(pe, par, hf)
            for k in range(2):
                s_ex.back(pe, t, 1)
                for h in range(H):
                    i = pe.transpose(pX[:, k, h, :], br[:, par, k, h, :, :].rearrange("p n d -> p (n d)"), ident[:, :])
                s_tx.by(i)
            yield
            s_sq.wait(dve, t=t)
            s_v.by(dve.tensor_reduce(stt[:, par, 0, :], sq[:, :, :], AX, ALU.add))
            s_v.wait(dve, 2, t=t)
            s_v.by(dve.tensor_scalar(stt[:, par, 0, :], stt[:, par, 0, :], 1.0 / D, 1e-8, ALU.mult, ALU.max))
            s_tx.wait(act, 1, t=t)
            s_m1.back(act, t, 2)
            s_ex.by(act.activation(bT5[:, par, 0, :, :], pX[:, 0, :, :], ACT.Copy))
            s_v.wait(act, t=t)
            s_rt.by(act.activation(stt[:, par, 0, :], stt[:, par, 0, :], ACT.Sqrt))
            s_tx.wait(dve, 2, t=t)
            s_m1.back(dve, t, 2)
            s_ex.by(dve.tensor_copy(bT5[:, par, 1, :, :], pX[:, 1, :, :]))
            yield
            s_rt.wait(pe, t=t)
            s_es.back(pe, t, 1)
            i = pe.transpose(pS[0:2 * NG, 0:P], stt[:, par, :, :].rearrange("p s g -> p (s g)"), ident[:, :])
            s_ts.by(i)
            s_ts.wait(dve, t=t)
            s_es.by(dve.tensor_copy(sT[:, par, :], pS[0:2 * NG, 0:P]))

        def logits(t, par, hf):
            s_ex.wait(pe, t=t)
            s_ge.back(pe, t, 2)
            for k in range(KT):
                pe.matmul(pM[:, par, :, :], w1h[:, k, :], ht[:, par, k, :].unsqueeze(1).broadcast_to([P, H, P]),
                          start=(k == 0), stop=False, skip_group_check=True)
            for k in range(2):
                pe.matmul(pM[:, par, :, :], w1b[:, k, :], bT5[:, par, k, :, :], start=False, stop=False, skip_group_check=True)
            s_es.wait(pe, t=t)
            for h in range(H):
                i = pe.matmul(pM[:, par, h, :], wst[:, h, :], sT[:, par, :], start=False, stop=True, skip_group_check=True)
            s_m1.by(i)
            yield
            s_m1.wait(act, t=t)
            s_l.back(act, t, 2)
            s_ge.by(act.activation(hm[:, par, :, :], pM[:, par, :, :], ACT.Gelu, bias=b1[:, 0:1]))
            yield
            s_ge.wait(pe, t=t)
            s_lo.back(pe, t, 2)
            for h in range(H):
                i = pe.matmul(pL[:, par, h * NBR:(h + 1) * NBR], hm[:, par, h, :], w2[:, :], start=True, stop=True)
            s_l.by(i)
            s_l.wait(dve, t=t)
            s_lo.by(dve.tensor_tensor(weight[:, bass.ds(t, 1), :, :].rearrange("p o h n -> p (o h) n"),
                                      pL[:, par, 0:NG].rearrange("p (h n) -> p h n", h=H),
                                      b2[:, :].unsqueeze(1).broadcast_to([P, H, NBR]), ALU.add))

        pipeline(nc, TILES, features, logits)
        barrier()
        s_ld.close()
        q.close()
        p.close()

    with ExitStack() as st:
        mx = sb(st, "mx", [P, TILES * H])
        p = sems.loop(1)
        s_v, s_e = p.step(14), p.step()
        n_v = 0

        def chained(ins):
            nonlocal n_v
            n_v += 1
            s_v.by(ins)
            s_v.wait(dve, n_v)

        w3 = weight[:, :, :, :].rearrange("p t h n -> p (t h) n")
        w4 = weight[:, :, :, :].rearrange("p t h n -> p t (h n)")

        def wide(x):
            return x.unsqueeze(2).broadcast_to([P, TILES * H, NBR])

        chained(dve.tensor_scalar(temp[:, :], temp[:, :], 0.2, 10.0, ALU.max, ALU.min))
        chained(dve.reciprocal(temp[:, :], temp[:, :]))
        chained(dve.tensor_scalar(floor[:, :], floor[:, :], 1e-7, 0.1, ALU.max, ALU.min))
        chained(dve.tensor_tensor(weight[:, :, :, :], weight[:, :, :, :],
                                  temp[:, :].unsqueeze(1).unsqueeze(3).broadcast_to([P, TILES, H, NBR]), ALU.mult))
        chained(dve.tensor_reduce(mx[:, :], w3, AX, ALU.max))
        chained(dve.tensor_tensor(w3, w3, wide(mx[:, :]), ALU.subtract))
        s_v.wait(act, n_v)
        s_e.by(act.activation(w3, w3, ACT.Exp))
        s_e.wait(dve)
        for low in (True, False):
            chained(dve.tensor_reduce(mx[:, :], w3, AX, ALU.add))
            chained(dve.reciprocal(mx[:, :], mx[:, :]))
            chained(dve.tensor_tensor(w3, w3, wide(mx[:, :]), ALU.mult))
            if low:
                chained(dve.tensor_tensor(w4, w4, floor[:, :].unsqueeze(1).broadcast_to([P, TILES, NG]), ALU.max))
        if "w_d" in dbg:
            w_d = dram("w_d", [TOK, NG])
            s_x = p.dma()
            s_v.wait(sp, n_v)
            s_x.by(sp.dma_start(w_d.rearrange("(t p) g -> p t g", p=P), w4))
            s_x.wait(sp)
        s_v.per_turn = n_v
        barrier()
        p.close()

    with ExitStack() as st:
        wo = sb(st, "wo", [P, KT, C])
        gw = sb(st, "gw", [P, KT, NE])
        br = sb(st, "br6", [P, 2, NBR, C])
        xt = sb(st, "xt", [P, 2, C])
        pr = sb(st, "pr", [P, NBR, C])
        mix = sb(st, "mix", [P, C])
        msq = sb(st, "msq", [P, C])
        rr = sb(st, "rr", [P, H])
        on = sb(st, "on", [P, 2, C])
        oT = sb(st, "oT", [P, KT, P])
        x2 = sb(st, "x2", [P, 2, C])
        bn = sb(st, "bn", [P, 6])
        mv = sb(st, "mv", [P, 2])
        h2 = sb(st, "h2", [P, 2, C])
        h2T = sb(st, "h2T", [P, KT, P])
        pO = ps(st, "pO", [P, KT, P])
        pW = ps(st, "pW", [P, C])
        pH2 = ps(st, "pH2", [P, KT, P])
        pg = ps(st, "pg", [P, 512])
        p = sems.loop(1)
        s_w, s_wo = p.dma(2), p.step()
        s_w.by(sp.dma_start(wo[:, :, :], a["Wo"].rearrange("(k p) n -> p k n", p=P)))
        s_w.by(sp.dma_start(gw[:, :, :], a["gate_w"].rearrange("(k p) n -> p k n", p=P)))
        s_w.wait(dve)
        s_w.wait(pe)
        s_wo.by(dve.tensor_scalar(wo[:, :, :], wo[:, :, :], onorm[:, 0:1], None, ALU.mult))
        s_wo.wait(pe)

        q = sems.loop(TILES)
        s_ld, s_st = Pair(sems, TILES, NBR + 1), Pair(sems, TILES, 2)
        s_pr, s_mx, s_ms, s_r, s_rt, s_on = q.step(), q.step(), q.step(), q.step(3), q.step(), q.step()
        s_to, s_eo, s_wm, s_x2, s_b, s_sr, s_h, s_th, s_eh, s_gm, s_g = (
            q.step(), q.step(), q.step(), q.step(2), q.step(4), q.step(), q.step(3), q.step(), q.step(), q.step(), q.step())

        def mixing(t, par, hf):
            s_pr.back(sp, t, 2)
            s_x2.back(sp, t, 2)
            for n in range(NBR):
                s_ld.by(sp.dma_start(br[:, par, n, :], branch(n, t)), par)
            s_ld.by(sp.dma_start(xt[:, par, :], a["x"][bass.ds(t * P, P), :]), par)
            s_ld.wait(pool, par, hf)
            s_mx.back(pool, t, 1)
            w = weight[:, bass.ds(t, 1), :, :].rearrange("p o h n -> p n (o h)")
            s_pr.by(pool.tensor_tensor(pr[:, :, :].rearrange("p n (h d) -> p n h d", h=H),
                                       br[:, par, :, :].rearrange("p n (h d) -> p n h d", h=H),
                                       w.unsqueeze(3).broadcast_to([P, NBR, H, D]), ALU.mult))
            yield
            s_pr.wait(dve, t=t)
            s_ms.back(dve, t, 1)
            s_mx.by(dve.tensor_reduce(mix[:, :], pr[:, :, :].rearrange("p n c -> p c n"), AX, ALU.add))
            s_mx.wait(act, t=t)
            s_r.back(act, t, 1)
            s_ms.by(act.activation(msq[:, :], mix[:, :], ACT.Square))
            yield
            s_ms.wait(dve, t=t)
            s_r.by(dve.tensor_reduce(rr[:, :], msq[:, :].rearrange("p (h d) -> p h d", h=H), AX, ALU.add))
            s_r.wait(dve, 1, t=t)
            s_r.by(dve.tensor_scalar(rr[:, :], rr[:, :], 1.0 / D, EPS_RMS, ALU.mult, ALU.add))
            s_r.wait(act, 2, t=t)
            s_rt.by(act.activation(rr[:, :], rr[:, :], ACT.Sqrt))
            yield
            s_rt.wait(dve, t=t)
            s_r.by(dve.reciprocal(rr[:, :], rr[:, :]))
            s_r.wait(dve, t=t)
            s_to.back(dve, t, 2)
            s_on.by(dve.tensor_tensor(on[:, par, :].rearrange("p (h d) -> p h d", h=H),
                                      mix[:, :].rearrange("p (h d) -> p h d", h=H),
                                      rr[:, :].unsqueeze(2).broadcast_to([P, H, D]), ALU.mult))

        def row(n, t):
            return rows[:, n, bass.ds(t // (TILES // B), 1), :].rearrange("p o c -> p (o c)")

        def project_out(t, par, hf):
            s_on.wait(pe, t=t)
            s_eo.back(pe, t, 1)
            for k in range(KT):
                i = pe.transpose(pO[:, k, :], on[:, par, k * P:(k + 1) * P], ident[:, :])
            s_to.by(i)
            s_to.wait(act, t=t)
            s_wm.back(act, t, 1)
            s_eo.by(act.activation(oT[:, :, :], pO[:, :, :], ACT.Copy))
            s_eo.wait(pe, t=t)
            s_x2.back(pe, t, 1)
            for k in range(KT):
                i = pe.matmul(pW[:, :], oT[:, k, :], wo[:, k, :], start=(k == 0), stop=(k == KT - 1))
            s_wm.by(i)
            yield
            s_wm.wait(dve, t=t)
            s_st.free(dve, par, hf)
            s_x2.by(dve.tensor_tensor(x2[:, par, :], pW[:, :], row(0, t), ALU.mult))
            s_x2.wait(dve, 1, t=t)
            s_x2.by(dve.tensor_tensor(x2[:, par, :], x2[:, par, :], xt[:, par, :], ALU.add))
            s_x2.wait(dve, t=t)
            s_x2.wait(sp, t=t)
            s_st.by(sp.dma_start(x2_d[bass.ds(t * P, P), :], x2[:, par, :]), par)
            s_b.by(dve.bn_stats(bn[:, :], x2[:, par, :]))
            s_b.wait(dve, 1, t=t, alone=True)
            s_b.by(dve.bn_aggr(mv[:, :], bn[:, :]))
            s_b.wait(dve, 2, t=t)
            s_b.by(dve.tensor_scalar(mv[:, 1:2], mv[:, 1:2], EPS_LN, None, ALU.add))
            s_b.wait(act, 3, t=t)
            s_sr.by(act.activation(mv[:, 1:2], mv[:, 1:2], ACT.Sqrt))
            yield
            s_sr.wait(dve, t=t)
            s_b.by(dve.reciprocal(mv[:, 1:2], mv[:, 1:2]))
            s_b.wait(dve, t=t)
            s_th.back(dve, t, 2)
            s_h.by(dve.tensor_scalar(h2[:, par, :], x2[:, par, :], mv[:, 0:1], mv[:, 1:2], ALU.subtract, ALU.mult))
            s_h.wait(dve, 1, t=t)
            s_h.by(dve.tensor_tensor(h2[:, par, :], h2[:, par, :], row(2, t), ALU.mult))
            s_h.wait(dve, 2, t=t)
            s_h.by(dve.tensor_tensor(h2[:, par, :], h2[:, par, :], row(1, t), ALU.add))
            s_h.wait(sp, t=t)
            s_st.by(sp.dma_start(h2_d[bass.ds(t * P, P), :], h2[:, par, :]), par)
            s_h.wait(pe, t=t)
            s_eh.back(pe, t, 1)
            for k in range(KT):
                i = pe.transpose(pH2[:, k, :], h2[:, par, k * P:(k + 1) * P], ident[:, :])
            s_th.by(i)
            s_th.wait(act, t=t)
            s_gm.back(act, t, 1)
            s_eh.by(act.activation(h2T[:, :, :], pH2[:, :, :], ACT.Copy))
            yield
            s_eh.wait(pe, t=t)
            s_g.back(pe, t, 1)
            for k in range(KT):
                i = pe.matmul(pg[:, 0:NE], h2T[:, k, :], gw[:, k, :], start=(k == 0), stop=(k == KT - 1))
            s_gm.by(i)
            s_gm.wait(dve, t=t)
            s_g.by(dve.tensor_scalar(gates[:, bass.ds(t % TPB, 1), bass.ds(t // TPB, 1), :].rearrange("p o b e -> p (o b e)"), pg[:, 0:NE], 1e-6, None, ALU.max))

        pipeline(nc, TILES, mixing, project_out)
        s_st.wait_all(sp)
        barrier()
        s_st.close()
        s_ld.close()
        q.close()
        p.close()
    gate.close()

    R = B * NE
    route = ExitStack()
    top = sb(route, "top", [R, CAP])
    topi = sb(route, "topi", [R, CAP])
    with ExitStack() as st:
        cs7 = sb(st, "cs7", [P, R])
        rs7 = sb(st, "rs7", [P, TILES])
        G = sb(st, "G", [R, L])
        m8 = sb(st, "m8", [R, 8])
        i8 = sb(st, "i8", [R, 8], U32)
        zero = sb(st, "zero", [P, TOK * NE // P])
        pc = ps(st, "pc", [P, R])
        pgt = ps(st, "pgt", [R, 4, 4, P])
        p = sems.loop(1)
        s_z, s_zo = p.step(), p.pool_dma()
        s_z.by(pool.memset(zero[:, :], 0.0))
        s_z.wait(pool)
        s_zo.by(pool.dma_start(key_d.rearrange("(p x) o -> p (x o)", p=P), zero[:, :]))
        q = sems.loop(8)
        s_s, s_cm = q.step(6), q.step()
        g3 = gates[:, :, :, :].rearrange("p t b e -> p t (b e)")
        gr7 = gates[:, :, :, :].rearrange("p t b e -> p (t b) e")
        with nc.Fori(0, 8, engines=[ENG.DVE, ENG.PE]) as i:
            q.it = i
            s_s.by(dve.tensor_reduce(cs7[:, :], g3.rearrange("p t r -> p r t"), AX, ALU.add))
            s_s.wait(pe, 1)
            s_cm.by(pe.matmul(pc[:, :], ones[:, :], cs7[:, :], start=True, stop=True))
            s_cm.wait(dve)
            s_s.by(dve.reciprocal(cs7[:, :], pc[:, :]))
            s_s.wait(dve, 2)
            s_s.by(dve.tensor_tensor(g3, g3, cs7[:, :].unsqueeze(1).broadcast_to([P, TPB, R]), ALU.mult))
            s_s.wait(dve, 3)
            s_s.by(dve.tensor_reduce(rs7[:, :], gr7, AX, ALU.add))
            s_s.wait(dve, 4)
            s_s.by(dve.reciprocal(rs7[:, :], rs7[:, :]))
            s_s.wait(dve, 5)
            s_s.by(dve.tensor_tensor(gr7, gr7, rs7[:, :].unsqueeze(2).broadcast_to([P, TILES, NE]), ALU.mult))
            s_s.wait(dve, 6)
        s_s.wait_all(pe)
        s_t, s_e = p.step(4), p.step(4)
        for j in range(TPB):
            i = pe.transpose(pgt[:, j // 4, j % 4, :], g3[:, j, :], ident[:, :])
            if j % 4 == 3:
                s_t.by(i)
        for w in range(4):
            s_t.wait(dve, w + 1)
            s_e.by(dve.tensor_copy(G[:, w * 512:(w + 1) * 512], pgt[:, w, :, :].rearrange("r t p -> r (t p)")))
        s_e.wait(dve)
        q2 = sems.loop(CAP // 8)
        s_k = q2.step(5)
        with nc.Fori(0, CAP // 8, engines=[ENG.DVE]) as i:
            q2.it = i
            s_k.by(dve.max(m8[:, :], G[:, :]))
            s_k.wait(dve, 1, alone=True)
            s_k.by(dve.max_index(i8[:, :], m8[:, :], G[:, :]))
            s_k.wait(dve, 2, alone=True)
            s_k.by(dve.match_replace(G[:, :], m8[:, :], G[:, :], -1.0))
            s_k.by(dve.tensor_copy(top[:, bass.ds(i * 8, 8)], m8[:, :]))
            s_k.by(dve.tensor_copy(topi[:, bass.ds(i * 8, 8)], i8[:, :]))
            s_k.wait(dve, 5)
        s_zo.wait(pool)
        barrier()
        q2.close()
        q.close()
        p.close()

    with ExitStack() as st:
        NH = CAP // P
        exw = sb(st, "exw", [P, KT, NE, C])
        hot = sb(st, "hot", [P, NH, R])
        tokf = sb(st, "tokf", [P, NH, R])
        keyf = sb(st, "keyf", [P, NH, R])
        toku = sb(st, "toku", [P, NH, R], U32)
        keyu = sb(st, "keyu", [P, NH, R], U32)
        keyv = sb(st, "keyv", [P, NH, NE])
        keyi = sb(st, "keyi", [P, NH, NE], mybir.dt.int32)
        cur = sb(st, "cur8", [P, NH, NE], U32)
        pt = ps(st, "pt", [P, 2, NH, R])
        p = sems.loop(1)
        s_w, s_i, s_kv = p.dma(KT), p.step(), p.step()
        for k in range(KT):
            s_w.by(sp.dma_start(exw[:, k, :, :], a["experts"].rearrange("(e k p) n -> k p e n", k=KT, p=P)[k]))
        s_i.by(pool.iota(keyi[:, :, :], pattern=[[P * NE, NH], [1, NE]], base=1, channel_multiplier=NE))
        s_i.wait(dve)
        s_kv.by(dve.tensor_copy(keyv[:, :, :], keyi[:, :, :]))
        s_t, s_c = p.step(), p.step(2)
        for w in range(NH):
            pe.transpose(pt[:, 0, w, :], topi[:, w * P:(w + 1) * P], ident[0:R, 0:R])
            i = pe.transpose(pt[:, 1, w, :], top[:, w * P:(w + 1) * P], ident[0:R, 0:R])
        s_t.by(i)
        s_t.wait(dve)
        s_v = p.step(B + NE + 3)
        for b in range(B):
            r = slice(b * NE, (b + 1) * NE)
            s_v.by(dve.tensor_scalar(tokf[:, :, r], pt[:, 0, :, r], float(b * L), None, ALU.add))
        s_v.by(dve.tensor_scalar(hot[:, :, :], pt[:, 1, :, :], 0.5, None, ALU.is_gt))
        s_v.wait(dve, B + 1)
        for e in range(NE):
            by_e = lambda x: x[:, :, :].rearrange("p w (b e) -> p w b e", b=B)[:, :, :, e]
            s_v.by(dve.tensor_scalar(by_e(keyf), by_e(tokf), float(NE), float(e), ALU.mult, ALU.add))
        s_v.by(dve.tensor_copy(toku[:, :, :], tokf[:, :, :]))
        s_v.wait(dve, B + NE + 2)
        s_v.by(dve.tensor_copy(keyu[:, :, :], keyf[:, :, :]))
        s_v.wait(dve)
        s_kv.wait(pool)

        q = sems.loop(B)
        s_cu, s_sc = q.step(), q.pool_dma(NH * NE)
        with nc.Fori(0, B, engines=[ENG.DVE, ENG.Pool]) as b:
            q.it = b
            s_cu.by(dve.tensor_copy(cur[:, :, :], keyu[:, :, bass.ds(b * NE, NE)]))
            s_cu.wait(pool)
            for w in range(NH):
                for e in range(NE):
                    s_sc.by(pool.indirect_dma_start(key_d, bass.IndirectOffsetOnAxis(ap=cur[:, w, e:e + 1], axis=0),
                                                    keyv[:, w, e:e + 1], None))
            s_sc.wait(dve)
        s_sc.wait_all(sp)
        keys = sb(st, "keys", [P, TILES, NE])
        won = sb(st, "won", [P, TILES])
        mask = sb(st, "mask", [P, TILES])
        rowu = sb(st, "rowu", [P, TILES], U32)
        s_kl = p.dma()
        s_kl.by(sp.dma_start(keys[:, :, :], key_d.rearrange("(t p e) o -> p t (e o)", p=P, e=NE)))
        s_kl.wait(dve)
        s_n = p.step(2 + B + 1)
        s_n.by(dve.tensor_reduce(won[:, :], keys[:, :, :], AX, ALU.max))
        s_n.wait(dve, 1)
        s_n.by(dve.tensor_scalar(mask[:, :], won[:, :], 1.0, None, ALU.min))
        s_n.wait(dve, 2)
        for b in range(B):
            r = slice(b * TILES // B, (b + 1) * TILES // B)
            s_n.by(dve.tensor_scalar(won[:, r], won[:, r], 1.0, float(b * L + 1), ALU.max, ALU.add))
        s_n.wait(dve, 2 + B)
        s_n.by(dve.tensor_scalar(rowu[:, :], won[:, :], -2.0, None, ALU.add))
        s_n.wait(dve)

        idx = sb(st, "idx", [P, 2, NH], U32)
        hg = sb(st, "hg", [P, 2, NH, C])
        hgT = sb(st, "hgT", [P, NH, KT, P])
        eo = sb(st, "eo", [P, 2, NH, C])
        pT8 = ps(st, "pT8", [P, NH, KT, P])
        pE8 = ps(st, "pE8", [P, 2, 512])
        q3 = sems.loop(R)
        s_id, s_tr, s_ev, s_mm, s_oe = q3.step(), q3.step(), q3.step(), q3.step(), q3.step(NH)
        s_ga, s_eo = Pair(sems, R, NH, pool=True), Pair(sems, R)
        s_w.wait(pe)

        def gather(t, par, hf):
            s_ga.free(dve, par, hf)
            s_id.by(dve.tensor_copy(idx[:, par, :], toku[:, :, bass.ds(t, 1)].rearrange("p w o -> p (w o)")))
            s_id.wait(pool, t=t)
            s_tr.back(pool, t, 2)
            for w in range(NH):
                s_ga.by(pool.indirect_dma_start(hg[:, par, w, :], None, h2_d,
                                                bass.IndirectOffsetOnAxis(ap=idx[:, par, w:w + 1], axis=0)), par)
            yield

        def expert(t, par, hf):
            s_ga.wait(pe, par, hf)
            s_ev.back(pe, t, 1)
            for w in range(NH):
                for k in range(KT):
                    i = pe.transpose(pT8[:, w, k, :], hg[:, par, w, k * P:(k + 1) * P], ident[:, :])
            s_tr.by(i)
            s_tr.wait(act, t=t)
            s_mm.back(act, t, 1)
            s_ev.by(act.activation(hgT[:, :, :, :], pT8[:, :, :, :], ACT.Copy))
            s_ev.wait(pe, t=t)
            s_oe.back(pe, t, 1)
            for w in range(NH):
                for k in range(KT):
                    i = pe.matmul(pE8[:, w, 0:C], hgT[:, w, k, :],
                                  exw[:, k, bass.ds(t % NE, 1), :].rearrange("p o n -> p (o n)"), start=(k == 0), stop=(k == KT - 1))
            s_mm.by(i)
            s_mm.wait(dve, t=t)
            s_eo.free(dve, par, hf)
            for w in range(NH):
                s_oe.by(dve.tensor_scalar(eo[:, par, w, :], pE8[:, w, 0:C], hot[:, w, bass.ds(t, 1)], None, ALU.mult))
            s_oe.wait(sp, t=t)
            dst = bass.AP(routed_d.tensor, ((t // NE) * (CAP * NE) + (t % NE)) * C, [[NE * C, P], [P * NE * C, NH], [1, C]])
            s_eo.by(sp.dma_start(dst, eo[:, par, :, :]), par)
            yield

        pipeline(nc, R, gather, expert)
        s_eo.wait_all(pool)

        ix = sb(st, "ix", [P, 2], U32)
        og = sb(st, "og", [P, 2, C])
        xr = sb(st, "xr", [P, 2, C])
        y = sb(st, "y9", [P, 2, C])
        q4 = sems.loop(TILES)
        s_ix, s_o = q4.step(), q4.step(2)
        s_og, s_xr, s_y = Pair(sems, TILES, pool=True), Pair(sems, TILES), Pair(sems, TILES)

        def fetch(t, par, hf):
            s_og.free(dve, par, hf)
            s_ix.by(dve.tensor_copy(ix[:, par:par + 1], rowu[:, bass.ds(t, 1)]))
            s_ix.wait(pool, t=t)
            s_o.back(pool, t, 2)
            s_og.by(pool.indirect_dma_start(og[:, par, :], None, routed_d,
                                            bass.IndirectOffsetOnAxis(ap=ix[:, par:par + 1], axis=0)), par)
            s_o.back(sp, t, 2)
            s_xr.by(sp.dma_start(xr[:, par, :], x2_d[bass.ds(t * P, P), :]), par)
            yield

        def finish(t, par, hf):
            s_og.wait(dve, par, hf)
            s_xr.wait(dve, par, hf)
            s_y.free(dve, par, hf)
            s_o.by(dve.scalar_tensor_tensor(y[:, par, :], og[:, par, :], mask[:, bass.ds(t, 1)], row(3, t), ALU.mult, ALU.mult))
            s_o.wait(dve, 1, t=t)
            s_o.by(dve.tensor_tensor(y[:, par, :], y[:, par, :], xr[:, par, :], ALU.add))
            s_o.wait(act, t=t)
            s_y.by(act.dma_start(out[bass.ds(t * P, P), :], y[:, par, :]), par)
            yield

        pipeline(nc, TILES, fetch, finish)
        s_y.wait_all(sp)
        barrier()
    route.close()
    whole.close()



INS = {"x": "L0_attn_x", "Wq": "L0_attn_Wq", "Wk": "L0_attn_Wk", "Wv": "L0_attn_Wv", "Wb": "L0_attn_Wb",
       "qc": "L0_attn_qc_w", "kc": "L0_attn_kc_w", "vc": "L0_attn_vc_w", "fir_s": "L0_attn_fir_s",
       "fir_l": "L0_attn_fir_l", "gW1": "L0_attn_gW1", "gb1": "L0_attn_gb1", "gW2": "L0_attn_gW2",
       "gb2": "L0_attn_gb2", "temp": "L0_attn_temp", "floor": "L0_attn_eps_floor",
       "onorm": "L0_attn_onorm_w", "Wo": "L0_attn_Wo", "gate_w": "L0_ffn_gate_w",
       "experts": "L0_ffn_experts", "cT": "L0_c", "wmod": "L0_wmod"}


def lay_out(inputs):
    import numpy as np
    shape = {"x": (TOK, C), "fir_s": (C, FIRS), "fir_l": (C, FIRL), "gb1": (P, 1), "gb2": (1, 4), "temp": (1, H),
             "floor": (1, 16), "onorm": (1, D), "gate_w": (C, NE), "experts": (NE * C, C)}
    got = {}
    for name, full in INS.items():
        v = np.asarray(inputs[full])
        if name in shape:
            v = v.reshape(shape[name])
        if name == "cT":
            v = v.T
        got[name] = np.ascontiguousarray(v)
    return got


def kernel(**inputs):
    import concourse.bacc as bacc
    from concourse.bass_utils import run_bass_kernel_spmd

    nc = bacc.Bacc("TRN2", target_bir_lowering=False, num_devices=1)
    arrays = lay_out(inputs)
    a = {n: nc.dram_tensor(f"in_{n}", list(v.shape), F32, kind="ExternalInput").ap() for n, v in arrays.items()}
    out = nc.dram_tensor("y", [TOK, C], F32, kind="ExternalOutput").ap()
    build(nc, a, out)
    r = run_bass_kernel_spmd(nc, [{f"in_{n}": v for n, v in arrays.items()}], core_ids=[0])
    return r.results[0]["y"].reshape(B, L, C)
```

```python
from contextlib import ExitStack

import concourse.bass as bass
from concourse import mybir

ALU = mybir.AluOpType
ACT = mybir.ActivationFunctionType
F32 = mybir.dt.float32
U32 = mybir.dt.uint32
AX = mybir.AxisListType.X
ENG = mybir.EngineType

P = 128
B, L, C, H = 4, 2048, 256, 4
D = C // H
TOK = B * L
TILES = TOK // P
CH = 32
TPB = TILES // B
UNITS = TOK // CH
CPB = L // CH
KT = C // P
WIN = 512
TAPS, FIRL, FIRS = 4, 31, 3
BLK = 64
NBLK = TOK // BLK
SPAN = BLK + FIRL - 1
RW = SPAN + BLK
NBR = 4
NE = 8
CAP = L // NE
EPS_LN, EPS_L2, EPS_RMS = 1e-5, 1e-6, 1e-5


class Sems:

    def __init__(self, nc, n):
        self.plain = (nc.sync, nc.gpsimd)
        self.free = [[nc.alloc_semaphore(f"s{i}"), 1] for i in range(n)]
        engines = (nc.sync, nc.scalar, nc.tensor, nc.vector, nc.gpsimd)
        for i, (sem, _) in enumerate(self.free):
            engines[i % 5].sem_inc(sem, 1)
        nc.all_engine_barrier()
        self.soft = [[nc.alloc_semaphore(f"pool_dma{i}"), 0] for i in range(10)]

    def loop(self, turns):
        return Loop(self, turns)


class Loop:

    def __init__(self, sems, turns):
        self.sems, self.turns, self.it, self.steps = sems, turns, 0, []

    def step(self, per_turn=1):
        s = Step(self, self.sems.free.pop(0), per_turn)
        self.steps.append(s)
        return s

    def dma(self, n=1):
        s = self.step(16 * n)
        s.unit = 16
        return s

    def pool_dma(self, n=1):
        s = Step(self, self.sems.soft.pop(0), 16 * n)
        s.unit = 16
        return s

    def close(self):
        for s in self.steps:
            s.slot[1] += s.per_turn * self.turns
            self.sems.free.append(s.slot)


class Ring:

    def __init__(self, sems, turns, n=1, slots=4, pool=False):
        self.loop = sems.loop(turns // slots)
        make = self.loop.pool_dma if pool else self.loop.dma
        self.of = [make(n) for _ in range(slots)]

    def by(self, instruction, slot):
        return self.of[slot].by(instruction)

    def wait(self, engine, slot, round):
        self.of[slot].wait(engine, t=round)

    def free(self, engine, slot, round):
        self.of[slot].back(engine, round, 1)

    def wait_all(self, engine):
        for s in self.of:
            s.wait_all(engine)

    def close(self):
        self.loop.close()


def Pair(sems, turns, n=1, pool=False):
    return Ring(sems, turns, n, 2, pool)


class Step:
    def __init__(self, loop, slot, per_turn):
        self.loop, self.slot, self.per_turn, self.unit = loop, slot, per_turn, 1
        self.sem, self.base = slot

    def by(self, instruction):
        return instruction.then_inc(self.sem, self.unit)

    def until(self, engine, t, k, alone=False):
        count = t * self.per_turn + (self.base + k)
        if not isinstance(t, int) and (alone or engine in self.loop.sems.plain):
            count = engine.snap(engine.to_reg(count))
            engine.wait_ge(self.sem, self.base + max(k, 0))
        engine.wait_ge(self.sem, count)

    def wait(self, engine, k=None, t=None, alone=False):
        self.until(engine, self.loop.it if t is None else t, self.per_turn if k is None else k, alone)

    def wait_last(self, engine):
        self.back(engine, self.loop.it, 1)

    def back(self, engine, t, n, alone=False):
        if not isinstance(t, int) or t >= n:
            self.until(engine, t, (1 - n) * self.per_turn, alone)

    def wait_all(self, engine):
        engine.wait_ge(self.sem, self.base + self.per_turn * self.loop.turns)


def weave(*stages):
    stages = list(stages)
    while stages:
        for s in list(stages):
            if next(s, stages) is stages:
                stages.remove(s)


def pipeline(nc, turns, first, second):
    weave(first(0, 0, 0))
    weave(second(0, 0, 0), first(1, 1, 0))
    with nc.Fori(1, turns // 2) as i:
        weave(second(i * 2 - 1, 1, i - 1), first(i * 2, 0, i))
        weave(second(i * 2, 0, i), first(i * 2 + 1, 1, i))
    weave(second(turns - 1, 1, turns // 2 - 1))


def flow(nc, turns, stages, peel, slots=4):
    def turn(group, u, peeled):
        for stage, lag in stages:
            t, slot, round = group * slots + (u - lag), (u - lag) % slots, group + (u - lag) // slots
            if not peeled or 0 <= t < turns:
                stage(t, slot, round)

    for i in range(peel * slots):
        turn(i // slots, i % slots, True)
    with nc.Fori(peel, turns // slots) as g:
        for u in range(slots):
            turn(g, u, False)
    for i in range(turns, turns + max(lag for _, lag in stages)):
        turn(i // slots, i % slots, True)


def oldest_first(*stages):
    return [(stage, lag) for lag, stage in reversed(list(enumerate(stages))) if stage]


def build(nc, a, out, dbg=()):
    pe, dve, act, pool, sp = nc.tensor, nc.vector, nc.scalar, nc.gpsimd, nc.sync
    sems = Sems(nc, 90)
    whole = ExitStack()

    def dram(name, shape, dt=F32):
        kind = "ExternalOutput" if name in dbg else "Internal"
        return nc.dram_tensor(name, list(shape), dt, kind=kind).ap()

    hT_d = dram("hT_d", [KT, P, TOK])
    qkv_d = dram("qkv_d", [3, TOK, C])
    beta_d = dram("beta_d", [H, TOK])
    taps_d = dram("taps_d", [C, 2, RW])
    fir_d = dram("fir_d", [2, TOK, C])
    gram_d = dram("gram_d", [UNITS, P, CH])
    tinv_d = dram("tinv_d", [UNITS, P, CH])
    delta_d = dram("delta_d", [TOK, C])
    x2_d = dram("x2_d", [TOK, C])
    h2_d = dram("h2_d", [TOK, C])
    key_d = dram("key_d", [TOK * NE, 1])
    routed_d = dram("routed_d", [B * CAP * NE, C])

    def sb(stack, name, shape, dt=F32):
        return stack.enter_context(nc.sbuf_tensor(name, list(shape), dt))

    def ps(stack, name, shape):
        return stack.enter_context(nc.psum_tensor(name, list(shape), F32))

    def barrier():
        nc.all_engine_barrier()

    ident = sb(whole, "ident", [P, P])
    ones = sb(whole, "ones", [P, P])
    blockdiag = sb(whole, "blockdiag", [P, P])
    causal = sb(whole, "causal", [P, P])
    parity = sb(whole, "parity", [P, 2])
    rows = sb(whole, "rows", [P, 4, B, C])
    scT = sb(whole, "scT", [P, B, 2, KT])
    mean = sb(whole, "mean", [P, TILES])
    rstd = sb(whole, "rstd", [P, TILES])
    gates = sb(whole, "gates", [P, TPB, B, NE])

    with ExitStack() as st:
        p = sems.loop(1)
        cT = sb(st, "cT", [P, KT, B])
        cs = sb(st, "cs", [P, KT, B])
        crep = sb(st, "crep", [P, KT, B, P])
        wmod = sb(st, "wmod", [P, KT, 6 * C])
        xs = sb(st, "xs", [P, TILES, C])
        bst = sb(st, "bst", [P, TILES, 6])
        ta = sb(st, "ta", [P, TILES])
        tb = sb(st, "tb", [P, TILES])
        sgn = sb(st, "sgn", [P, 2, B, C])
        mag = sb(st, "mag", [P, 2, B, C])
        tapr = sb(st, "tapr", [P, KT, 2, RW])
        pcol = ps(st, "pcol", [P, 2, KT, B])
        prow = ps(st, "prow", [P, 2, 512])

        s_c, s_x, s_tap, s_tapz, s_tapo = p.dma(2), p.dma(4), p.dma(2 * KT), p.step(), p.dma()
        for src, n in ((a["cT"], 0), (a["wmod"], 1)):
            s_c.by(sp.dma_start((cT if n == 0 else wmod)[:, :, :], src.rearrange("(k p) n -> p k n", p=P)))
        for b in range(4):
            nt = TILES // 4
            s_x.by(sp.dma_start(xs[:, nt * b:nt * (b + 1), :],
                                a["x"][b * nt * P:(b + 1) * nt * P, :].rearrange("(t p) c -> p t c", p=P)))
        s_tapz.by(dve.memset(tapr[:, :, :, :], 0.0))
        s_tapz.wait(act)
        for k in range(KT):
            s_tap.by(act.dma_start(tapr[:, k, 0, BLK - 1:BLK - 1 + FIRL], a["fir_l"][k * P:(k + 1) * P, :]))
            s_tap.by(act.dma_start(tapr[:, k, 1, BLK - 1 + FIRL - FIRS:BLK - 1 + FIRL], a["fir_s"][k * P:(k + 1) * P, :]))
        s_tap.wait(act)
        s_tapo.by(act.dma_start(taps_d.rearrange("(k p) f w -> p k f w", p=P), tapr[:, :, :, :]))

        s_sel = p.step(4 + 3 * H)
        n_sel = 0

        def in_order(ins):
            nonlocal n_sel
            n_sel += 1
            s_sel.by(ins)
            s_sel.wait(pool, n_sel)

        in_order(pool.memset(ones[:, :], 1.0))
        in_order(pool.affine_select(out=ident[:, :], in_=ones[:, :], pattern=[[-1, P]], compare_op=ALU.is_equal,
                                    fill=0.0, base=0, channel_multiplier=1))
        in_order(pool.memset(parity[:, :], 0.0))
        in_order(pool.memset(blockdiag[:, :], 0.0))
        pool.wait_ge(s_sel.sem, s_sel.base + n_sel)
        causal_z = p.step()
        causal_z.by(pool.memset(causal[:, :], 0.0))
        causal_z.wait(pool)
        for h in range(H):
            r = slice(CH * h, CH * (h + 1))
            in_order(pool.memset(parity[r, h % 2:h % 2 + 1], 1.0))
            in_order(pool.memset(blockdiag[r, r], 1.0))
            in_order(pool.affine_select(out=causal[r, r], in_=ones[r, 0:CH], pattern=[[1, CH]],
                                        compare_op=ALU.is_ge, fill=0.0, base=0, channel_multiplier=-1))

        s_silu, s_rep, s_col, s_cole = p.step(), p.step(), p.step(), p.step(2)
        s_c.wait(act)
        s_silu.by(act.activation(cs[:, :, :], cT[:, :, :], ACT.Silu))
        s_silu.wait(dve)
        s_rep.by(dve.tensor_copy(crep[:, :, :, :], cs[:, :, :].unsqueeze(3).broadcast_to([P, KT, B, P])))
        s_c.wait(pe)
        s_silu.wait(pe)
        for w in range(2):
            for m in range(KT):
                for k in range(KT):
                    i = pe.matmul(pcol[:, w, m, :], wmod[:, k, w * C + m * P:w * C + (m + 1) * P], cs[:, k, :],
                                  start=(k == 0), stop=(k == KT - 1))
        s_col.by(i)
        s_col.wait(dve)
        for w in range(2):
            s_cole.by(dve.tensor_scalar(scT[:, :, w, :], pcol[:, w, :, :].rearrange("p m b -> p b m"),
                                        float(w), None, ALU.add))
        s_rep.wait(pe)
        s_row, s_rowe = p.step(2 * B), p.step(2 * B)
        for b in range(B):
            for g in range(2):
                n = b * 2 + g
                if n >= 2:
                    s_rowe.wait(pe, n - 1)
                for k in range(KT):
                    i = pe.matmul(prow[:, n % 2, :], crep[:, k, b, :], wmod[:, k, 2 * C + g * 512:2 * C + (g + 1) * 512],
                                  start=(k == 0), stop=(k == KT - 1))
                s_row.by(i)
                s_row.wait(dve, n + 1)
                s_rowe.by(dve.tensor_copy(rows[:, 2 * g:2 * g + 2, b, :], prow[:, n % 2, :].rearrange("p (r c) -> p r c", r=2)))
        s_sg, s_ab, s_rfin = p.step(4), p.step(2), p.step(3)
        s_rowe.wait(dve)
        for n, r in enumerate((0, 3)):
            s_sg.by(dve.tensor_scalar(sgn[:, n, :, :], rows[:, r, :, :], 0.0, 2.0, ALU.is_ge, ALU.mult))
            g = rows[:, r, :, :].rearrange("p b c -> p (b c)")
            m = mag[:, n, :, :].rearrange("p b c -> p (b c)")
            s_sg.by(dve.scalar_tensor_tensor(m, g, -1.0, g, ALU.mult, ALU.max))
        s_sg.wait(dve)
        for n in range(2):
            s_ab.by(dve.tensor_scalar(mag[:, n, :, :], mag[:, n, :, :], 0.25, None, ALU.max))
        s_ab.wait(dve)
        for n, r in enumerate((0, 3)):
            s_rfin.by(dve.scalar_tensor_tensor(rows[:, r, :, :].rearrange("p b c -> p (b c)"),
                                               sgn[:, n, :, :].rearrange("p b c -> p (b c)"), 1.0,
                                               mag[:, n, :, :].rearrange("p b c -> p (b c)"), ALU.subtract, ALU.mult))
        s_rfin.by(dve.tensor_scalar(rows[:, 2, :, :], rows[:, 2, :, :], 1.0, None, ALU.add))

        s_x.wait(dve)
        q = sems.loop(TILES // 4)
        s_b = q.step()
        with nc.Fori(0, TILES // 4, engines=[ENG.DVE]) as i:
            for n in range(4):
                last = dve.bn_stats(bst[:, bass.ds(i * 4 + n, 1), :].rearrange("p a s -> p (a s)"),
                                    xs[:, bass.ds(i * 4 + n, 1), :].rearrange("p a c -> p (a c)"))
            s_b.by(last)
        s_b.wait_all(dve)
        s_v = p.step(7)
        v = 0

        def chain(ins):
            nonlocal v
            v += 1
            s_v.by(ins)
            s_v.wait(dve, v)

        chain(dve.tensor_tensor(mean[:, :], bst[:, :, 1], bst[:, :, 4], ALU.add))
        chain(dve.tensor_tensor(ta[:, :], bst[:, :, 1], bst[:, :, 4], ALU.subtract))
        chain(dve.tensor_tensor(tb[:, :], bst[:, :, 2], bst[:, :, 5], ALU.add))
        chain(dve.tensor_tensor(ta[:, :], ta[:, :], ta[:, :], ALU.mult))
        chain(dve.tensor_scalar(tb[:, :], tb[:, :], 1.0 / C, EPS_LN, ALU.mult, ALU.add))
        chain(dve.scalar_tensor_tensor(tb[:, :], ta[:, :], 0.25, tb[:, :], ALU.mult, ALU.add))
        chain(dve.tensor_scalar(mean[:, :], mean[:, :], -0.5, None, ALU.mult))
        s_sq, s_rs = p.step(), p.step()
        s_v.wait(act)
        s_sq.by(act.activation(ta[:, :], tb[:, :], ACT.Sqrt))
        s_sq.wait(dve)
        s_rs.by(dve.reciprocal(rstd[:, :], ta[:, :]))
        s_tapo.wait(act)
        barrier()
        q.close()
        p.close()

    with ExitStack() as st:
        wqkv = sb(st, "wqkv", [P, KT, 3, C])
        wb = sb(st, "wb", [P, KT, H])
        cw = sb(st, "cw", [P, 6, TAPS])
        proj = sb(st, "proj", [P, 6, TAPS - 1 + L])
        xw = sb(st, "xw", [P, 2, WIN // P, C])
        xn = sb(st, "xn", [P, 2, WIN // P, C])
        cur = sb(st, "cur", [P, 2, KT])
        hT = sb(st, "hT", [P, KT, WIN])
        acc = sb(st, "acc", [P, 2, WIN])
        sil = sb(st, "sil", [P, 3, WIN])
        tm = sb(st, "tm", [P, WIN // P, 3, C])
        bT = sb(st, "bT", [H, WIN])
        pT = ps(st, "pT", [P, KT, WIN])
        pP = ps(st, "pP", [P, 3, WIN])
        pB = ps(st, "pB", [P, WIN])
        pK = ps(st, "pK", [P, 2, WIN])
        NM = 6

        p = sems.loop(1)
        s_w, s_z = p.dma(7), p.step()
        for n, w in enumerate(("Wq", "Wk", "Wv")):
            s_w.by(sp.dma_start(wqkv[:, :, n, :], a[w].rearrange("(k p) n -> p k n", p=P)))
        s_w.by(sp.dma_start(wb[:, :, :], a["Wb"].rearrange("(k p) n -> p k n", p=P)))
        for n, w in enumerate(("qc", "kc", "vc")):
            s_w.by(sp.dma_start(cw[:, 2 * n:2 * n + 2, :], a[w].rearrange("(k p) n -> p k n", p=P)))
        s_z.by(dve.memset(proj[:, :, 0:TAPS - 1], 0.0))
        for e in (pe, act, dve):
            s_w.wait(e)
        s_z.wait(dve)

        q = sems.loop(TOK // WIN)
        NW = L // WIN
        s_ld, s_cur, s_ln = q.dma(), q.step(), q.step(4)
        s_tr, s_ht, s_hto = q.step(), q.step(2), q.dma()
        s_pr, s_bt, s_be, s_bo = q.step(NM), q.step(), q.step(), q.dma()
        s_ev, s_cv, s_si, s_tt, s_te, s_tmo = (q.step(NM), q.step(3 * NM), q.step(NM), q.step(NM), q.step(NM), q.dma(3))
        with nc.Fori(0, B) as b, nc.Fori(0, NW) as j:
            q.it = b * NW + j
            s_ln.wait_last(sp)
            s_ld.by(sp.dma_start(xw[:, 0, :, :], a["x"][bass.ds(q.it * WIN, WIN), :].rearrange("(t p) c -> p t c", p=P)))
            s_ht.wait_last(dve)
            s_cur.by(dve.tensor_copy(cur[:, :, :], scT[:, bass.ds(b, 1), :, :].rearrange("p a w k -> p (a w) k")))
            s_ld.wait(dve)
            s_tr.wait_last(dve)
            for t in range(4):
                s_ln.by(dve.tensor_scalar(xn[:, 0, t, :], xw[:, 0, t, :], mean[:, bass.ds(q.it * 4 + t, 1)],
                                          rstd[:, bass.ds(q.it * 4 + t, 1)], ALU.add, ALU.mult))
            s_ln.wait(pe)
            s_ht.wait_last(pe)
            for k in range(KT):
                for t in range(4):
                    i = pe.transpose(pT[:, k, t * P:(t + 1) * P], xn[:, 0, t, k * P:(k + 1) * P], ident[:, :])
            s_tr.by(i)
            s_tr.wait(act)
            s_cur.wait(act)
            s_hto.wait_last(act)
            s_pr.wait_last(act)
            s_bt.wait_last(act)
            for k in range(KT):
                s_ht.by(act.activation(hT[:, k, :], pT[:, k, :], ACT.Identity, bias=cur[:, 0, k:k + 1], scale=cur[:, 1, k:k + 1]))
            s_ht.wait(sp)
            s_hto.by(sp.dma_start(hT_d.rearrange("k p t -> p k t")[:, :, bass.ds(q.it * WIN, WIN)], hT[:, :, :]))
            s_ht.wait(pe)

            def project(m):
                if m >= 3:
                    s_ev.wait(pe, m - 2)
                else:
                    s_ev.wait_last(pe)
                for k in range(KT):
                    i = pe.matmul(pP[:, m % 3, :], wqkv[:, k, m // 2, (m % 2) * P:(m % 2 + 1) * P], hT[:, k, :],
                                  start=(k == 0), stop=(k == KT - 1))
                s_pr.by(i)

            def convolve(m):
                s_pr.wait(act, m + 1)
                if m >= 2:
                    s_si.wait(act, m - 1)
                act.activation(proj[:, m, bass.ds(j * WIN + TAPS - 1, WIN)], pP[:, m % 3, :], ACT.Copy)
                s_ev.by(act.activation(acc[:, m % 2, :], pP[:, m % 3, :], ACT.Copy, scale=cw[:, m, TAPS - 1:TAPS]))
                s_ev.wait(dve, m + 1)
                for n, tap in enumerate((2, 1, 0)):
                    if n:
                        s_cv.wait(dve, 3 * m + n)
                    s_cv.by(dve.scalar_tensor_tensor(acc[:, m % 2, :], proj[:, m, bass.ds(j * WIN + tap, WIN)],
                                                     cw[:, m, tap:tap + 1], acc[:, m % 2, :], ALU.mult, ALU.add))

            def silu(m):
                s_cv.wait(act, 3 * m + 3)
                if m >= 3:
                    s_tt.wait(act, m - 2)
                else:
                    s_tt.wait_last(act)
                s_si.by(act.activation(sil[:, m % 3, :], acc[:, m % 2, :], ACT.Silu))

            def to_tokens(m):
                s_si.wait(pe, m + 1)
                if m >= 2:
                    s_te.wait(pe, m - 1)
                else:
                    s_te.wait_last(pe)
                for t in range(4):
                    i = pe.transpose(pK[:, m % 2, t * P:(t + 1) * P], sil[:, m % 3, t * P:(t + 1) * P], ident[:, :])
                s_tt.by(i)

            def keep_tokens(m, e):
                s_tt.wait(e, m + 1)
                if m == 0:
                    s_tmo.wait_last(e)
                dst = tm[:, :, m // 2, (m % 2) * P:(m % 2 + 1) * P]
                src = pK[:, m % 2, :].rearrange("p (t c) -> p t c", t=4)
                s_te.by(e.tensor_copy(dst, src))

            for m in range(3):
                project(m)
            s_be.wait_last(pe)
            for k in range(KT):
                i = pe.matmul(pB[0:H, :], wb[:, k, :], hT[:, k, :], start=(k == 0), stop=(k == KT - 1))
            s_bt.by(i)
            for m in range(NM + 2):
                if m < NM:
                    convolve(m)
                if 1 <= m <= NM:
                    silu(m - 1)
                    if 3 <= m + 2 < NM:
                        project(m + 2)
                    to_tokens(m - 1)
                if m >= 2:
                    keep_tokens(m - 2, dve)
            s_bt.wait(act)
            s_bo.wait_last(act)
            s_be.by(act.activation(bT[:, :], pB[0:H, :], ACT.Copy))
            s_be.wait(act)
            s_bo.by(act.dma_start(beta_d[:, bass.ds(q.it * WIN, WIN)], bT[:, :]))
            for n in range(3):
                s_te.wait(sp, 2 * n + 2)
                s_tmo.by(sp.dma_start(qkv_d[n, bass.ds(q.it * WIN, WIN), :].rearrange("(t p) c -> p t c", p=P), tm[:, :, n, :]))
        for s in (s_hto, s_bo, s_tmo):
            s.wait_all(sp)
        barrier()
        q.close()
        p.close()
    hold = ExitStack()
    rnorm = sb(hold, "rnorm", [P, UNITS])
    betac = sb(hold, "betac", [P, UNITS])
    with ExitStack() as st:
        NU = 8
        turns = UNITS // NU
        kq = sb(st, "kq", [P, 2, 2, NU, D])
        sqr = sb(st, "sqr", [P, 2, NU, D])
        ssum = sb(st, "ssum", [P, 2, NU])
        root = sb(st, "root", [P, 2, NU])
        kn = sb(st, "kn", [P, NU, D])
        kT2 = sb(st, "kT2", [D, NU, P])
        gr = sb(st, "gr", [P, 2, NU, CH])
        bu = sb(st, "bu", [P, 2, H, CH])
        pk2 = ps(st, "pk2", [P, NU, P])
        pg2 = ps(st, "pg2", [P, NU, P])

        p = sems.loop(1)
        s_bl, s_sg, s_bt, s_bc = p.dma(2 * H), p.step(), p.step(), p.step()
        for h in range(H):
            for w in range(2):
                s_bl.by(sp.dma_start(bu[:, w, h, :], beta_d[h, w * TOK // 2:(w + 1) * TOK // 2].rearrange("(u i) -> u i", i=CH)))
        s_bl.wait(act)
        s_sg.by(act.activation(bu[:, :, :, :], bu[:, :, :, :], ACT.Sigmoid))
        s_sg.wait(pe)
        for w in range(2):
            i = pe.transpose(pk2[:, w, :], bu[:, w, :, :].rearrange("p h i -> p (h i)"), ident[:, :])
        s_bt.by(i)
        s_bt.wait(dve)
        s_bc.by(dve.tensor_copy(betac[:, :], pk2[:, 0:2, :].rearrange("p w u -> p (w u)")))
        s_bc.wait(pe)

        q = sems.loop(turns)
        s_ld, s_go = Pair(sems, turns, 2 * H), Pair(sems, turns)
        s_n, s_rt, s_rn, s_kn = q.step(3), q.step(), q.step(), q.step()
        s_tr, s_kt, s_gm, s_ge = q.step(), q.step(2), q.step(), q.step(H)

        def norms(t, par, half):
            s_kn.back(sp, t, 2)
            for h in range(H):
                for n in range(2):
                    src = qkv_d[n, bass.ds(t * NU * CH, NU * CH), h * D:(h + 1) * D].rearrange("(u i) d -> i u d", i=CH)
                    s_ld.by(sp.dma_start(kq[h * CH:(h + 1) * CH, par, n, :, :], src), par)
            s_ld.wait(dve, par, half)
            s_n.by(dve.tensor_tensor(sqr[:, :, :, :], kq[:, par, :, :, :], kq[:, par, :, :, :], ALU.mult))
            s_n.wait(dve, 1, t=t)
            s_n.by(dve.tensor_reduce(ssum[:, :, :], sqr[:, :, :, :], AX, ALU.add))
            s_n.wait(dve, 2, t=t)
            s_n.by(dve.tensor_scalar(ssum[:, :, :], ssum[:, :, :], EPS_L2, None, ALU.add))
            yield
            s_n.wait(act, 3, t=t)
            s_rt.by(act.activation(root[:, :, :], ssum[:, :, :], ACT.Sqrt))
            s_rt.wait(dve, t=t)
            s_rn.by(dve.reciprocal(rnorm[:, bass.ds(t * NU, NU)], root[:, 1, :]))
            s_rn.wait(dve, t=t)
            s_tr.back(dve, t, 1)
            s_kn.by(dve.tensor_tensor(kn[:, :, :], kq[:, par, 1, :, :],
                                      rnorm[:, bass.ds(t * NU, NU)].unsqueeze(2).broadcast_to([P, NU, D]), ALU.mult))

        def gram(t, par, half):
            s_kt.back(pe, t, 1, alone=True)
            s_kn.wait(pe, t=t, alone=True)
            for u in range(NU):
                i = pe.transpose(pk2[0:D, u, :], kn[:, u, :], ident[:, :])
            s_tr.by(i)
            s_tr.wait(act, t=t)
            s_gm.back(act, t, 1)
            for w in range(2):
                s_kt.by(act.activation(kT2[:, 4 * w:4 * w + 4, :], pk2[0:D, 4 * w:4 * w + 4, :], ACT.Copy))
            yield
            s_kt.wait(pe, t=t)
            s_ge.back(pe, t, 1)
            for u in range(NU):
                i = pe.matmul(pg2[:, u, :], kT2[:, u, :], kT2[:, u, :], start=True, stop=True)
            s_gm.by(i)
            s_go.free(act, par, half)
            s_go.free(dve, par, half)
            for h in range(H):
                e = act if h % 2 else dve
                s_gm.wait(e, t=t)
                r = slice(h * CH, (h + 1) * CH)
                if h % 2:
                    s_ge.by(act.activation(gr[r, par, :, :], pg2[r, :, r], ACT.Copy))
                else:
                    s_ge.by(dve.tensor_copy(gr[r, par, :, :], pg2[r, :, r]))
            s_ge.wait(act, t=t)
            s_go.by(act.dma_start(gram_d[bass.ds(t * NU, NU)].rearrange("u p j -> p u j"), gr[:, par, :, :]), par)

        pipeline(nc, turns, norms, gram)
        s_go.wait_all(sp)
        barrier()
        s_go.close()
        s_ld.close()
        q.close()
        p.close()

    with ExitStack() as st:
        QC, G = 64, 4
        NS = UNITS * H // P
        vwin = sb(st, "vwin", [SPAN, NBLK, QC])
        band = sb(st, "band", [SPAN, 2, G, 2, BLK])
        vst = sb(st, "vst", [SPAN, 2, G, NBLK])
        fo = sb(st, "fo", [NBLK, 2, 2, BLK, QC])
        amat = sb(st, "amat", [P, NS, CH, CH])
        tinv = sb(st, "tinv", [P, NS, CH, CH])
        prod = sb(st, "prod", [P, NS, CH * CH // 4])
        bs = sb(st, "bs", [P, NS, CH])
        pf = ps(st, "pf", [NBLK, 2, G, 2, BLK])

        p = sems.loop(1)
        s_a, s_sg, s_i = p.dma(1 + H), p.step(), p.step(3)
        s_a.by(act.dma_start(amat[:, :, :, :].rearrange("p s i j -> p (s i j)"),
                             gram_d.rearrange("u (h i) j -> (u h i j)", h=H).rearrange("(p x) -> p x", p=P)))
        for h in range(H):
            s_a.by(act.dma_start(bs[:, :, :].rearrange("p (u h) i -> p u h i", h=H)[:, :, h, :],
                                 beta_d[h].rearrange("(p u i) -> p u i", p=P, i=CH)))
        s_i.by(dve.memset(tinv[:, :, :, :], 0.0))
        s_a.wait(act)
        s_sg.by(act.activation(bs[:, :, :], bs[:, :, :], ACT.Sigmoid))
        s_i.wait(dve, 1)
        s_i.by(dve.memset(tinv[:, :, :, :].rearrange("p s i j -> p s (i j)")[:, :, 0:CH * CH:CH + 1], 1.0))
        s_sg.wait(dve)
        s_i.by(dve.tensor_tensor(amat[:, :, :, :], amat[:, :, :, :],
                                 bs[:, :, :].unsqueeze(3).broadcast_to([P, NS, CH, CH]), ALU.mult))
        s_i.wait(dve)
        s_f = p.step(2 * (CH - 1))
        for j in range(CH - 1):
            nc_, ni = j + 1, CH - 1 - j
            col = amat[:, :, j + 1:, j].unsqueeze(2).broadcast_to([P, NS, nc_, ni])
            row = tinv[:, :, 0:nc_, j].unsqueeze(3).broadcast_to([P, NS, nc_, ni])
            tmp = prod[:, :, 0:nc_ * ni].rearrange("p s (c i) -> p s c i", c=nc_)
            s_f.by(dve.tensor_tensor(tmp, col, row, ALU.mult))
            s_f.wait(dve, 2 * j + 1)
            s_f.by(dve.tensor_tensor(tinv[:, :, 0:nc_, j + 1:], tinv[:, :, 0:nc_, j + 1:], tmp, ALU.subtract))
            s_f.wait(dve, 2 * j + 2)

        s_vz, s_v = p.step(B), p.dma(4 * (B + B))
        GT = QC // G
        q = sems.loop(4 * GT // 2)
        s_bd, s_cp, s_mm, s_ev = [[make() for _ in range(2)] for make in (q.dma, q.step, q.step, q.step)]
        s_fo = Pair(sems, 4, 2)
        for b in range(B):
            s_vz.by(pool.memset(vwin[0:FIRL - 1, b * (NBLK // B), :], 0.0))
        s_vz.wait(sp)
        s_vz.wait(pool)
        for c4 in range(C // QC):
            c0 = c4 * QC
            if c4:
                for par in range(2):
                    s_cp[par].wait(sp, t=c4 * GT // 2 - 1)
            for b in range(B):
                vb = qkv_d[2, b * L:(b + 1) * L, c0:c0 + QC]
                nb = NBLK // B
                wins = bass.AP(vb.tensor, vb.offset + (BLK - FIRL + 1) * C, [[C, SPAN], [BLK * C, nb - 1], [1, QC]])
                s_v.by(sp.dma_start(vwin[:, b * nb + 1:(b + 1) * nb, :], wins))
                s_v.by(sp.dma_start(vwin[FIRL - 1:SPAN, b * nb, :], vb[0:BLK, :]))
            s_v.wait(pool, 16 * 8 * (c4 + 1))
            s_fo.free(act, c4 % 2, c4 // 2)
            with nc.Fori(0, GT // 2, engines=[ENG.SP, ENG.PE, ENG.Activation, ENG.Pool]) as i:
                for par in range(2):
                    t2 = i + c4 * GT // 2
                    s_mm[par].back(sp, t2, 1)
                    cb = (i * (2 * G) + (c0 + par * G)) * (2 * RW)
                    src = bass.AP(taps_d.tensor, cb, [[1, SPAN], [RW, 2 * G], [1, BLK]])
                    s_bd[par].by(sp.dma_start(band[:, par, :, :, :].rearrange("p g f t -> p (g f) t"), src))
                    s_mm[par].back(pool, t2, 1)
                    s_cp[par].by(pool.tensor_copy(vst[:, par, :, :], vwin[:, :, bass.ds((i * 2 + par) * G, G)].rearrange("p n g -> p g n")))
                    s_cp[par].wait(pe, t=t2)
                    s_bd[par].wait(pe, t=t2)
                    s_ev[par].back(pe, t2, 1)
                    for g in range(G):
                        mm = pe.matmul(pf[:, par, g, :, :], vst[:, par, g, :], band[:, par, g, :, :], start=True, stop=True)
                    s_mm[par].by(mm)
                    s_mm[par].wait(act, t=t2)
                    s_ev[par].by(act.activation(fo[:, c4 % 2, :, :, bass.ds((i * 2 + par) * G, G)],
                                                pf[:, par, :, :, ::-1].rearrange("p g f t -> p f t g"), ACT.Copy))
            s_ev[0].wait(sp, t=(c4 + 1) * GT // 2 - 1)
            s_ev[1].wait(sp, t=(c4 + 1) * GT // 2 - 1)
            for f in range(2):
                dst = fir_d[f, :, c0:c0 + QC].rearrange("(n t) c -> n t c", t=BLK)
                s_fo.by(sp.dma_start(dst, fo[:, c4 % 2, f, :, :]), c4 % 2)
        s_to = p.dma()
        s_f.wait(sp)
        s_to.by(sp.dma_start(tinv_d.rearrange("u (h i) j -> (u h i j)", h=H).rearrange("(p x) -> p x", p=P),
                             tinv[:, :, :, :].rearrange("p s i j -> p (s i j)")))
        s_to.wait(sp)
        s_fo.wait_all(sp)
        barrier()
        s_fo.close()
        q.close()
        p.close()

    with ExitStack() as st:
        turns = CPB
        NP = H // 2
        rk = sb(st, "rk", [P, 2, UNITS])
        kqv = sb(st, "kqv", [P, 4, 3, B, D])
        tc = sb(st, "tc", [P, 4, B, CH])
        kx = sb(st, "kx", [P, 4, B, P])
        qx = sb(st, "qx", [P, 4, B, P])
        qq = sb(st, "qq", [P, 4, B, D])
        rq = sb(st, "rq", [P, 4, B])
        kbx = sb(st, "kbx", [P, 4, B, P])
        vb = sb(st, "vb", [P, 4, B, D])
        tx = sb(st, "tx", [P, 4, B, P])
        kT = sb(st, "kT", [P, 4, B, P])
        qT = sb(st, "qT", [P, 4, B, P])
        atT = sb(st, "atT", [P, 4, B, P])
        wT = sb(st, "wT", [P, 4, B, P])
        uu = sb(st, "uu", [P, 4, B, D])
        ui = sb(st, "ui", [P, 4, B, D])
        state = sb(st, "state", [P, B, NP, D])
        do = sb(st, "do", [P, 4, B, D])
        pA = ps(st, "pA", [P, B, P])
        pBq = ps(st, "pBq", [P, B, P])
        pC = ps(st, "pC", [P, B, P])
        pD = ps(st, "pD", [P, B, P])
        pF = ps(st, "pF", [P, B, 2 * D])
        pG = ps(st, "pG", [P, B, 2 * D])
        pH = ps(st, "pH", [P, NP, 512])

        p = sems.loop(1)
        s_z, s_r = p.step(), p.step(2)
        s_z.by(dve.memset(state[:, :, :, :], 0.0))
        for s in range(2):
            s_r.by(dve.tensor_scalar(rk[:, s, :], rnorm[:, :], parity[:, s:s + 1], None, ALU.mult))
        s_r.wait(pool)
        s_z.wait(pe)
        q = sems.loop(turns)
        s_ld, s_do = Ring(sems, turns, H + 1), Ring(sems, turns, H)
        s_kx, s_qx, s_kb, s_vb, s_tx = q.step(), q.step(), q.step(), q.step(), q.step()
        s_qq, s_qn, s_qr, s_rq = q.step(), q.step(2), q.step(), q.step()
        s_tk, s_tq, s_ek, s_eq = q.step(), q.step(), q.step(), q.step()
        s_at, s_ea, s_w, s_ew, s_u, s_eu = q.step(), q.step(), q.step(), q.step(), q.step(), q.step()
        s_ws, s_ui, s_qs, s_ku, s_st, s_o, s_eo = [q.step() for _ in range(7)]

        def unit_cols(ap2, t):
            return ap2.rearrange("p (b c) -> p b c", b=B)[:, :, bass.ds(t, 1)].rearrange("p b c -> p (b c)")

        def per_half(x):
            return x.rearrange("p b (s d) -> p b s d", s=2)

        def load4(t, slot, round):
            for s in (s_kx, s_qx, s_vb, s_tx, s_qq):
                s.back(sp, t, 4)
            for h in range(H):
                src = qkv_d[:, :, h * D:(h + 1) * D].rearrange("n (b c i) f -> c i n b f", b=B, i=CH)
                s_ld.by(sp.dma_start(kqv[h * CH:(h + 1) * CH, slot, :, :, :],
                                     src[bass.ds(t, 1)].rearrange("o i n b f -> (o i) n b f")), slot)
            s_ld.by(sp.dma_start(tc[:, slot, :, :], tinv_d.rearrange("(b c) p i -> c p b i", b=B)[bass.ds(t, 1)]
                                 .rearrange("o p b i -> (o p) b i")), slot)

        def expand(t, slot, round):
            s_ld.wait(pool, slot, round)
            s_ku.back(pool, t, 4)
            s_tk.back(pool, t, 4)
            s_kb.back(pool, t, 4)
            sc = rk[:, :, :].rearrange("p s (b c) -> p b s c", b=B)[:, :, :, bass.ds(t, 1)].rearrange("p b s c -> p b (s c)")
            s_kx.by(pool.tensor_tensor(per_half(kx[:, slot, :, :]), kqv[:, slot, 1, :, :].unsqueeze(2).broadcast_to([P, B, 2, D]),
                                       sc.unsqueeze(3).broadcast_to([P, B, 2, D]), ALU.mult))
            s_tq.back(pool, t, 4)
            s_qx.by(pool.tensor_tensor(per_half(qx[:, slot, :, :]), kqv[:, slot, 0, :, :].unsqueeze(2).broadcast_to([P, B, 2, D]),
                                       parity[:, :].unsqueeze(1).unsqueeze(3).broadcast_to([P, B, 2, D]), ALU.mult))
            beta = unit_cols(betac[:, :], t)
            s_u.back(pool, t, 4)
            s_vb.by(pool.tensor_tensor(vb[:, slot, :, :], kqv[:, slot, 2, :, :], beta.unsqueeze(2).broadcast_to([P, B, D]), ALU.mult))
            s_ld.wait(act, slot, round)
            s_qn.back(act, t, 4)
            s_qq.by(act.activation(qq[:, slot, :, :], kqv[:, slot, 0, :, :], ACT.Square))
            s_ld.wait(dve, slot, round)
            s_u.back(dve, t, 4)
            s_w.back(dve, t, 4)
            s_tx.by(dve.tensor_tensor(tx[:, slot, :, :].rearrange("p b (h i) -> p b h i", h=H),
                                      tc[:, slot, :, :].unsqueeze(2).broadcast_to([P, B, H, CH]),
                                      blockdiag[:, :].rearrange("p (h i) -> p h i", h=H).unsqueeze(1).broadcast_to([P, B, H, CH]),
                                      ALU.mult))

        def turn_kq(t, slot, round):
            s_kx.wait(pe, t=t)
            s_eu.back(pe, t, 1)
            for b in range(B):
                i = pe.transpose(pA[:, b, :], kx[:, slot, b, :], ident[:, :])
            s_tk.by(i)
            s_qx.wait(pe, t=t)
            s_eq.back(pe, t, 1)
            for b in range(B):
                i = pe.transpose(pBq[:, b, :], qx[:, slot, b, :], ident[:, :])
            s_tq.by(i)
            s_tk.wait(act, t=t)
            s_at.back(act, t, 4)
            s_ek.by(act.activation(kT[:, slot, :, :], pA[:, :, :], ACT.Copy))
            s_tq.wait(act, t=t)
            s_qs.back(act, t, 4)
            s_eq.by(act.activation(qT[:, slot, :, :], pBq[:, :, :], ACT.Copy))
            s_kx.wait(dve, t=t)
            s_w.back(dve, t, 4)
            s_kb.by(dve.tensor_tensor(kbx[:, slot, :, :], kx[:, slot, :, :],
                                      unit_cols(betac[:, :], t).unsqueeze(2).broadcast_to([P, B, P]), ALU.mult))
            s_qq.wait(dve, t=t)
            s_eo.back(dve, t, 4)
            s_qn.by(dve.tensor_reduce(rq[:, slot, :], qq[:, slot, :, :], AX, ALU.add))
            s_qn.wait(dve, 1, t=t)
            s_qn.by(dve.tensor_scalar(rq[:, slot, :], rq[:, slot, :], EPS_L2, None, ALU.add))

        def q_root(t, slot, round):
            s_qn.wait(act, t=t)
            s_qr.by(act.activation(rq[:, slot, :], rq[:, slot, :], ACT.Sqrt))

        def q_inverse(t, slot, round):
            s_qr.wait(dve, t=t)
            s_rq.by(dve.reciprocal(rq[:, slot, :], rq[:, slot, :]))

        def attention(t, slot, round):
            s_ek.wait(pe, t=t)
            s_eq.wait(pe, t=t)
            s_ea.back(pe, t, 1)
            for b in range(B):
                i = pe.matmul(pC[:, b, :], kT[:, slot, b, :], qT[:, slot, b, :], start=True, stop=True)
            s_at.by(i)
            s_at.wait(dve, t=t)
            s_o.back(dve, t, 4)
            s_ea.by(dve.tensor_tensor(atT[:, slot, :, :], pC[:, :, :], causal[:, :].unsqueeze(1).broadcast_to([P, B, P]), ALU.mult))

        def w_and_u(t, slot, round):
            s_kb.wait(pe, t=t)
            s_tx.wait(pe, t=t)
            s_ew.back(pe, t, 1)
            for b in range(B):
                i = pe.matmul(pD[:, b, :], kbx[:, slot, b, :], tx[:, slot, b, :], start=True, stop=True)
            s_w.by(i)
            s_w.wait(act, t=t)
            s_ws.back(act, t, 4)
            s_ew.by(act.activation(wT[:, slot, :, :], pD[:, :, :], ACT.Copy))
            s_vb.wait(pe, t=t)
            s_ek.wait(pe, t=t)
            for b in range(B):
                i = pe.matmul(pA[:, b, 0:D], tx[:, slot, b, :], vb[:, slot, b, :], start=True, stop=True)
            s_u.by(i)
            s_u.wait(act, t=t)
            s_ui.back(act, t, 4)
            s_eu.by(act.activation(uu[:, slot, :, :], pA[:, :, 0:D], ACT.Copy))

        def correct(t, slot, round):
            s_st.back(pe, t, 1)
            s_ew.wait(pe, t=t)
            s_ui.back(pe, t, 1)
            for b in range(B):
                for n in range(NP):
                    r = slice(n * D, (n + 1) * D)
                    i = pe.matmul(pF[r, b, 0:D], wT[:, slot, b, r], state[:, b, n, :], start=True, stop=True)
            s_ws.by(i)
            s_ws.wait(dve, t=t)
            s_eu.wait(dve, t=t)
            s_ku.back(dve, t, 4)
            s_o.back(dve, t, 4)
            s_ui.by(dve.tensor_tensor(ui[:, slot, :, :], uu[:, slot, :, :], pF[:, :, 0:D], ALU.subtract))
            s_eo.back(pe, t, 1)
            for b in range(B):
                for n in range(NP):
                    r = slice(n * D, (n + 1) * D)
                    i = pe.matmul(pG[r, b, 0:D], qT[:, slot, b, r], state[:, b, n, :], start=(b == 0), stop=False,
                                  skip_group_check=True)
            s_qs.by(i)

        def advance(t, slot, round):
            s_ui.wait(pe, t=t)
            for b in range(B):
                for n in range(NP):
                    r = slice(n * D, (n + 1) * D)
                    i = pe.matmul(pH[:, n, b * D:(b + 1) * D], kx[r, slot, b, :], ui[r, slot, b, :], start=True, stop=True)
            s_ku.by(i)
            s_ku.wait(dve, t=t)
            s_qs.wait(dve, t=t)
            s_st.by(dve.tensor_tensor(state[:, :, :, :], state[:, :, :, :], pH[:, :, 0:B * D].rearrange("p n (b d) -> p b n d", b=B), ALU.add))

        def attend(t, slot, round):
            s_ea.wait(pe, t=t)
            for b in range(B):
                i = pe.matmul(pG[:, b, 0:D], atT[:, slot, b, :], ui[:, slot, b, :], start=False, stop=True, skip_group_check=True)
            s_o.by(i)

        def keep_delta(t, slot, round):
            s_o.wait(dve, t=t)
            s_rq.wait(dve, t=t)
            s_do.free(dve, slot, round)
            s_eo.by(dve.tensor_tensor(do[:, slot, :, :], pG[:, :, 0:D], rq[:, slot, :].unsqueeze(2).broadcast_to([P, B, D]), ALU.mult))
            s_eo.wait(sp, t=t)
            for h in range(H):
                dst = delta_d[:, h * D:(h + 1) * D].rearrange("(b c i) f -> c i b f", b=B, i=CH)
                s_do.by(sp.dma_start(dst[bass.ds(t, 1)].rearrange("o i b f -> (o i) b f"), do[h * CH:(h + 1) * CH, slot, :, :]), slot)

        flow(nc, turns, [(load4, 0), (correct, 4), (attention, 3), (q_root, 3), (advance, 4), (w_and_u, 3), (attend, 4),
                         (q_inverse, 4), (turn_kq, 2), (keep_delta, 4), (expand, 1)], 2)
        s_do.wait_all(sp)
        barrier()
        s_do.close()
        s_ld.close()
        q.close()
        p.close()
    hold.close()

    gate = ExitStack()
    weight = sb(gate, "weight", [P, TILES, H, NBR])
    BR = (("fir", 1), ("fir", 0), ("delta", 0), ("qkv", 2))

    def branch(n, t):
        kind, i = BR[n]
        src = {"fir": fir_d, "delta": None, "qkv": qkv_d}[kind]
        src = delta_d if src is None else src[i]
        return src[bass.ds(t * P, P), :]

    NG = H * NBR
    temp = sb(gate, "temp", [P, H])
    floor = sb(gate, "floor", [P, NG])
    onorm = sb(gate, "onorm", [P, 1])
    GW = P
    with ExitStack() as st:
        w1h = sb(st, "w1h", [P, KT, GW])
        w1b = sb(st, "w1b", [P, 2, GW])
        w1m = sb(st, "w1m", [P, 2, GW])
        w1s = sb(st, "w1s", [D, NBR, 2, GW])
        half = sb(st, "half", [P, P])
        pick = sb(st, "pick", [D, 4 * NG - 1])
        wst = sb(st, "wst", [2 * NG, H, GW])
        w2 = sb(st, "w2", [GW, NBR])
        b1 = sb(st, "b1", [GW, 1])
        b2 = sb(st, "b2", [P, NBR])
        br = sb(st, "br", [P, 4, 2, H, 2, D])
        ht = sb(st, "ht", [P, 4, KT, P])
        sq = sb(st, "sq", [P, 4, NG, D])
        stt = sb(st, "stt", [P, 4, 2, NG])
        bT5 = sb(st, "bT5", [P, 4, 2, H, P])
        sT = sb(st, "sT", [2 * NG, 4, P])
        hid = sb(st, "hid", [P, 4, P])
        hm = sb(st, "hm", [P, 4, H, P])
        pX = ps(st, "pX", [P, 2, H, P])
        pS = ps(st, "pS", [P, 512])
        pI = ps(st, "pI", [P, 512])
        pM = ps(st, "pM", [P, 2, H, P])
        pL = ps(st, "pL", [P, 2, 512])

        p = sems.loop(1)
        s_w, s_c = p.dma(10 + 3 * NBR), p.step(3)
        s_w.by(sp.dma_start(w1h[:, :, :], a["gW1"][0:C, :].rearrange("(k p) n -> p k n", p=P)))
        s_w.by(sp.dma_start(w1b[:, :, :], a["gW1"][C + 3 * NBR * D:, :].rearrange("(k p) n -> p k n", p=P)))
        for n in range(NBR):
            r = C + 3 * D * n
            s_w.by(sp.dma_start(w1m[(n % 2) * D:(n % 2 + 1) * D, n // 2, :], a["gW1"][r:r + D, :]))
            for s in range(2):
                s_w.by(sp.dma_start(w1s[:, n, s, :], a["gW1"][r + (s + 1) * D:r + (s + 2) * D, :]))
        s_w.by(sp.dma_start(w2[:, :], a["gW2"]))
        s_w.by(sp.dma_start(b1[:, :], a["gb1"]))
        s_w.by(sp.dma_start(b2[:, :], a["gb2"][0].partition_broadcast(P)))
        s_w.by(sp.dma_start(temp[:, :], a["temp"][0].partition_broadcast(P)))
        s_w.by(sp.dma_start(floor[:, :], a["floor"][0].partition_broadcast(P)))
        for n in range(2):
            s_w.by(sp.dma_start(onorm[n * D:(n + 1) * D, :], a["onorm"].rearrange("o d -> d o")))
        s_w.by(sp.dma_start(sT[:, 0, :], a["gW1"][0:2 * NG, :]))
        s_c.by(dve.memset(half[:, :], 0.0))
        s_c.by(dve.memset(pick[:, :], 0.0))
        s_c.wait(dve, 2)
        dve.memset(half[0:D, 0:D], 1.0 / D)
        dve.memset(half[D:P, D:P], 1.0 / D)
        s_c.by(dve.memset(pick[:, 2 * NG - 1:2 * NG], 1.0))
        s_c.wait(pe)
        s_w.wait(pe)
        s_m, s_ma = p.step(1 + H), p.step(1 + H)
        for k in range(2):
            i = pe.matmul(pX[:, 0, k, :], half[:, :], w1m[:, k, :], start=True, stop=True)
        s_m.by(i)
        s_m.wait(dve, 1)
        s_w.wait(dve)
        s_ma.by(dve.tensor_tensor(w1b[:, :, :], w1b[:, :, :], pX[:, 0, 0:2, :], ALU.add))
        for h in range(H):
            if h:
                s_ma.wait(pe, h + 1)
            for n in range(NBR):
                for s in range(2):
                    c = s * NG + (n // 2) * 2 * H + h * 2 + n % 2
                    i = pe.matmul(pS[0:2 * NG, 0:GW], pick[:, 2 * NG - 1 - c:4 * NG - 1 - c], w1s[:, n, s, :],
                                  start=(n + s == 0), stop=(n == NBR - 1 and s == 1))
            s_m.by(i)
            s_m.wait(dve, h + 2)
            s_ma.by(dve.tensor_copy(wst[:, h, :], pS[0:2 * NG, 0:GW]))
        s_ma.wait(pe)
        s_w.wait(act)

        q = sems.loop(TILES)
        s_ld = Ring(sems, TILES, NBR + 1)
        s_sq, s_mx, s_v, s_rt, s_tx, s_ex, s_ts, s_es = q.step(), q.step(), q.step(2), q.step(), q.step(2), q.step(2), q.step(), q.step()
        s_hi, s_eh, s_m1, s_ad, s_ge, s_l, s_lo = [q.step() for _ in range(7)]

        def load5(t, slot, round):
            s_tx.back(sp, t, 4)
            s_sq.back(sp, t, 4)
            s_mx.back(sp, t, 4)
            s_hi.back(sp, t, 4)
            for n in range(NBR):
                s_ld.by(sp.dma_start(br[:, slot, n // 2, :, n % 2, :], branch(n, t).rearrange("p (h d) -> p h d", h=H)), slot)
            s_ld.by(sp.dma_start(ht[:, slot, :, :], hT_d.rearrange("k p t -> p k t")[:, :, bass.ds(t * P, P)]), slot)

        def square_and_turn(t, slot, round):
            groups = br[:, slot, :, :, :, :].rearrange("p k h n d -> p (k h n) d")
            s_ld.wait(pool, slot, round)
            s_v.back(pool, t, 4)
            s_sq.by(pool.tensor_tensor(sq[:, slot, :, :], groups, groups, ALU.mult))
            s_ld.wait(dve, slot, round)
            s_ts.back(dve, t, 4)
            s_mx.by(dve.tensor_reduce(stt[:, slot, 1, :], groups, AX, ALU.max))
            s_ld.wait(pe, slot, round)
            for k in range(2):
                s_ex.back(pe, t, 1)
                for h in range(H):
                    i = pe.transpose(pX[:, k, h, :], br[:, slot, k, h, :, :].rearrange("p n d -> p (n d)"), ident[:, :])
                s_tx.by(i)

        def keep_turned(t, slot, round):
            s_tx.wait(act, 1, t=t)
            s_m1.back(act, t, 4)
            s_ex.by(act.activation(bT5[:, slot, 0, :, :], pX[:, 0, :, :], ACT.Copy))
            s_tx.wait(dve, 2, t=t)
            s_m1.back(dve, t, 4)
            s_ex.by(dve.tensor_copy(bT5[:, slot, 1, :, :], pX[:, 1, :, :]))
            s_sq.wait(dve, t=t)
            s_v.by(dve.tensor_reduce(stt[:, slot, 0, :], sq[:, slot, :, :], AX, ALU.add))
            s_v.wait(dve, 1, t=t)
            s_v.by(dve.tensor_scalar(stt[:, slot, 0, :], stt[:, slot, 0, :], 1.0 / D, 1e-8, ALU.mult, ALU.max))
            s_eh.back(pe, t, 1)
            for k in range(KT):
                i = pe.matmul(pI[:, 0:P], w1h[:, k, :], ht[:, slot, k, :], start=(k == 0), stop=(k == KT - 1))
            s_hi.by(i)

        def root(t, slot, round):
            s_hi.wait(act, t=t)
            s_ad.back(act, t, 4)
            s_eh.by(act.activation(hid[:, slot, :], pI[:, 0:P], ACT.Copy))
            s_v.wait(act, t=t)
            s_rt.by(act.activation(stt[:, slot, 0, :], stt[:, slot, 0, :], ACT.Sqrt))

        def turn_stats(t, slot, round):
            s_rt.wait(pe, t=t)
            s_mx.wait(pe, t=t)
            s_es.back(pe, t, 1)
            i = pe.transpose(pS[0:2 * NG, 0:P], stt[:, slot, :, :].rearrange("p s g -> p (s g)"), ident[:, :])
            s_ts.by(i)
            s_ts.wait(dve, t=t)
            s_m1.back(dve, t, 4)
            s_es.by(dve.tensor_copy(sT[:, slot, :], pS[0:2 * NG, 0:P]))

        def first_layer(t, slot, round):
            s_ex.wait(pe, t=t)
            s_ad.back(pe, t, 2)
            for k in range(2):
                pe.matmul(pM[:, slot % 2, :, :], w1b[:, k, :], bT5[:, slot, k, :, :], start=(k == 0), stop=False, skip_group_check=True)
            s_es.wait(pe, t=t)
            for h in range(H):
                i = pe.matmul(pM[:, slot % 2, h, :], wst[:, h, :], sT[:, slot, :], start=False, stop=True, skip_group_check=True)
            s_m1.by(i)

        def gelu(t, slot, round):
            s_m1.wait(dve, t=t)
            s_eh.wait(dve, t=t)
            s_l.back(dve, t, 4)
            s_ad.by(dve.tensor_tensor(hm[:, slot, :, :], pM[:, slot % 2, :, :], hid[:, slot, :].unsqueeze(1).broadcast_to([P, H, P]), ALU.add))
            s_ad.wait(act, t=t)
            s_ge.by(act.activation(hm[:, slot, :, :], hm[:, slot, :, :], ACT.Gelu, bias=b1[:, 0:1]))

        def second_layer(t, slot, round):
            s_ge.wait(pe, t=t)
            s_lo.back(pe, t, 2)
            for h in range(H):
                i = pe.matmul(pL[:, slot % 2, h * NBR:(h + 1) * NBR], hm[:, slot, h, :], w2[:, :], start=True, stop=True)
            s_l.by(i)

        def keep_logits(t, slot, round):
            s_l.wait(dve, t=t)
            s_lo.by(dve.tensor_tensor(weight[:, bass.ds(t, 1), :, :].rearrange("p o h n -> p (o h) n"),
                                      pL[:, slot % 2, 0:NG].rearrange("p (h n) -> p h n", h=H),
                                      b2[:, :].unsqueeze(1).broadcast_to([P, H, NBR]), ALU.add))

        flow(nc, TILES, oldest_first(load5, square_and_turn, keep_turned, root, turn_stats, first_layer, gelu, second_layer, keep_logits), 3)
        barrier()
        s_ld.close()
        q.close()
        p.close()

    with ExitStack() as st:
        mx = sb(st, "mx", [P, TILES * H])
        p = sems.loop(1)
        s_v, s_e = p.step(14), p.step()
        n_v = 0

        def chained(ins):
            nonlocal n_v
            n_v += 1
            s_v.by(ins)
            s_v.wait(dve, n_v)

        w3 = weight[:, :, :, :].rearrange("p t h n -> p (t h) n")
        w4 = weight[:, :, :, :].rearrange("p t h n -> p t (h n)")

        def wide(x):
            return x.unsqueeze(2).broadcast_to([P, TILES * H, NBR])

        chained(dve.tensor_scalar(temp[:, :], temp[:, :], 0.2, 10.0, ALU.max, ALU.min))
        chained(dve.reciprocal(temp[:, :], temp[:, :]))
        chained(dve.tensor_scalar(floor[:, :], floor[:, :], 1e-7, 0.1, ALU.max, ALU.min))
        chained(dve.tensor_tensor(weight[:, :, :, :], weight[:, :, :, :],
                                  temp[:, :].unsqueeze(1).unsqueeze(3).broadcast_to([P, TILES, H, NBR]), ALU.mult))
        chained(dve.tensor_reduce(mx[:, :], w3, AX, ALU.max))
        chained(dve.tensor_tensor(w3, w3, wide(mx[:, :]), ALU.subtract))
        s_v.wait(act, n_v)
        s_e.by(act.activation(w3, w3, ACT.Exp))
        s_e.wait(dve)
        for low in (True, False):
            chained(dve.tensor_reduce(mx[:, :], w3, AX, ALU.add))
            chained(dve.reciprocal(mx[:, :], mx[:, :]))
            chained(dve.tensor_tensor(w3, w3, wide(mx[:, :]), ALU.mult))
            if low:
                chained(dve.tensor_tensor(w4, w4, floor[:, :].unsqueeze(1).broadcast_to([P, TILES, NG]), ALU.max))
        if "w_d" in dbg:
            w_d = dram("w_d", [TOK, NG])
            s_x = p.dma()
            s_v.wait(sp, n_v)
            s_x.by(sp.dma_start(w_d.rearrange("(t p) g -> p t g", p=P), w4))
            s_x.wait(sp)
        s_v.per_turn = n_v
        barrier()
        p.close()

    with ExitStack() as st:
        wo = sb(st, "wo", [P, KT, C])
        gw = sb(st, "gw", [P, KT, NE])
        br = sb(st, "br6", [P, 4, NBR, C])
        xt = sb(st, "xt", [P, 4, C])
        pr = sb(st, "pr", [P, 4, NBR, C])
        mix = sb(st, "mix", [P, 4, C])
        msq = sb(st, "msq", [P, 4, C])
        rr = sb(st, "rr", [P, 4, H])
        on = sb(st, "on", [P, 4, C])
        oT = sb(st, "oT", [P, 2, KT, P])
        x2 = sb(st, "x2", [P, 4, C])
        bn = sb(st, "bn", [P, 4, 6])
        mv = sb(st, "mv", [P, 4, 2])
        h2 = sb(st, "h2", [P, 4, C])
        h2T = sb(st, "h2T", [P, 2, KT, P])
        pO = ps(st, "pO", [P, 2, 512])
        pW = ps(st, "pW", [P, 2, 512])
        pH2 = ps(st, "pH2", [P, 2, 512])
        pg = ps(st, "pg", [P, 2, 512])
        p = sems.loop(1)
        s_w, s_wo = p.dma(2), p.step()
        s_w.by(sp.dma_start(wo[:, :, :], a["Wo"].rearrange("(k p) n -> p k n", p=P)))
        s_w.by(sp.dma_start(gw[:, :, :], a["gate_w"].rearrange("(k p) n -> p k n", p=P)))
        s_w.wait(dve)
        s_w.wait(pe)
        s_wo.by(dve.tensor_scalar(wo[:, :, :], wo[:, :, :], onorm[:, 0:1], None, ALU.mult))
        s_wo.wait(pe)

        q = sems.loop(TILES)
        s_ld, s_xt, s_x2o, s_h2o = [Ring(sems, TILES, n) for n in (NBR, 1, 1, 1)]
        s_pr, s_mx, s_ms, s_r, s_rt, s_rc, s_on = q.step(), q.step(), q.step(), q.step(2), q.step(), q.step(), q.step()
        s_to, s_eo, s_wm, s_ga, s_x2, s_b, s_sr, s_ri, s_n, s_h, s_th, s_eh, s_gm, s_g = (
            q.step(), q.step(), q.step(), q.step(), q.step(), q.step(3), q.step(), q.step(), q.step(), q.step(2),
            q.step(), q.step(), q.step(), q.step())

        def row(n, t):
            return rows[:, n, bass.ds(t // (TILES // B), 1), :].rearrange("p o c -> p (o c)")

        def load6(t, slot, round):
            s_pr.back(sp, t, 4)
            for n in range(NBR):
                s_ld.by(sp.dma_start(br[:, slot, n, :], branch(n, t)), slot)

        def weigh(t, slot, round):
            s_ld.wait(pool, slot, round)
            s_mx.back(pool, t, 4)
            w = weight[:, bass.ds(t, 1), :, :].rearrange("p o h n -> p n (o h)")
            s_pr.by(pool.tensor_tensor(pr[:, slot, :, :].rearrange("p n (h d) -> p n h d", h=H),
                                       br[:, slot, :, :].rearrange("p n (h d) -> p n h d", h=H),
                                       w.unsqueeze(3).broadcast_to([P, NBR, H, D]), ALU.mult))

        def mix_branches(t, slot, round):
            s_pr.wait(dve, t=t)
            s_on.back(dve, t, 4)
            s_mx.by(dve.tensor_reduce(mix[:, slot, :], pr[:, slot, :, :].rearrange("p n c -> p c n"), AX, ALU.add))
            s_mx.wait(act, t=t)
            s_r.back(act, t, 4)
            s_ms.by(act.activation(msq[:, slot, :], mix[:, slot, :], ACT.Square))

        def mean_square(t, slot, round):
            s_ms.wait(dve, t=t)
            s_r.by(dve.tensor_reduce(rr[:, slot, :], msq[:, slot, :].rearrange("p (h d) -> p h d", h=H), AX, ALU.add))
            s_r.wait(dve, 1, t=t)
            s_r.by(dve.tensor_scalar(rr[:, slot, :], rr[:, slot, :], 1.0 / D, EPS_RMS, ALU.mult, ALU.add))
            s_r.wait(act, t=t)
            s_rt.by(act.activation(rr[:, slot, :], rr[:, slot, :], ACT.Sqrt))

        def normalise(t, slot, round):
            s_rt.wait(dve, t=t)
            s_rc.by(dve.reciprocal(rr[:, slot, :], rr[:, slot, :]))
            s_rc.wait(dve, t=t)
            s_to.back(dve, t, 4)
            s_on.by(dve.tensor_tensor(on[:, slot, :].rearrange("p (h d) -> p h d", h=H),
                                      mix[:, slot, :].rearrange("p (h d) -> p h d", h=H),
                                      rr[:, slot, :].unsqueeze(2).broadcast_to([P, H, D]), ALU.mult))
            s_on.wait(pe, t=t)
            s_eo.back(pe, t, 2)
            for k in range(KT):
                i = pe.transpose(pO[:, slot % 2, k * P:(k + 1) * P], on[:, slot, k * P:(k + 1) * P], ident[:, :])
            s_to.by(i)
            s_x2.back(sp, t, 4)
            s_xt.by(sp.dma_start(xt[:, slot, :], a["x"][bass.ds(t * P, P), :]), slot)

        def project_out(t, slot, round):
            s_to.wait(act, t=t)
            s_wm.back(act, t, 2)
            s_eo.by(act.activation(oT[:, slot % 2, :, :].rearrange("p k t -> p (k t)"), pO[:, slot % 2, 0:C], ACT.Copy))
            s_eo.wait(pe, t=t)
            s_ga.back(pe, t, 2)
            for k in range(KT):
                i = pe.matmul(pW[:, slot % 2, 0:C], oT[:, slot % 2, k, :], wo[:, k, :], start=(k == 0), stop=(k == KT - 1))
            s_wm.by(i)

        def residual(t, slot, round):
            s_wm.wait(dve, t=t)
            s_x2o.free(dve, slot, round)
            s_n.back(dve, t, 4)
            s_ga.by(dve.tensor_tensor(x2[:, slot, :], pW[:, slot % 2, 0:C], row(0, t), ALU.mult))
            s_ga.wait(pool, t=t)
            s_xt.wait(pool, slot, round)
            s_x2.by(pool.tensor_tensor(x2[:, slot, :], x2[:, slot, :], xt[:, slot, :], ALU.add))
            s_x2.wait(sp, t=t)
            s_x2o.by(sp.dma_start(x2_d[bass.ds(t * P, P), :], x2[:, slot, :]), slot)

        def second_stats(t, slot, round):
            s_x2.wait(dve, t=t)
            s_b.by(dve.bn_stats(bn[:, slot, :], x2[:, slot, :]))
            s_b.wait(dve, 1, t=t, alone=True)
            s_b.by(dve.bn_aggr(mv[:, slot, :], bn[:, slot, :]))
            s_b.wait(dve, 2, t=t)
            s_b.by(dve.tensor_scalar(mv[:, slot, 1:2], mv[:, slot, 1:2], EPS_LN, None, ALU.add))
            s_b.wait(act, 3, t=t)
            s_sr.by(act.activation(mv[:, slot, 1:2], mv[:, slot, 1:2], ACT.Sqrt))

        def second_norm(t, slot, round):
            s_sr.wait(dve, t=t)
            s_ri.by(dve.reciprocal(mv[:, slot, 1:2], mv[:, slot, 1:2]))
            s_ri.wait(dve, t=t)
            s_th.back(dve, t, 4)
            s_h2o.free(dve, slot, round)
            s_n.by(dve.tensor_scalar(h2[:, slot, :], x2[:, slot, :], mv[:, slot, 0:1], mv[:, slot, 1:2], ALU.subtract, ALU.mult))
            s_n.wait(pool, t=t)
            s_h.by(pool.tensor_tensor(h2[:, slot, :], h2[:, slot, :], row(2, t), ALU.mult))
            s_h.wait(pool, 1, t=t)
            s_h.by(pool.tensor_tensor(h2[:, slot, :], h2[:, slot, :], row(1, t), ALU.add))
            s_h.wait(sp, t=t)
            s_h2o.by(sp.dma_start(h2_d[bass.ds(t * P, P), :], h2[:, slot, :]), slot)

        def router(t, slot, round):
            s_h.wait(pe, t=t)
            s_eh.back(pe, t, 2)
            for k in range(KT):
                i = pe.transpose(pH2[:, slot % 2, k * P:(k + 1) * P], h2[:, slot, k * P:(k + 1) * P], ident[:, :])
            s_th.by(i)
            s_th.wait(act, t=t)
            s_gm.back(act, t, 2)
            s_eh.by(act.activation(h2T[:, slot % 2, :, :].rearrange("p k t -> p (k t)"), pH2[:, slot % 2, 0:C], ACT.Copy))
            s_eh.wait(pe, t=t)
            s_g.back(pe, t, 2)
            for k in range(KT):
                i = pe.matmul(pg[:, slot % 2, 0:NE], h2T[:, slot % 2, k, :], gw[:, k, :], start=(k == 0), stop=(k == KT - 1))
            s_gm.by(i)

        def keep_router(t, slot, round):
            s_gm.wait(dve, t=t)
            s_g.by(dve.tensor_scalar(gates[:, bass.ds(t % TPB, 1), bass.ds(t // TPB, 1), :].rearrange("p o b e -> p (o b e)"),
                                     pg[:, slot % 2, 0:NE], 1e-6, None, ALU.max))

        flow(nc, TILES, oldest_first(load6, weigh, mix_branches, mean_square, normalise, project_out, residual,
                                     second_stats, second_norm, router, keep_router), 3)
        for s in (s_x2o, s_h2o):
            s.wait_all(sp)
        barrier()
        for s in (s_ld, s_xt, s_x2o, s_h2o):
            s.close()
        q.close()
        p.close()
    gate.close()

    R = B * NE
    route = ExitStack()
    top = sb(route, "top", [R, CAP])
    topi = sb(route, "topi", [R, CAP])
    with ExitStack() as st:
        cs7 = sb(st, "cs7", [P, R])
        rs7 = sb(st, "rs7", [P, TILES])
        G = sb(st, "G", [R, L])
        m8 = sb(st, "m8", [R, 8])
        i8 = sb(st, "i8", [R, 8], U32)
        zero = sb(st, "zero", [P, TOK * NE // P])
        pc = ps(st, "pc", [P, R])
        pgt = ps(st, "pgt", [R, 4, 4, P])
        p = sems.loop(1)
        s_z, s_zo = p.step(), p.pool_dma()
        s_z.by(pool.memset(zero[:, :], 0.0))
        s_z.wait(pool)
        s_zo.by(pool.dma_start(key_d.rearrange("(p x) o -> p (x o)", p=P), zero[:, :]))
        q = sems.loop(8)
        s_s, s_cm = q.step(6), q.step()
        g3 = gates[:, :, :, :].rearrange("p t b e -> p t (b e)")
        gr7 = gates[:, :, :, :].rearrange("p t b e -> p (t b) e")
        with nc.Fori(0, 8, engines=[ENG.DVE, ENG.PE]) as i:
            q.it = i
            s_s.by(dve.tensor_reduce(cs7[:, :], g3.rearrange("p t r -> p r t"), AX, ALU.add))
            s_s.wait(pe, 1)
            s_cm.by(pe.matmul(pc[:, :], ones[:, :], cs7[:, :], start=True, stop=True))
            s_cm.wait(dve)
            s_s.by(dve.reciprocal(cs7[:, :], pc[:, :]))
            s_s.wait(dve, 2)
            s_s.by(dve.tensor_tensor(g3, g3, cs7[:, :].unsqueeze(1).broadcast_to([P, TPB, R]), ALU.mult))
            s_s.wait(dve, 3)
            s_s.by(dve.tensor_reduce(rs7[:, :], gr7, AX, ALU.add))
            s_s.wait(dve, 4)
            s_s.by(dve.reciprocal(rs7[:, :], rs7[:, :]))
            s_s.wait(dve, 5)
            s_s.by(dve.tensor_tensor(gr7, gr7, rs7[:, :].unsqueeze(2).broadcast_to([P, TILES, NE]), ALU.mult))
            s_s.wait(dve, 6)
        s_s.wait_all(pe)
        s_t, s_e = p.step(4), p.step(4)
        for j in range(TPB):
            i = pe.transpose(pgt[:, j // 4, j % 4, :], g3[:, j, :], ident[:, :])
            if j % 4 == 3:
                s_t.by(i)
        for w in range(4):
            s_t.wait(dve, w + 1)
            s_e.by(dve.tensor_copy(G[:, w * 512:(w + 1) * 512], pgt[:, w, :, :].rearrange("r t p -> r (t p)")))
        s_e.wait(dve)
        q2 = sems.loop(CAP // 8)
        s_k = q2.step(5)
        with nc.Fori(0, CAP // 8, engines=[ENG.DVE]) as i:
            q2.it = i
            s_k.by(dve.max(m8[:, :], G[:, :]))
            s_k.wait(dve, 1, alone=True)
            s_k.by(dve.max_index(i8[:, :], m8[:, :], G[:, :]))
            s_k.wait(dve, 2, alone=True)
            s_k.by(dve.match_replace(G[:, :], m8[:, :], G[:, :], -1.0))
            s_k.by(dve.tensor_copy(top[:, bass.ds(i * 8, 8)], m8[:, :]))
            s_k.by(dve.tensor_copy(topi[:, bass.ds(i * 8, 8)], i8[:, :]))
            s_k.wait(dve, 5)
        s_zo.wait(pool)
        barrier()
        q2.close()
        q.close()
        p.close()

    with ExitStack() as st:
        NH = CAP // P
        exw = sb(st, "exw", [P, KT, NE, C])
        hot = sb(st, "hot", [P, NH, R])
        tokf = sb(st, "tokf", [P, NH, R])
        keyf = sb(st, "keyf", [P, NH, R])
        toku = sb(st, "toku", [P, NH, R], U32)
        keyu = sb(st, "keyu", [P, NH, R], U32)
        keyv = sb(st, "keyv", [P, NH, NE])
        keyi = sb(st, "keyi", [P, NH, NE], mybir.dt.int32)
        cur = sb(st, "cur8", [P, NH, NE], U32)
        pt = ps(st, "pt", [P, 2, NH, R])
        p = sems.loop(1)
        s_w, s_i, s_kv = p.dma(KT), p.step(), p.step()
        for k in range(KT):
            s_w.by(sp.dma_start(exw[:, k, :, :], a["experts"].rearrange("(e k p) n -> k p e n", k=KT, p=P)[k]))
        s_i.by(pool.iota(keyi[:, :, :], pattern=[[P * NE, NH], [1, NE]], base=1, channel_multiplier=NE))
        s_i.wait(dve)
        s_kv.by(dve.tensor_copy(keyv[:, :, :], keyi[:, :, :]))
        s_t, s_c = p.step(), p.step(2)
        for w in range(NH):
            pe.transpose(pt[:, 0, w, :], topi[:, w * P:(w + 1) * P], ident[0:R, 0:R])
            i = pe.transpose(pt[:, 1, w, :], top[:, w * P:(w + 1) * P], ident[0:R, 0:R])
        s_t.by(i)
        s_t.wait(dve)
        s_v = p.step(B + NE + 3)
        for b in range(B):
            r = slice(b * NE, (b + 1) * NE)
            s_v.by(dve.tensor_scalar(tokf[:, :, r], pt[:, 0, :, r], float(b * L), None, ALU.add))
        s_v.by(dve.tensor_scalar(hot[:, :, :], pt[:, 1, :, :], 0.5, None, ALU.is_gt))
        s_v.wait(dve, B + 1)
        for e in range(NE):
            by_e = lambda x: x[:, :, :].rearrange("p w (b e) -> p w b e", b=B)[:, :, :, e]
            s_v.by(dve.tensor_scalar(by_e(keyf), by_e(tokf), float(NE), float(e), ALU.mult, ALU.add))
        s_v.by(dve.tensor_copy(toku[:, :, :], tokf[:, :, :]))
        s_v.wait(dve, B + NE + 2)
        s_v.by(dve.tensor_copy(keyu[:, :, :], keyf[:, :, :]))
        s_v.wait(dve)
        s_kv.wait(pool)

        q = sems.loop(B)
        s_cu, s_sc = q.step(), q.pool_dma(NH * NE)
        with nc.Fori(0, B, engines=[ENG.DVE, ENG.Pool]) as b:
            q.it = b
            s_cu.by(dve.tensor_copy(cur[:, :, :], keyu[:, :, bass.ds(b * NE, NE)]))
            s_cu.wait(pool)
            for w in range(NH):
                for e in range(NE):
                    s_sc.by(pool.indirect_dma_start(key_d, bass.IndirectOffsetOnAxis(ap=cur[:, w, e:e + 1], axis=0),
                                                    keyv[:, w, e:e + 1], None))
            s_sc.wait(dve)
        s_sc.wait_all(sp)
        keys = sb(st, "keys", [P, TILES, NE])
        won = sb(st, "won", [P, TILES])
        mask = sb(st, "mask", [P, TILES])
        rowu = sb(st, "rowu", [P, TILES], U32)
        s_kl = p.dma()
        s_kl.by(sp.dma_start(keys[:, :, :], key_d.rearrange("(t p e) o -> p t (e o)", p=P, e=NE)))
        s_kl.wait(dve)
        s_n = p.step(2 + B + 1)
        s_n.by(dve.tensor_reduce(won[:, :], keys[:, :, :], AX, ALU.max))
        s_n.wait(dve, 1)
        s_n.by(dve.tensor_scalar(mask[:, :], won[:, :], 1.0, None, ALU.min))
        s_n.wait(dve, 2)
        for b in range(B):
            r = slice(b * TILES // B, (b + 1) * TILES // B)
            s_n.by(dve.tensor_scalar(won[:, r], won[:, r], 1.0, float(b * L + 1), ALU.max, ALU.add))
        s_n.wait(dve, 2 + B)
        s_n.by(dve.tensor_scalar(rowu[:, :], won[:, :], -2.0, None, ALU.add))
        s_n.wait(dve)

        idx = sb(st, "idx", [P, 4, NH], U32)
        hg = sb(st, "hg", [P, 4, NH, C])
        hgT = sb(st, "hgT", [P, 2, NH, KT, P])
        eo = sb(st, "eo", [P, 4, NH, C])
        pT8 = ps(st, "pT8", [P, 2, NH, KT, P])
        pE8 = ps(st, "pE8", [P, 2, 512])
        q3 = sems.loop(R)
        s_id, s_tr, s_ev, s_mm, s_oe = q3.step(), q3.step(), q3.step(), q3.step(), q3.step(NH)
        s_ga, s_eo = Ring(sems, R, NH, pool=True), Ring(sems, R)
        s_w.wait(pe)

        def gather(t, slot, round):
            s_ga.free(dve, slot, round)
            s_id.by(dve.tensor_copy(idx[:, slot, :], toku[:, :, bass.ds(t, 1)].rearrange("p w o -> p (w o)")))
            s_id.wait(pool, t=t)
            s_tr.back(pool, t, 4)
            for w in range(NH):
                s_ga.by(pool.indirect_dma_start(hg[:, slot, w, :], None, h2_d,
                                                bass.IndirectOffsetOnAxis(ap=idx[:, slot, w:w + 1], axis=0)), slot)

        def turn_gathered(t, slot, round):
            s_ga.wait(pe, slot, round)
            s_ev.back(pe, t, 2)
            for w in range(NH):
                for k in range(KT):
                    i = pe.transpose(pT8[:, slot % 2, w, k, :], hg[:, slot, w, k * P:(k + 1) * P], ident[:, :])
            s_tr.by(i)
            s_tr.wait(act, t=t)
            s_mm.back(act, t, 2)
            s_ev.by(act.activation(hgT[:, slot % 2, :, :, :], pT8[:, slot % 2, :, :, :], ACT.Copy))

        def expert(t, slot, round):
            s_ev.wait(pe, t=t)
            s_oe.back(pe, t, 1)
            for w in range(NH):
                for k in range(KT):
                    i = pe.matmul(pE8[:, w, 0:C], hgT[:, slot % 2, w, k, :],
                                  exw[:, k, bass.ds(t % NE, 1), :].rearrange("p o n -> p (o n)"), start=(k == 0), stop=(k == KT - 1))
            s_mm.by(i)
            s_mm.wait(dve, t=t)
            s_eo.free(dve, slot, round)
            for w in range(NH):
                s_oe.by(dve.tensor_scalar(eo[:, slot, w, :], pE8[:, w, 0:C], hot[:, w, bass.ds(t, 1)], None, ALU.mult))
            s_oe.wait(sp, t=t)
            dst = bass.AP(routed_d.tensor, ((t // NE) * (CAP * NE) + (t % NE)) * C, [[NE * C, P], [P * NE * C, NH], [1, C]])
            s_eo.by(sp.dma_start(dst, eo[:, slot, :, :]), slot)

        flow(nc, R, oldest_first(gather, None, turn_gathered, expert), 2)
        s_eo.wait_all(pool)

        ix = sb(st, "ix", [P, 4], U32)
        og = sb(st, "og", [P, 4, C])
        xr = sb(st, "xr", [P, 4, C])
        y = sb(st, "y9", [P, 4, C])
        q4 = sems.loop(TILES)
        s_ix, s_o, s_fy = q4.step(), q4.step(), q4.step()
        s_og, s_xr, s_y = Ring(sems, TILES, pool=True), Ring(sems, TILES), Ring(sems, TILES)

        def fetch(t, slot, round):
            s_og.free(dve, slot, round)
            s_ix.by(dve.tensor_copy(ix[:, slot:slot + 1], rowu[:, bass.ds(t, 1)]))
            s_ix.wait(pool, t=t)
            s_o.back(pool, t, 4)
            s_og.by(pool.indirect_dma_start(og[:, slot, :], None, routed_d,
                                            bass.IndirectOffsetOnAxis(ap=ix[:, slot:slot + 1], axis=0)), slot)
            s_fy.back(sp, t, 4)
            s_xr.by(sp.dma_start(xr[:, slot, :], x2_d[bass.ds(t * P, P), :]), slot)

        def finish(t, slot, round):
            s_og.wait(dve, slot, round)
            s_y.free(dve, slot, round)
            s_o.by(dve.scalar_tensor_tensor(y[:, slot, :], og[:, slot, :], mask[:, bass.ds(t, 1)], row(3, t), ALU.mult, ALU.mult))
            s_xr.wait(dve, slot, round)
            s_o.wait(dve, t=t)
            s_fy.by(dve.tensor_tensor(y[:, slot, :], y[:, slot, :], xr[:, slot, :], ALU.add))
            s_fy.wait(act, t=t)
            s_y.by(act.dma_start(out[bass.ds(t * P, P), :], y[:, slot, :]), slot)

        flow(nc, TILES, oldest_first(fetch, None, None, finish), 2)
        s_y.wait_all(sp)
        barrier()
    route.close()
    whole.close()



INS = {"x": "L0_attn_x", "Wq": "L0_attn_Wq", "Wk": "L0_attn_Wk", "Wv": "L0_attn_Wv", "Wb": "L0_attn_Wb",
       "qc": "L0_attn_qc_w", "kc": "L0_attn_kc_w", "vc": "L0_attn_vc_w", "fir_s": "L0_attn_fir_s",
       "fir_l": "L0_attn_fir_l", "gW1": "L0_attn_gW1", "gb1": "L0_attn_gb1", "gW2": "L0_attn_gW2",
       "gb2": "L0_attn_gb2", "temp": "L0_attn_temp", "floor": "L0_attn_eps_floor",
       "onorm": "L0_attn_onorm_w", "Wo": "L0_attn_Wo", "gate_w": "L0_ffn_gate_w",
       "experts": "L0_ffn_experts", "cT": "L0_c", "wmod": "L0_wmod"}


def lay_out(inputs):
    import numpy as np
    shape = {"x": (TOK, C), "fir_s": (C, FIRS), "fir_l": (C, FIRL), "gb1": (P, 1), "gb2": (1, 4), "temp": (1, H),
             "floor": (1, 16), "onorm": (1, D), "gate_w": (C, NE), "experts": (NE * C, C)}
    got = {}
    for name, full in INS.items():
        v = np.asarray(inputs[full])
        if name in shape:
            v = v.reshape(shape[name])
        if name == "cT":
            v = v.T
        got[name] = np.ascontiguousarray(v)
    return got


def kernel(**inputs):
    import concourse.bacc as bacc
    from concourse.bass_utils import run_bass_kernel_spmd

    nc = bacc.Bacc("TRN2", target_bir_lowering=False, num_devices=1)
    arrays = lay_out(inputs)
    a = {n: nc.dram_tensor(f"in_{n}", list(v.shape), F32, kind="ExternalInput").ap() for n, v in arrays.items()}
    out = nc.dram_tensor("y", [TOK, C], F32, kind="ExternalOutput").ap()
    build(nc, a, out)
    r = run_bass_kernel_spmd(nc, [{f"in_{n}": v for n, v in arrays.items()}], core_ids=[0])
    return r.results[0]["y"].reshape(B, L, C)
```

```python
from contextlib import ExitStack

import concourse.bass as bass
from concourse import mybir

ALU = mybir.AluOpType
ACT = mybir.ActivationFunctionType
F32 = mybir.dt.float32
U32 = mybir.dt.uint32
AX = mybir.AxisListType.X
ENG = mybir.EngineType

P = 128
B, L, C, H = 4, 2048, 256, 4
D = C // H
TOK = B * L
TILES = TOK // P
CH = 32
TPB = TILES // B
UNITS = TOK // CH
CPB = L // CH
KT = C // P
WIN = 512
TAPS, FIRL, FIRS = 4, 31, 3
BLK = 64
NBLK = TOK // BLK
SPAN = BLK + FIRL - 1
RW = SPAN + BLK
NBR = 4
NE = 8
CAP = L // NE
EPS_LN, EPS_L2, EPS_RMS = 1e-5, 1e-6, 1e-5


class Sems:

    def __init__(self, nc, n):
        self.plain = (nc.sync, nc.gpsimd)
        self.free = [[nc.alloc_semaphore(f"s{i}"), 1] for i in range(n)]
        engines = (nc.sync, nc.scalar, nc.tensor, nc.vector, nc.gpsimd)
        for i, (sem, _) in enumerate(self.free):
            engines[i % 5].sem_inc(sem, 1)
        nc.all_engine_barrier()
        self.soft = [[nc.alloc_semaphore(f"pool_dma{i}"), 0] for i in range(13)]

    def loop(self, turns):
        return Loop(self, turns)


class Loop:

    def __init__(self, sems, turns):
        self.sems, self.turns, self.it, self.steps = sems, turns, 0, []

    def step(self, per_turn=1):
        s = Step(self, self.sems.free.pop(0), per_turn)
        self.steps.append(s)
        return s

    def dma(self, n=1):
        s = self.step(16 * n)
        s.unit = 16
        return s

    def pool_dma(self, n=1):
        s = Step(self, self.sems.soft.pop(0), 16 * n)
        s.unit = 16
        return s

    def close(self):
        for s in self.steps:
            s.slot[1] += s.per_turn * self.turns
            self.sems.free.append(s.slot)


class Ring:

    def __init__(self, sems, turns, n=1, slots=4, pool=False):
        self.loop = sems.loop(turns // slots)
        make = self.loop.pool_dma if pool else self.loop.dma
        self.of = [make(n) for _ in range(slots)]

    def by(self, instruction, slot):
        return self.of[slot].by(instruction)

    def wait(self, engine, slot, round):
        self.of[slot].wait(engine, t=round)

    def free(self, engine, slot, round):
        self.of[slot].back(engine, round, 1)

    def wait_all(self, engine):
        for s in self.of:
            s.wait_all(engine)

    def close(self):
        self.loop.close()


class Step:
    def __init__(self, loop, slot, per_turn):
        self.loop, self.slot, self.per_turn, self.unit = loop, slot, per_turn, 1
        self.sem, self.base = slot

    def by(self, instruction):
        return instruction.then_inc(self.sem, self.unit)

    def until(self, engine, t, k, alone=False):
        count = t * self.per_turn + (self.base + k)
        if not isinstance(t, int) and (alone or engine in self.loop.sems.plain):
            count = engine.snap(engine.to_reg(count))
            engine.wait_ge(self.sem, self.base + max(k, 0))
        engine.wait_ge(self.sem, count)

    def wait(self, engine, k=None, t=None, alone=False):
        self.until(engine, self.loop.it if t is None else t, self.per_turn if k is None else k, alone)

    def wait_last(self, engine):
        self.back(engine, self.loop.it, 1)

    def back(self, engine, t, n, alone=False):
        if not isinstance(t, int) or t >= n:
            self.until(engine, t, (1 - n) * self.per_turn, alone)

    def wait_all(self, engine):
        engine.wait_ge(self.sem, self.base + self.per_turn * self.loop.turns)


def flow(nc, turns, stages, peel, slots=4, engines=None):
    def turn(group, u, peeled):
        for stage, lag in stages:
            t, slot, round = group * slots + (u - lag), (u - lag) % slots, group + (u - lag) // slots
            if not peeled or 0 <= t < turns:
                stage(t, slot, round)

    for i in range(peel * slots):
        turn(i // slots, i % slots, True)
    with nc.Fori(peel, turns // slots, **({"engines": engines} if engines else {})) as g:
        for u in range(slots):
            turn(g, u, False)
    for i in range(turns, turns + max(lag for _, lag in stages)):
        turn(i // slots, i % slots, True)


def oldest_first(*stages):
    return [(stage, lag) for lag, stage in reversed(list(enumerate(stages))) if stage]


def build(nc, a, out, dbg=()):
    pe, dve, act, pool, sp = nc.tensor, nc.vector, nc.scalar, nc.gpsimd, nc.sync
    sems = Sems(nc, 90)
    whole = ExitStack()

    def dram(name, shape, dt=F32):
        kind = "ExternalOutput" if name in dbg else "Internal"
        return nc.dram_tensor(name, list(shape), dt, kind=kind).ap()

    hT_d = dram("hT_d", [KT, P, TOK])
    qkv_d = dram("qkv_d", [4, TOK, C])
    beta_d = dram("beta_d", [TILES, H, P])
    taps_d = dram("taps_d", [C, RW])
    fir_d = dram("fir_d", [TOK, C])
    gram_d = dram("gram_d", [TOK, H, CH])
    tinv_d = dram("tinv_d", [UNITS, P, CH])
    delta_d = dram("delta_d", [TOK, C])
    x2_d = dram("x2_d", [TOK, C])
    h2_d = dram("h2_d", [TOK, C])
    key_d = dram("key_d", [TOK * NE, 1])
    routed_d = dram("routed_d", [B * CAP * NE, C])

    def sb(stack, name, shape, dt=F32):
        return stack.enter_context(nc.sbuf_tensor(name, list(shape), dt))

    def ps(stack, name, shape):
        return stack.enter_context(nc.psum_tensor(name, list(shape), F32))

    def barrier():
        nc.all_engine_barrier()

    ident = sb(whole, "ident", [P, P])
    ones = sb(whole, "ones", [P, P])
    blockdiag = sb(whole, "blockdiag", [P, P])
    causal = sb(whole, "causal", [P, P])
    parity = sb(whole, "parity", [P, 2])
    rows = sb(whole, "rows", [P, 4, B, C])
    scT = sb(whole, "scT", [P, B, 2, KT])
    gates = sb(whole, "gates", [P, TPB, B, NE])

    with ExitStack() as st:
        p = sems.loop(1)
        cT = sb(st, "cT", [P, KT, B])
        cs = sb(st, "cs", [P, KT, B])
        crep = sb(st, "crep", [P, KT, B, P])
        wmod = sb(st, "wmod", [P, KT, 6 * C])
        sgn = sb(st, "sgn", [P, 2, B, C])
        mag = sb(st, "mag", [P, 2, B, C])
        tapr = sb(st, "tapr", [P, KT, RW])
        pcol = ps(st, "pcol", [P, 2, KT, B])
        prow = ps(st, "prow", [P, 2, 512])

        s_c, s_tap, s_tapz, s_tapo = p.dma(2), p.dma(KT), p.step(), p.dma()
        for src, n in ((a["cT"], 0), (a["wmod"], 1)):
            s_c.by(sp.dma_start((cT if n == 0 else wmod)[:, :, :], src.rearrange("(k p) n -> p k n", p=P)))
        s_tapz.by(dve.memset(tapr[:, :, :], 0.0))
        s_tapz.wait(act)
        for k in range(KT):
            s_tap.by(act.dma_start(tapr[:, k, BLK - 1:BLK - 1 + FIRL], a["fir_l"][k * P:(k + 1) * P, :]))
        s_tap.wait(act)
        s_tapo.by(act.dma_start(taps_d.rearrange("(k p) w -> p k w", p=P), tapr[:, :, :]))

        s_sel = p.step(4 + 3 * H)
        n_sel = 0

        def in_order(ins):
            nonlocal n_sel
            n_sel += 1
            s_sel.by(ins)
            s_sel.wait(pool, n_sel)

        in_order(pool.memset(ones[:, :], 1.0))
        in_order(pool.affine_select(out=ident[:, :], in_=ones[:, :], pattern=[[-1, P]], compare_op=ALU.is_equal,
                                    fill=0.0, base=0, channel_multiplier=1))
        in_order(pool.memset(parity[:, :], 0.0))
        in_order(pool.memset(blockdiag[:, :], 0.0))
        pool.wait_ge(s_sel.sem, s_sel.base + n_sel)
        causal_z = p.step()
        causal_z.by(pool.memset(causal[:, :], 0.0))
        causal_z.wait(pool)
        for h in range(H):
            r = slice(CH * h, CH * (h + 1))
            in_order(pool.memset(parity[r, h % 2:h % 2 + 1], 1.0))
            in_order(pool.memset(blockdiag[r, r], 1.0))
            in_order(pool.affine_select(out=causal[r, r], in_=ones[r, 0:CH], pattern=[[1, CH]],
                                        compare_op=ALU.is_ge, fill=0.0, base=0, channel_multiplier=-1))

        s_silu, s_rep, s_col, s_cole = p.step(), p.step(), p.step(), p.step(2)
        s_c.wait(act)
        s_silu.by(act.activation(cs[:, :, :], cT[:, :, :], ACT.Silu))
        s_silu.wait(dve)
        s_rep.by(dve.tensor_copy(crep[:, :, :, :], cs[:, :, :].unsqueeze(3).broadcast_to([P, KT, B, P])))
        s_c.wait(pe)
        s_silu.wait(pe)
        for w in range(2):
            for m in range(KT):
                for k in range(KT):
                    i = pe.matmul(pcol[:, w, m, :], wmod[:, k, w * C + m * P:w * C + (m + 1) * P], cs[:, k, :],
                                  start=(k == 0), stop=(k == KT - 1))
        s_col.by(i)
        s_col.wait(dve)
        for w in range(2):
            s_cole.by(dve.tensor_scalar(scT[:, :, w, :], pcol[:, w, :, :].rearrange("p m b -> p b m"),
                                        float(w), None, ALU.add))
        s_rep.wait(pe)
        s_row, s_rowe = p.step(2 * B), p.step(2 * B)
        for b in range(B):
            for g in range(2):
                n = b * 2 + g
                if n >= 2:
                    s_rowe.wait(pe, n - 1)
                for k in range(KT):
                    i = pe.matmul(prow[:, n % 2, :], crep[:, k, b, :], wmod[:, k, 2 * C + g * 512:2 * C + (g + 1) * 512],
                                  start=(k == 0), stop=(k == KT - 1))
                s_row.by(i)
                s_row.wait(dve, n + 1)
                s_rowe.by(dve.tensor_copy(rows[:, 2 * g:2 * g + 2, b, :], prow[:, n % 2, :].rearrange("p (r c) -> p r c", r=2)))
        s_sg, s_ab, s_rfin = p.step(4), p.step(2), p.step(3)
        s_rowe.wait(dve)
        for n, r in enumerate((0, 3)):
            s_sg.by(dve.tensor_scalar(sgn[:, n, :, :], rows[:, r, :, :], 0.0, 2.0, ALU.is_ge, ALU.mult))
            g = rows[:, r, :, :].rearrange("p b c -> p (b c)")
            m = mag[:, n, :, :].rearrange("p b c -> p (b c)")
            s_sg.by(dve.scalar_tensor_tensor(m, g, -1.0, g, ALU.mult, ALU.max))
        s_sg.wait(dve)
        for n in range(2):
            s_ab.by(dve.tensor_scalar(mag[:, n, :, :], mag[:, n, :, :], 0.25, None, ALU.max))
        s_ab.wait(dve)
        for n, r in enumerate((0, 3)):
            s_rfin.by(dve.scalar_tensor_tensor(rows[:, r, :, :].rearrange("p b c -> p (b c)"),
                                               sgn[:, n, :, :].rearrange("p b c -> p (b c)"), 1.0,
                                               mag[:, n, :, :].rearrange("p b c -> p (b c)"), ALU.subtract, ALU.mult))
        s_rfin.by(dve.tensor_scalar(rows[:, 2, :, :], rows[:, 2, :, :], 1.0, None, ALU.add))

        s_tapo.wait(act)
        barrier()
        p.close()

    with ExitStack() as st:
        NM, NT = 3 * KT, WIN // P
        wqkv = sb(st, "wqkv", [P, KT, 3, C])
        wb = sb(st, "wb", [P, KT, H])
        cw = sb(st, "cw", [P, 6, TAPS])
        proj = sb(st, "proj", [P, 6, TAPS - 1 + L])
        btok = sb(st, "btok", [P, TILES, H])
        bT = sb(st, "bT", [P, 2, P])
        xw = sb(st, "xw", [P, 2, NT, C])
        xn = sb(st, "xn", [P, 2, NT, C])
        cur = sb(st, "cur", [P, 2, 2, KT])
        hT = sb(st, "hT", [P, 2, KT, WIN])
        acc = sb(st, "acc", [P, 2, WIN])
        sil = sb(st, "sil", [P, NM, WIN])
        tm = sb(st, "tm", [P, 2, NT, 4, C])
        vs = sb(st, "vs", [P, KT, FIRS - 1 + L])
        fs = sb(st, "fs", [P, KT, FIRS])
        short = sb(st, "short", [P, KT, WIN])
        part = sb(st, "part", [P, WIN])
        bn = sb(st, "bn1", [P, 2, NT, 6])
        mv = sb(st, "mv1", [P, 2, NT, 2])
        gro = sb(st, "gro", [P, 2, NT, 2, 2, CH])
        pT = ps(st, "pT", [P, WIN])
        pP = ps(st, "pP", [P, 2, WIN])
        pB = ps(st, "pB", [P, WIN])
        pK = ps(st, "pK", [P, 2, WIN])
        pR = ps(st, "pR", [P, 2, NT, 2 * 2, CH])

        p = sems.loop(1)
        s_w, s_z = p.dma(8), p.step(2)
        s_w.by(sp.dma_start(fs[:, :, :], a["fir_s"].rearrange("(k p) n -> p k n", p=P)))
        s_z.by(dve.memset(vs[:, :, 0:FIRS - 1], 0.0))
        for n, w in enumerate(("Wq", "Wk", "Wv")):
            s_w.by(sp.dma_start(wqkv[:, :, n, :], a[w].rearrange("(k p) n -> p k n", p=P)))
        s_w.by(sp.dma_start(wb[:, :, :], a["Wb"].rearrange("(k p) n -> p k n", p=P)))
        for n, w in enumerate(("qc", "kc", "vc")):
            s_w.by(sp.dma_start(cw[:, 2 * n:2 * n + 2, :], a[w].rearrange("(k p) n -> p k n", p=P)))
        s_z.by(dve.memset(proj[:, :, 0:TAPS - 1], 0.0))
        for e in (pe, act, dve, pool):
            s_w.wait(e)
        s_z.wait(dve)
        s_z.wait(pool)

        WINS, NW = TOK // WIN, L // WIN
        q = sems.loop(WINS)
        s_ld, s_hto, s_tmo, s_gro = [Ring(sems, WINS, n, 2) for n in (1, 1, 4, 1)]
        s_cur, s_ln, s_tr, s_ht, s_bt, s_be = q.step(), q.step(NT), q.step(KT), q.step(KT), q.step(), q.step()
        s_pr, s_ev, s_cv, s_si, s_tt, s_te = q.step(NM), q.step(NM), q.step(3 * NM), q.step(NM), q.step(NM), q.step(NM)
        s_gm, s_ge = q.step(2), q.step()
        s_bn, s_mv, s_va, s_sd, s_ri = q.step(NT), q.step(NT), q.step(), q.step(), q.step()
        s_sh, s_ts, s_es = q.step(KT * (2 * FIRS - 1)), q.step(KT), q.step(KT)

        def done(step, e, t, m, alone=False):
            if not isinstance(t, int) or t * NM + m >= 0:
                step.until(e, t, m + 1, alone)

        def load1(t, slot, round):
            s_ln.back(sp, t, 2)
            s_ld.by(sp.dma_start(xw[:, slot, :, :], a["x"][bass.ds(t * WIN, WIN), :].rearrange("(t p) c -> p t c", p=P)), slot)

        def stats(t, slot, round):
            s_ht.back(dve, t, 2)
            s_cur.by(dve.tensor_copy(cur[:, slot, :, :], scT[:, bass.ds(t // NW, 1), :, :].rearrange("p a w k -> p (a w) k")))
            s_ld.wait(dve, slot, round)
            for n in range(NT):
                s_bn.by(dve.bn_stats(bn[:, slot, n, :], xw[:, slot, n, :]))
            s_bn.wait(dve, t=t, alone=True)
            s_ln.back(dve, t, 2, alone=True)
            for n in range(NT):
                s_mv.by(dve.bn_aggr(mv[:, slot, n, :], bn[:, slot, n, :]))
            s_mv.wait(dve, t=t)
            s_va.by(dve.tensor_scalar(mv[:, slot, :, 1], mv[:, slot, :, 1], EPS_LN, None, ALU.add))
            s_va.wait(act, t=t)
            s_sd.by(act.activation(mv[:, slot, :, 1], mv[:, slot, :, 1], ACT.Sqrt))

        def norm(t, slot, round):
            s_sd.wait(dve, t=t)
            s_ri.by(dve.reciprocal(mv[:, slot, :, 1], mv[:, slot, :, 1]))
            s_ri.wait(dve, t=t)
            s_tr.back(dve, t, 2)
            for n in range(NT):
                s_ln.by(dve.tensor_scalar(xn[:, slot, n, :], xw[:, slot, n, :], mv[:, slot, n, 0:1],
                                          mv[:, slot, n, 1:2], ALU.subtract, ALU.mult))

        def channels_first(k):
            def stage(t, slot, round):
                s_ln.wait(pe, t=t)
                s_ht.until(pe, t, k)
                for n in range(NT):
                    i = pe.transpose(pT[:, n * P:(n + 1) * P], xn[:, slot, n, k * P:(k + 1) * P], ident[:, :])
                s_tr.by(i)
            return stage

        def modulate(k):
            def stage(t, slot, round):
                s_tr.wait(act, k + 1, t=t)
                s_cur.wait(act, t=t)
                s_hto.free(act, slot, round)
                s_pr.back(act, t, 2)
                s_bt.back(act, t, 2)
                s_ht.by(act.activation(hT[:, slot, k, :], pT[:, :], ACT.Identity, bias=cur[:, slot, 0, k:k + 1],
                                       scale=cur[:, slot, 1, k:k + 1]))
                if k == KT - 1:
                    s_ht.wait(sp, t=t)
                    s_hto.by(sp.dma_start(hT_d.rearrange("k p t -> p k t")[:, :, bass.ds(t * WIN, WIN)], hT[:, slot, :, :]), slot)
            return stage

        def beta_logits(t, slot, round):
            s_ht.wait(pe, t=t)
            s_be.back(pe, t, 1)
            s_es.back(pe, t, 2)
            for n in range(NT):
                for k in range(KT):
                    i = pe.matmul(pB[:, n * H:(n + 1) * H], hT[:, slot, k, n * P:(n + 1) * P], wb[:, k, :],
                                  start=(k == 0), stop=(k == KT - 1))
            s_bt.by(i)

        def keep_beta(t, slot, round):
            s_bt.wait(dve, t=t)
            s_be.by(dve.tensor_copy(btok[:, bass.ds(t * NT, NT), :].rearrange("p n h -> p (n h)"), pB[:, 0:NT * H]))

        def project(m):
            def stage(t, slot, round):
                if m == 0:
                    s_ht.wait(pe, t=t)
                done(s_ev, pe, t, m - 2)
                for k in range(KT):
                    i = pe.matmul(pP[:, m % 2, :], wqkv[:, k, m // 2, (m % 2) * P:(m % 2 + 1) * P], hT[:, slot, k, :],
                                  start=(k == 0), stop=(k == KT - 1))
                s_pr.by(i)
            return stage

        def convolve(m):
            def stage(t, slot, round):
                done(s_pr, act, t, m)
                done(s_si, act, t, m - 2)
                act.activation(proj[:, m, bass.ds(t % NW * WIN + TAPS - 1, WIN)], pP[:, m % 2, :], ACT.Copy)
                s_ev.by(act.activation(acc[:, m % 2, :], pP[:, m % 2, :], ACT.Copy, scale=cw[:, m, TAPS - 1:TAPS]))
                done(s_ev, dve, t, m)
                for n, tap in enumerate((2, 1, 0)):
                    if n:
                        s_cv.wait(dve, 3 * m + n, t=t)
                    s_cv.by(dve.scalar_tensor_tensor(acc[:, m % 2, :], proj[:, m, bass.ds(t % NW * WIN + tap, WIN)],
                                                     cw[:, m, tap:tap + 1], acc[:, m % 2, :], ALU.mult, ALU.add))
            return stage

        def silu(m):
            def stage(t, slot, round):
                s_cv.wait(act, 3 * m + 3, t=t)
                done(s_tt, act, t, m - NM)
                if m // 2 == 1:
                    s_gm.back(act, t, 1)
                if m // 2 == 2:
                    act.activation(vs[:, m - 4, bass.ds(t % NW * WIN + FIRS - 1, WIN)], acc[:, m % 2, :], ACT.Silu)
                s_si.by(act.activation(sil[:, m, :], acc[:, m % 2, :], ACT.Silu))
            return stage

        def to_tokens(m):
            def stage(t, slot, round):
                done(s_si, pe, t, m)
                done(s_te, pe, t, m - 2)
                for n in range(NT):
                    i = pe.transpose(pK[:, m % 2, n * P:(n + 1) * P], sil[:, m, n * P:(n + 1) * P], ident[:, :])
                s_tt.by(i)
            return stage

        def keep_tokens(m):
            def stage(t, slot, round):
                done(s_tt, dve, t, m)
                if m == 0:
                    s_tmo.free(dve, slot, round)
                s_te.by(dve.tensor_copy(tm[:, slot, :, m // 2, (m % 2) * P:(m % 2 + 1) * P],
                                        pK[:, m % 2, :].rearrange("p (t c) -> p t c", t=NT)))
                if m % 2:
                    done(s_te, sp, t, m)
                    s_tmo.by(sp.dma_start(qkv_d[m // 2, bass.ds(t * WIN, WIN), :].rearrange("(t p) c -> p t c", p=P),
                                          tm[:, slot, :, m // 2, :]), slot)
            return stage

        def gram(w):
            def stage(t, slot, round):
                done(s_si, pe, t, 2 + w, alone=True)
                if w == 0:
                    s_ge.back(pe, t, 1, alone=True)
                for n in range(NT):
                    for c in range(P // CH):
                        for h in range(2):
                            keys = sil[h * D:(h + 1) * D, 2 + w, n * P + c * CH:n * P + (c + 1) * CH]
                            i = pe.matmul(pR[c * CH:(c + 1) * CH, h, n, w, :], keys, keys, start=True, stop=True,
                                          tile_position=(h * D, c * CH))
                s_gm.by(i)
            return stage

        def short_fir(k):
            def stage(t, slot, round):
                done(s_si, pool, t, 4 + k)
                s_ts.back(pool, t, 1)
                n_sh = k * (2 * FIRS - 1)
                for n in range(FIRS):
                    dst = short[:, k, :] if n == 0 else part[:, :]
                    if n_sh:
                        s_sh.wait(pool, n_sh, t=t)
                    else:
                        s_sh.back(pool, t, 1)
                    s_sh.by(pool.tensor_tensor(dst, vs[:, k, bass.ds(t % NW * WIN + n, WIN)],
                                               fs[:, k, n:n + 1].broadcast_to([P, WIN]), ALU.mult))
                    n_sh += 1
                    if n:
                        s_sh.wait(pool, n_sh, t=t)
                        s_sh.by(pool.tensor_tensor(short[:, k, :], short[:, k, :], part[:, :], ALU.add))
                        n_sh += 1
            return stage

        def short_to_tokens(k):
            def stage(t, slot, round):
                s_sh.wait(pe, (k + 1) * (2 * FIRS - 1), t=t)
                s_be.wait(pe, t=min(t + 1, WINS - 1) if isinstance(t, int) else t + 1)
                s_es.until(pe, t, k)
                for n in range(NT):
                    i = pe.transpose(pB[:, n * P:(n + 1) * P], short[:, k, n * P:(n + 1) * P], ident[:, :])
                s_ts.by(i)
            return stage

        def keep_short(k):
            def stage(t, slot, round):
                s_ts.wait(act, k + 1, t=t)
                if k == 0:
                    s_tmo.free(act, slot, round)
                s_es.by(act.activation(tm[:, slot, :, 3, k * P:(k + 1) * P], pB[:, :].rearrange("p (t c) -> p t c", t=NT), ACT.Copy))
                if k == KT - 1:
                    s_es.wait(sp, t=t)
                    s_tmo.by(sp.dma_start(qkv_d[3, bass.ds(t * WIN, WIN), :].rearrange("(t p) c -> p t c", p=P), tm[:, slot, :, 3, :]), slot)
            return stage

        def keep_gram(t, slot, round):
            s_gm.wait(act, t=t)
            s_gro.free(act, slot, round)
            for h in range(2):
                i = act.activation(gro[:, slot, :, :, h, :], pR[:, h, :, 0:2, :], ACT.Copy)
            s_ge.by(i)
            s_ge.wait(sp, t=t)
            s_gro.by(sp.dma_start(gram_d[bass.ds(t * WIN, WIN)].rearrange("(t p) h j -> p t (h j)", p=P),
                                  gro[:, slot, :, :, :, :].rearrange("p t w h j -> p t (w h j)")), slot)

        order = [(load1, 0)]
        copies = {0: [(keep_gram, 3), (keep_beta, 2)], 3: [(modulate(0), 1)], 4: [(modulate(1), 1), (keep_short(0), 3)],
                  5: [(keep_short(1), 3)]}
        between = {0: [(stats, 1), (short_fir(0), 3)], 1: [(norm, 1), (short_fir(1), 3)], 2: [(channels_first(0), 1)],
                   3: [(channels_first(1), 1), (short_to_tokens(0), 3)], 4: [(gram(0), 2), (short_to_tokens(1), 3)],
                   5: [(gram(1), 2), (beta_logits, 1)]}
        for m in range(NM):
            order.append((convolve(m), 2))
            order.append((silu((m - 1) % NM), 2 + (m < 1)))
            order += copies.get(m, [])
            order.append((project((m + 2) % NM), 2 - (m + 2 >= NM)))
            order.append((to_tokens((m - 2) % NM), 2 + (m < 2)))
            order.append((keep_tokens((m - 3) % NM), 2 + (m < 3)))
            order += between[m]
        flow(nc, WINS, order, 3, slots=2)
        s_q, s_qe, s_qo = p.step(), p.step(), p.dma()
        s_be.wait_all(pe)
        s_es.wait_all(pe)
        s_be.wait_all(dve)
        for w in range(2):
            i = pe.transpose(pB[:, w * P:(w + 1) * P], btok[:, w * TILES // 2:(w + 1) * TILES // 2, :].rearrange("p t h -> p (t h)"),
                             ident[:, :])
        s_q.by(i)
        s_q.wait(dve)
        s_qe.by(dve.tensor_copy(bT[:, :, :], pB[:, 0:2 * P].rearrange("p (w t) -> p w t", w=2)))
        s_qe.wait(sp)
        s_qo.by(sp.dma_start(beta_d.rearrange("(w t) h p -> (t h) w p", w=2), bT[:, :, :]))
        s_qo.wait(sp)
        for s in (s_hto, s_tmo, s_gro):
            s.wait_all(sp)
        barrier()
        for s in (s_ld, s_hto, s_tmo, s_gro):
            s.close()
        q.close()
        p.close()

    hold = ExitStack()
    rnorm = sb(hold, "rnorm", [P, UNITS])
    betac = sb(hold, "betac", [P, UNITS])
    with ExitStack() as st:
        QC, G = 64, 4
        NB = 4
        NS = UNITS * H // P
        vwin = sb(st, "vwin", [SPAN, 2, NBLK, QC])
        band = sb(st, "band", [SPAN, NB, G, BLK])
        vst = sb(st, "vst", [SPAN, NB, G, NBLK])
        fo = sb(st, "fo", [NBLK, BLK, 2 * QC])
        amat = sb(st, "amat", [P, NS, CH, CH])
        tinv = sb(st, "tinv", [P, NS, CH, CH])
        prod = sb(st, "prod", [P, NS, CH * CH // 4])
        bs = sb(st, "bs", [P, NS, CH])
        rk = sb(st, "rkc", [P, NS, CH])
        coef = sb(st, "coef", [P, NS, CH])
        pf = ps(st, "pf", [NBLK, NB, 512])
        pn = ps(st, "pn", [P, 4, P])

        NQ = C // QC
        GT = QC // G
        rounds = GT // NB
        q = sems.loop(NQ * rounds)
        s_bd, s_cp, s_mm, s_ev = [[make() for _ in range(NB)] for make in (q.dma, q.step, q.step, q.step)]
        w = sems.loop(1)
        s_v, s_vz = [w.dma(2 * NB) for _ in range(NQ)], w.step(NQ)
        PIECE = NBLK // (2 * NB)

        def load_windows(e, c4, n):
            wins = bass.AP(qkv_d.tensor, (n * (PIECE * BLK) + (2 * TOK - (FIRL - 1))) * C + c4 * QC,
                           [[C, SPAN], [BLK * C, PIECE], [1, QC]])
            s_v[c4].by(e.dma_start(vwin[:, c4 % 2, bass.ds(n * PIECE, PIECE), :], wins))

        for n in range(2 * NB):
            load_windows(sp, 0, n)

        p = sems.loop(1)
        s_a, s_b, s_sg, s_d, s_sq, s_i = p.dma(), p.dma(2 * H), p.step(), p.step(2), p.step(), p.step(8)
        raw = tinv
        s_a.by(act.dma_start(raw[:, :, :, :].rearrange("p s i j -> p (s i j)"),
                             gram_d.rearrange("t h j -> (t h j)").rearrange("(p x) -> p x", p=P)))
        for h in range(H):
            for u in range(2):
                src = bass.AP(beta_d.tensor, beta_d.offset + h * P + u * CH, [[H * P, TILES], [2 * CH, P // (2 * CH)], [1, CH]])
                s_b.by(act.dma_start(bs[:, u * H + h, :], src))
        s_b.wait(act)
        s_sg.by(act.activation(bs[:, :, :], bs[:, :, :], ACT.Sigmoid))
        raw5 = raw[:, :, :, :].rearrange("p s i j -> p (s i j)").rearrange("p (u i h j) -> p u h i j", u=2, i=CH, h=H)
        flat = raw[:, :, :, :].rearrange("p s i j -> p (s i j)")
        s_a.wait(dve)
        for u in range(2):
            base = u * H * CH * CH
            for h in range(H):
                i = dve.tensor_scalar(coef[:, u * H + h, :], flat[:, base + h * CH:base + h * CH + (CH - 1) * (H * CH + 1) + 1:H * CH + 1],
                                      EPS_L2, None, ALU.add)
            s_d.by(i)
        s_d.wait(act)
        s_sq.by(act.activation(coef[:, :, :], coef[:, :, :], ACT.Sqrt))
        s_sq.wait(dve)
        s_i.by(dve.reciprocal(rk[:, :, :], coef[:, :, :]))
        s_i.wait(dve, 1)
        s_sg.wait(dve)
        s_i.by(dve.tensor_tensor(coef[:, :, :], bs[:, :, :], rk[:, :, :], ALU.mult))
        s_i.wait(dve, 2)
        for u in range(2):
            s_i.by(dve.tensor_tensor(amat[:, u * H:(u + 1) * H, :, :], raw5[:, u], coef[:, u * H:(u + 1) * H, :].unsqueeze(3)
                                     .broadcast_to([P, H, CH, CH]), ALU.mult))
        s_i.wait(dve, 4)
        s_i.by(dve.tensor_tensor(amat[:, :, :, :], amat[:, :, :, :], rk[:, :, :].unsqueeze(2).broadcast_to([P, NS, CH, CH]), ALU.mult))
        s_i.by(dve.memset(tinv[:, :, :, :], 0.0))
        s_i.wait(dve, 6)
        s_i.by(dve.memset(tinv[:, :, :, :].rearrange("p s i j -> p s (i j)")[:, :, 0:CH * CH:CH + 1], 1.0))
        s_tn = p.step()
        s_i.wait(pe, 1)
        s_sg.wait(pe)
        for n, x in enumerate((rk, bs)):
            for u in range(2):
                i = pe.transpose(pn[:, 2 * n + u, :], x[:, u * H:(u + 1) * H, :].rearrange("p h i -> p (h i)"), ident[:, :])
        s_tn.by(i)
        s_tn.wait(dve)
        for n, x in enumerate((rnorm, betac)):
            i = dve.tensor_copy(x[:, :].rearrange("p (c u) -> p u c", u=2), pn[:, 2 * n:2 * n + 2, :])
        s_i.by(i)
        s_i.wait(dve)
        s_f = p.step(2 * (CH - 1))
        for j in range(CH - 1):
            nc_, ni = j + 1, CH - 1 - j
            col = amat[:, :, j + 1:, j].unsqueeze(2).broadcast_to([P, NS, nc_, ni])
            row = tinv[:, :, 0:nc_, j].unsqueeze(3).broadcast_to([P, NS, nc_, ni])
            tmp = prod[:, :, 0:nc_ * ni].rearrange("p s (c i) -> p s c i", c=nc_)
            s_f.by(dve.tensor_tensor(tmp, col, row, ALU.mult))
            s_f.wait(dve, 2 * j + 1)
            s_f.by(dve.tensor_tensor(tinv[:, :, 0:nc_, j + 1:], tinv[:, :, 0:nc_, j + 1:], tmp, ALU.subtract))
            s_f.wait(dve, 2 * j + 2)

        s_fo = p.dma(NQ // 2)
        for c4 in range(NQ):
            c0 = c4 * QC
            s_v[c4].wait(pool)
            i = pool.memset(vwin[0:FIRL - 1, c4 % 2, :, :].rearrange("p (b n) c -> p b n c", b=B)[:, :, 0, :], 0.0)
            s_vz.by(i)
            s_vz.wait(act, c4 + 1)
            if c4 == 2:
                act.wait_ge(s_fo.sem, s_fo.base + 16)
            if c4 + 1 < NQ and c4:
                for par in range(NB):
                    s_cp[par].wait(sp, t=c4 * rounds - 1)
            with nc.Fori(0, rounds, engines=[ENG.SP, ENG.PE, ENG.Activation]) as i:
                for par in range(NB):
                    t2 = i + c4 * rounds
                    s_mm[par].back(sp, t2, 1)
                    cb = (i * (NB * G) + (c0 + par * G)) * RW
                    src = bass.AP(taps_d.tensor, cb, [[1, SPAN], [RW, G], [1, BLK]])
                    s_bd[par].by(sp.dma_start(band[:, par, :, :], src))
                    if c4 + 1 < NQ and par % 2:
                        load_windows(sp, c4 + 1, i * 2 + par // 2)
                    s_mm[par].back(act, t2, 1)
                    s_cp[par].by(act.activation(vst[:, par, :, :], vwin[:, c4 % 2, :, bass.ds((i * NB + par) * G, G)]
                                                .rearrange("p n g -> p g n"), ACT.Copy))
                    s_cp[par].wait(pe, t=t2)
                    s_bd[par].wait(pe, t=t2)
                    s_ev[par].back(pe, t2, 1)
                    for g in range(G):
                        mm = pe.matmul(pf[:, par, g * BLK:(g + 1) * BLK], vst[:, par, g, :], band[:, par, g, :], start=True, stop=True)
                    s_mm[par].by(mm)
                    for n in ([par - 1] if par else []) + ([par] if par == NB - 1 else []):
                        s_mm[n].wait(act, t=t2)
                        s_ev[n].by(act.activation(fo[:, :, bass.ds((i * NB + n) * G + c4 % 2 * QC, G)],
                                                  pf[:, n, 0:G * BLK].rearrange("p (g t) -> p t g", g=G)[:, ::-1, :], ACT.Copy))
            for par in range(NB):
                s_ev[par].wait(sp, t=(c4 + 1) * rounds - 1)
            if c4 % 2:
                dst = fir_d[:, c0 - QC:c0 + QC].rearrange("(n t) c -> n t c", t=BLK)
                s_fo.by(sp.dma_start(dst, fo[:, :, :]))
        s_to = p.pool_dma()
        s_f.wait(pool)
        s_to.by(pool.dma_start(tinv_d.rearrange("u (h i) j -> (u h i j)", h=H).rearrange("(p x) -> p x", p=P),
                             tinv[:, :, :, :].rearrange("p s i j -> p (s i j)")))
        s_to.wait(sp)
        s_fo.wait(sp)
        barrier()
        w.close()
        q.close()
        p.close()

    with ExitStack() as st:
        turns = CPB
        NP = H // 2
        rk = sb(st, "rk", [P, 2, UNITS])
        kqv = sb(st, "kqv", [P, 4, 3, B, D])
        tc = sb(st, "tc", [P, 4, B, CH])
        kx = sb(st, "kx", [P, 4, B, P])
        qx = sb(st, "qx", [P, 4, B, P])
        qq = sb(st, "qq", [P, 4, B, D])
        rq = sb(st, "rq", [P, 4, B])
        kbx = sb(st, "kbx", [P, 4, B, P])
        vb = sb(st, "vb", [P, 4, B, D])
        tx = sb(st, "tx", [P, 4, B, P])
        kT = sb(st, "kT", [P, 4, B, P])
        qT = sb(st, "qT", [P, 4, B, P])
        atT = sb(st, "atT", [P, 4, B, P])
        wT = sb(st, "wT", [P, 4, B, P])
        uu = sb(st, "uu", [P, 4, B, D])
        ui = sb(st, "ui", [P, 4, B, D])
        state = sb(st, "state", [P, B, NP, D])
        do = sb(st, "do", [P, 4, B, D])
        pA = ps(st, "pA", [P, B, P])
        pBq = ps(st, "pBq", [P, B, P])
        pC = ps(st, "pC", [P, B, P])
        pD = ps(st, "pD", [P, B, P])
        pF = ps(st, "pF", [P, B, 2 * D])
        pG = ps(st, "pG", [P, B, 2 * D])
        pH = ps(st, "pH", [P, NP, 512])

        p = sems.loop(1)
        s_z, s_r = p.step(), p.step(2)
        s_z.by(dve.memset(state[:, :, :, :], 0.0))
        for s in range(2):
            s_r.by(dve.tensor_scalar(rk[:, s, :], rnorm[:, :], parity[:, s:s + 1], None, ALU.mult))
        s_r.wait(pool)
        s_z.wait(pe)
        q = sems.loop(turns)
        s_ld, s_do = Ring(sems, turns, H + 1), Ring(sems, turns, H)
        s_kx, s_qx, s_kb, s_vb, s_tx = q.step(), q.step(), q.step(), q.step(), q.step()
        s_qq, s_qn, s_qr, s_rq = q.step(), q.step(2), q.step(), q.step()
        s_tk, s_tq, s_ek, s_eq = q.step(), q.step(), q.step(), q.step()
        s_at, s_ea, s_w, s_ew, s_u, s_eu = q.step(), q.step(), q.step(), q.step(), q.step(), q.step()
        s_ws, s_ui, s_qs, s_ku, s_st, s_o, s_eo = [q.step() for _ in range(7)]

        def unit_cols(ap2, t):
            return ap2.rearrange("p (b c) -> p b c", b=B)[:, :, bass.ds(t, 1)].rearrange("p b c -> p (b c)")

        def per_half(x):
            return x.rearrange("p b (s d) -> p b s d", s=2)

        def load4(t, slot, round):
            for s in (s_kx, s_qx, s_vb, s_tx, s_qq):
                s.back(sp, t, 4)
            for h in range(H):
                src = qkv_d[0:3, :, h * D:(h + 1) * D].rearrange("n (b c i) f -> c i n b f", b=B, i=CH)
                s_ld.by(sp.dma_start(kqv[h * CH:(h + 1) * CH, slot, :, :, :],
                                     src[bass.ds(t, 1)].rearrange("o i n b f -> (o i) n b f")), slot)
            s_ld.by(sp.dma_start(tc[:, slot, :, :], tinv_d.rearrange("(b c) p i -> c p b i", b=B)[bass.ds(t, 1)]
                                 .rearrange("o p b i -> (o p) b i")), slot)

        def expand(t, slot, round):
            s_ld.wait(pool, slot, round)
            s_ku.back(pool, t, 4)
            s_tk.back(pool, t, 4)
            s_kb.back(pool, t, 4)
            sc = rk[:, :, :].rearrange("p s (b c) -> p b s c", b=B)[:, :, :, bass.ds(t, 1)].rearrange("p b s c -> p b (s c)")
            s_kx.by(pool.tensor_tensor(per_half(kx[:, slot, :, :]), kqv[:, slot, 1, :, :].unsqueeze(2).broadcast_to([P, B, 2, D]),
                                       sc.unsqueeze(3).broadcast_to([P, B, 2, D]), ALU.mult))
            s_tq.back(pool, t, 4)
            s_qx.by(pool.tensor_tensor(per_half(qx[:, slot, :, :]), kqv[:, slot, 0, :, :].unsqueeze(2).broadcast_to([P, B, 2, D]),
                                       parity[:, :].unsqueeze(1).unsqueeze(3).broadcast_to([P, B, 2, D]), ALU.mult))
            beta = unit_cols(betac[:, :], t)
            s_u.back(pool, t, 4)
            s_vb.by(pool.tensor_tensor(vb[:, slot, :, :], kqv[:, slot, 2, :, :], beta.unsqueeze(2).broadcast_to([P, B, D]), ALU.mult))
            s_ld.wait(act, slot, round)
            s_qn.back(act, t, 4)
            s_qq.by(act.activation(qq[:, slot, :, :], kqv[:, slot, 0, :, :], ACT.Square))
            s_ld.wait(dve, slot, round)
            s_u.back(dve, t, 4)
            s_w.back(dve, t, 4)
            s_tx.by(dve.tensor_tensor(tx[:, slot, :, :].rearrange("p b (h i) -> p b h i", h=H),
                                      tc[:, slot, :, :].unsqueeze(2).broadcast_to([P, B, H, CH]),
                                      blockdiag[:, :].rearrange("p (h i) -> p h i", h=H).unsqueeze(1).broadcast_to([P, B, H, CH]),
                                      ALU.mult))

        def turn_kq(t, slot, round):
            s_kx.wait(pe, t=t)
            s_eu.back(pe, t, 1)
            for b in range(B):
                i = pe.transpose(pA[:, b, :], kx[:, slot, b, :], ident[:, :])
            s_tk.by(i)
            s_qx.wait(pe, t=t)
            s_eq.back(pe, t, 1)
            for b in range(B):
                i = pe.transpose(pBq[:, b, :], qx[:, slot, b, :], ident[:, :])
            s_tq.by(i)
            s_tk.wait(act, t=t)
            s_at.back(act, t, 4)
            s_ek.by(act.activation(kT[:, slot, :, :], pA[:, :, :], ACT.Copy))
            s_tq.wait(act, t=t)
            s_qs.back(act, t, 4)
            s_eq.by(act.activation(qT[:, slot, :, :], pBq[:, :, :], ACT.Copy))
            s_kx.wait(dve, t=t)
            s_w.back(dve, t, 4)
            s_kb.by(dve.tensor_tensor(kbx[:, slot, :, :], kx[:, slot, :, :],
                                      unit_cols(betac[:, :], t).unsqueeze(2).broadcast_to([P, B, P]), ALU.mult))
            s_qq.wait(dve, t=t)
            s_eo.back(dve, t, 4)
            s_qn.by(dve.tensor_reduce(rq[:, slot, :], qq[:, slot, :, :], AX, ALU.add))
            s_qn.wait(dve, 1, t=t)
            s_qn.by(dve.tensor_scalar(rq[:, slot, :], rq[:, slot, :], EPS_L2, None, ALU.add))

        def q_root(t, slot, round):
            s_qn.wait(act, t=t)
            s_qr.by(act.activation(rq[:, slot, :], rq[:, slot, :], ACT.Sqrt))

        def q_inverse(t, slot, round):
            s_qr.wait(dve, t=t)
            s_rq.by(dve.reciprocal(rq[:, slot, :], rq[:, slot, :]))

        def attention(t, slot, round):
            s_ek.wait(pe, t=t)
            s_eq.wait(pe, t=t)
            s_ea.back(pe, t, 1)
            for b in range(B):
                i = pe.matmul(pC[:, b, :], kT[:, slot, b, :], qT[:, slot, b, :], start=True, stop=True)
            s_at.by(i)
            s_at.wait(dve, t=t)
            s_o.back(dve, t, 4)
            s_ea.by(dve.tensor_tensor(atT[:, slot, :, :], pC[:, :, :], causal[:, :].unsqueeze(1).broadcast_to([P, B, P]), ALU.mult))

        def w_and_u(t, slot, round):
            s_kb.wait(pe, t=t)
            s_tx.wait(pe, t=t)
            s_ew.back(pe, t, 1)
            for b in range(B):
                i = pe.matmul(pD[:, b, :], kbx[:, slot, b, :], tx[:, slot, b, :], start=True, stop=True)
            s_w.by(i)
            s_w.wait(act, t=t)
            s_ws.back(act, t, 4)
            s_ew.by(act.activation(wT[:, slot, :, :], pD[:, :, :], ACT.Copy))
            s_vb.wait(pe, t=t)
            s_ek.wait(pe, t=t)
            for b in range(B):
                i = pe.matmul(pA[:, b, 0:D], tx[:, slot, b, :], vb[:, slot, b, :], start=True, stop=True)
            s_u.by(i)
            s_u.wait(act, t=t)
            s_ui.back(act, t, 4)
            s_eu.by(act.activation(uu[:, slot, :, :], pA[:, :, 0:D], ACT.Copy))

        def correct(t, slot, round):
            s_st.back(pe, t, 1)
            s_ew.wait(pe, t=t)
            s_ui.back(pe, t, 1)
            for b in range(B):
                for n in range(NP):
                    r = slice(n * D, (n + 1) * D)
                    i = pe.matmul(pF[r, b, 0:D], wT[:, slot, b, r], state[:, b, n, :], start=True, stop=True)
            s_ws.by(i)
            s_ws.wait(dve, t=t)
            s_eu.wait(dve, t=t)
            s_ku.back(dve, t, 4)
            s_o.back(dve, t, 4)
            s_ui.by(dve.tensor_tensor(ui[:, slot, :, :], uu[:, slot, :, :], pF[:, :, 0:D], ALU.subtract))
            s_eo.back(pe, t, 1)
            for b in range(B):
                for n in range(NP):
                    r = slice(n * D, (n + 1) * D)
                    i = pe.matmul(pG[r, b, 0:D], qT[:, slot, b, r], state[:, b, n, :], start=(b == 0), stop=False,
                                  skip_group_check=True)
            s_qs.by(i)

        def advance(t, slot, round):
            s_ui.wait(pe, t=t)
            for b in range(B):
                for n in range(NP):
                    r = slice(n * D, (n + 1) * D)
                    i = pe.matmul(pH[:, n, b * D:(b + 1) * D], kx[r, slot, b, :], ui[r, slot, b, :], start=True, stop=True)
            s_ku.by(i)
            s_ku.wait(dve, t=t)
            s_qs.wait(dve, t=t)
            s_st.by(dve.tensor_tensor(state[:, :, :, :], state[:, :, :, :], pH[:, :, 0:B * D].rearrange("p n (b d) -> p b n d", b=B), ALU.add))

        def attend(t, slot, round):
            s_ea.wait(pe, t=t)
            for b in range(B):
                i = pe.matmul(pG[:, b, 0:D], atT[:, slot, b, :], ui[:, slot, b, :], start=False, stop=True, skip_group_check=True)
            s_o.by(i)

        def keep_delta(t, slot, round):
            s_o.wait(dve, t=t)
            s_rq.wait(dve, t=t)
            s_do.free(dve, slot, round)
            s_eo.by(dve.tensor_tensor(do[:, slot, :, :], pG[:, :, 0:D], rq[:, slot, :].unsqueeze(2).broadcast_to([P, B, D]), ALU.mult))
            s_eo.wait(sp, t=t)
            for h in range(H):
                dst = delta_d[:, h * D:(h + 1) * D].rearrange("(b c i) f -> c i b f", b=B, i=CH)
                s_do.by(sp.dma_start(dst[bass.ds(t, 1)].rearrange("o i b f -> (o i) b f"), do[h * CH:(h + 1) * CH, slot, :, :]), slot)

        flow(nc, turns, [(load4, 0), (correct, 4), (attention, 3), (q_root, 3), (advance, 4), (w_and_u, 3), (attend, 4),
                         (q_inverse, 4), (turn_kq, 2), (keep_delta, 4), (expand, 1)], 2)
        s_do.wait_all(sp)
        barrier()
        s_do.close()
        s_ld.close()
        q.close()
        p.close()
    hold.close()

    gate = ExitStack()
    weight = sb(gate, "weight", [P, TILES, H, NBR])
    BR = (qkv_d[3], fir_d, delta_d, qkv_d[2])

    def branch(n, t):
        return BR[n][bass.ds(t * P, P), :]

    NG = H * NBR
    temp = sb(gate, "temp", [P, H])
    floor = sb(gate, "floor", [P, NG])
    onorm = sb(gate, "onorm", [P, 1])
    GW = P
    with ExitStack() as st:
        w1h = sb(st, "w1h", [P, KT, GW])
        w1b = sb(st, "w1b", [P, 2, GW])
        w1m = sb(st, "w1m", [P, 2, GW])
        w1s = sb(st, "w1s", [D, NBR, 2, GW])
        half = sb(st, "half", [P, P])
        pick = sb(st, "pick", [D, 4 * NG - 1])
        wst = sb(st, "wst", [2 * NG, H, GW])
        w2 = sb(st, "w2", [GW, NBR])
        b1 = sb(st, "b1", [GW, 1])
        b2 = sb(st, "b2", [P, NBR])
        br = sb(st, "br", [P, 4, 2, H, 2, D])
        ht = sb(st, "ht", [P, 4, KT, P])
        sq = sb(st, "sq", [P, 4, NG, D])
        stt = sb(st, "stt", [P, 4, 2, NG])
        bT5 = sb(st, "bT5", [P, 4, 2, H, P])
        sT = sb(st, "sT", [2 * NG, 4, P])
        hid = sb(st, "hid", [P, 4, P])
        hm = sb(st, "hm", [P, 4, H, P])
        pX = ps(st, "pX", [P, 2, H, P])
        pS = ps(st, "pS", [P, 512])
        pI = ps(st, "pI", [P, 512])
        pM = ps(st, "pM", [P, 2, H, P])
        pL = ps(st, "pL", [P, 2, 512])

        p = sems.loop(1)
        s_w, s_c = p.dma(10 + 3 * NBR), p.step(3)
        s_w.by(sp.dma_start(w1h[:, :, :], a["gW1"][0:C, :].rearrange("(k p) n -> p k n", p=P)))
        s_w.by(sp.dma_start(w1b[:, :, :], a["gW1"][C + 3 * NBR * D:, :].rearrange("(k p) n -> p k n", p=P)))
        for n in range(NBR):
            r = C + 3 * D * n
            s_w.by(sp.dma_start(w1m[(n % 2) * D:(n % 2 + 1) * D, n // 2, :], a["gW1"][r:r + D, :]))
            for s in range(2):
                s_w.by(sp.dma_start(w1s[:, n, s, :], a["gW1"][r + (s + 1) * D:r + (s + 2) * D, :]))
        s_w.by(sp.dma_start(w2[:, :], a["gW2"]))
        s_w.by(sp.dma_start(b1[:, :], a["gb1"]))
        s_w.by(sp.dma_start(b2[:, :], a["gb2"][0].partition_broadcast(P)))
        s_w.by(sp.dma_start(temp[:, :], a["temp"][0].partition_broadcast(P)))
        s_w.by(sp.dma_start(floor[:, :], a["floor"][0].partition_broadcast(P)))
        for n in range(2):
            s_w.by(sp.dma_start(onorm[n * D:(n + 1) * D, :], a["onorm"].rearrange("o d -> d o")))
        s_w.by(sp.dma_start(sT[:, 0, :], a["gW1"][0:2 * NG, :]))
        s_c.by(dve.memset(half[:, :], 0.0))
        s_c.by(dve.memset(pick[:, :], 0.0))
        s_c.wait(dve, 2)
        dve.memset(half[0:D, 0:D], 1.0 / D)
        dve.memset(half[D:P, D:P], 1.0 / D)
        s_c.by(dve.memset(pick[:, 2 * NG - 1:2 * NG], 1.0))
        s_c.wait(pe)
        s_w.wait(pe)
        s_m, s_ma = p.step(1 + H), p.step(1 + H)
        for k in range(2):
            i = pe.matmul(pX[:, 0, k, :], half[:, :], w1m[:, k, :], start=True, stop=True)
        s_m.by(i)
        s_m.wait(dve, 1)
        s_w.wait(dve)
        s_ma.by(dve.tensor_tensor(w1b[:, :, :], w1b[:, :, :], pX[:, 0, 0:2, :], ALU.add))
        for h in range(H):
            if h:
                s_ma.wait(pe, h + 1)
            for n in range(NBR):
                for s in range(2):
                    c = s * NG + (n // 2) * 2 * H + h * 2 + n % 2
                    i = pe.matmul(pS[0:2 * NG, 0:GW], pick[:, 2 * NG - 1 - c:4 * NG - 1 - c], w1s[:, n, s, :],
                                  start=(n + s == 0), stop=(n == NBR - 1 and s == 1))
            s_m.by(i)
            s_m.wait(dve, h + 2)
            s_ma.by(dve.tensor_copy(wst[:, h, :], pS[0:2 * NG, 0:GW]))
        s_ma.wait(pe)
        s_w.wait(act)

        q = sems.loop(TILES)
        s_ld = Ring(sems, TILES, NBR + 1)
        s_sq, s_mx, s_v, s_rt, s_tx, s_ex, s_ts, s_es = q.step(), q.step(), q.step(2), q.step(), q.step(2), q.step(2), q.step(), q.step()
        s_hi, s_eh, s_m1, s_ad, s_ge, s_l, s_lo = [q.step() for _ in range(7)]

        def load_gate(t, slot, round):
            s_tx.back(sp, t, 4)
            s_sq.back(sp, t, 4)
            s_mx.back(sp, t, 4)
            s_hi.back(sp, t, 4)
            for n in range(NBR):
                s_ld.by(sp.dma_start(br[:, slot, n // 2, :, n % 2, :], branch(n, t).rearrange("p (h d) -> p h d", h=H)), slot)
            s_ld.by(sp.dma_start(ht[:, slot, :, :], hT_d.rearrange("k p t -> p k t")[:, :, bass.ds(t * P, P)]), slot)

        def square_and_turn(t, slot, round):
            groups = br[:, slot, :, :, :, :].rearrange("p k h n d -> p (k h n) d")
            s_ld.wait(pool, slot, round)
            s_v.back(pool, t, 4)
            s_sq.by(pool.tensor_tensor(sq[:, slot, :, :], groups, groups, ALU.mult))
            s_ld.wait(dve, slot, round)
            s_ts.back(dve, t, 4)
            s_mx.by(dve.tensor_reduce(stt[:, slot, 1, :], groups, AX, ALU.max))
            s_ld.wait(pe, slot, round)
            for k in range(2):
                s_ex.back(pe, t, 1)
                for h in range(H):
                    i = pe.transpose(pX[:, k, h, :], br[:, slot, k, h, :, :].rearrange("p n d -> p (n d)"), ident[:, :])
                s_tx.by(i)

        def keep_turned(t, slot, round):
            s_tx.wait(act, 1, t=t)
            s_m1.back(act, t, 4)
            s_ex.by(act.activation(bT5[:, slot, 0, :, :], pX[:, 0, :, :], ACT.Copy))
            s_tx.wait(dve, 2, t=t)
            s_m1.back(dve, t, 4)
            s_ex.by(dve.tensor_copy(bT5[:, slot, 1, :, :], pX[:, 1, :, :]))
            s_sq.wait(dve, t=t)
            s_v.by(dve.tensor_reduce(stt[:, slot, 0, :], sq[:, slot, :, :], AX, ALU.add))
            s_v.wait(dve, 1, t=t)
            s_v.by(dve.tensor_scalar(stt[:, slot, 0, :], stt[:, slot, 0, :], 1.0 / D, 1e-8, ALU.mult, ALU.max))

        def hidden_part(t, slot, round):
            s_eh.back(pe, t, 1)
            for k in range(KT):
                i = pe.matmul(pI[:, 0:P], w1h[:, k, :], ht[:, slot, k, :], start=(k == 0), stop=(k == KT - 1))
            s_hi.by(i)

        def root(t, slot, round):
            s_hi.wait(act, t=t)
            s_ad.back(act, t, 4)
            s_eh.by(act.activation(hid[:, slot, :], pI[:, 0:P], ACT.Copy))
            s_v.wait(act, t=t)
            s_rt.by(act.activation(stt[:, slot, 0, :], stt[:, slot, 0, :], ACT.Sqrt))

        def turn_stats(t, slot, round):
            s_rt.wait(pe, t=t)
            s_mx.wait(pe, t=t)
            s_es.back(pe, t, 1)
            i = pe.transpose(pS[0:2 * NG, 0:P], stt[:, slot, :, :].rearrange("p s g -> p (s g)"), ident[:, :])
            s_ts.by(i)
            s_ts.wait(dve, t=t)
            s_m1.back(dve, t, 4)
            s_es.by(dve.tensor_copy(sT[:, slot, :], pS[0:2 * NG, 0:P]))

        def first_layer(t, slot, round):
            s_ex.wait(pe, t=t)
            s_ad.back(pe, t, 2)
            for k in range(2):
                pe.matmul(pM[:, slot % 2, :, :], w1b[:, k, :], bT5[:, slot, k, :, :], start=(k == 0), stop=False, skip_group_check=True)
            s_es.wait(pe, t=t)
            for h in range(H):
                i = pe.matmul(pM[:, slot % 2, h, :], wst[:, h, :], sT[:, slot, :], start=False, stop=True, skip_group_check=True)
            s_m1.by(i)

        def gelu(t, slot, round):
            s_m1.wait(dve, t=t)
            s_eh.wait(dve, t=t)
            s_l.back(dve, t, 4)
            s_ad.by(dve.tensor_tensor(hm[:, slot, :, :], pM[:, slot % 2, :, :], hid[:, slot, :].unsqueeze(1).broadcast_to([P, H, P]), ALU.add))
            s_ad.wait(act, t=t)
            s_ge.by(act.activation(hm[:, slot, :, :], hm[:, slot, :, :], ACT.Gelu, bias=b1[:, 0:1]))

        def second_layer(t, slot, round):
            s_ge.wait(pe, t=t)
            s_lo.back(pe, t, 2)
            for h in range(H):
                i = pe.matmul(pL[:, slot % 2, h * NBR:(h + 1) * NBR], hm[:, slot, h, :], w2[:, :], start=True, stop=True)
            s_l.by(i)

        def keep_logits(t, slot, round):
            s_l.wait(dve, t=t)
            s_lo.by(dve.tensor_tensor(weight[:, bass.ds(t, 1), :, :].rearrange("p o h n -> p (o h) n"),
                                      pL[:, slot % 2, 0:NG].rearrange("p (h n) -> p h n", h=H),
                                      b2[:, :].unsqueeze(1).broadcast_to([P, H, NBR]), ALU.add))

        flow(nc, TILES, [(turn_stats, 4), (gelu, 6), (keep_turned, 2), (keep_logits, 8), (second_layer, 7), (first_layer, 5),
                         (root, 3), (square_and_turn, 1), (hidden_part, 2), (load_gate, 0)], 3)
        barrier()
        s_ld.close()
        q.close()
        p.close()

    with ExitStack() as st:
        mx = sb(st, "mx", [P, TILES * H])
        p = sems.loop(1)
        s_v, s_e = p.step(14), p.step()
        n_v = 0

        def chained(ins):
            nonlocal n_v
            n_v += 1
            s_v.by(ins)
            s_v.wait(dve, n_v)

        w3 = weight[:, :, :, :].rearrange("p t h n -> p (t h) n")
        w4 = weight[:, :, :, :].rearrange("p t h n -> p t (h n)")

        def wide(x):
            return x.unsqueeze(2).broadcast_to([P, TILES * H, NBR])

        chained(dve.tensor_scalar(temp[:, :], temp[:, :], 0.2, 10.0, ALU.max, ALU.min))
        chained(dve.reciprocal(temp[:, :], temp[:, :]))
        chained(dve.tensor_scalar(floor[:, :], floor[:, :], 1e-7, 0.1, ALU.max, ALU.min))
        chained(dve.tensor_tensor(weight[:, :, :, :], weight[:, :, :, :],
                                  temp[:, :].unsqueeze(1).unsqueeze(3).broadcast_to([P, TILES, H, NBR]), ALU.mult))
        chained(dve.tensor_reduce(mx[:, :], w3, AX, ALU.max))
        chained(dve.tensor_tensor(w3, w3, wide(mx[:, :]), ALU.subtract))
        s_v.wait(act, n_v)
        s_e.by(act.activation(w3, w3, ACT.Exp))
        s_e.wait(dve)
        for low in (True, False):
            chained(dve.tensor_reduce(mx[:, :], w3, AX, ALU.add))
            chained(dve.reciprocal(mx[:, :], mx[:, :]))
            chained(dve.tensor_tensor(w3, w3, wide(mx[:, :]), ALU.mult))
            if low:
                chained(dve.tensor_tensor(w4, w4, floor[:, :].unsqueeze(1).broadcast_to([P, TILES, NG]), ALU.max))
        if "w_d" in dbg:
            w_d = dram("w_d", [TOK, NG])
            s_x = p.dma()
            s_v.wait(sp, n_v)
            s_x.by(sp.dma_start(w_d.rearrange("(t p) g -> p t g", p=P), w4))
            s_x.wait(sp)
        s_v.per_turn = n_v
        barrier()
        p.close()

    with ExitStack() as st:
        wo = sb(st, "wo", [P, KT, C])
        gw = sb(st, "gw", [P, KT, NE])
        br = sb(st, "br6", [P, 4, NBR, C])
        xt = sb(st, "xt", [P, 4, C])
        pr = sb(st, "pr", [P, 4, NBR, C])
        mix = sb(st, "mix", [P, 4, C])
        msq = sb(st, "msq", [P, 4, C])
        rr = sb(st, "rr", [P, 4, H])
        on = sb(st, "on", [P, 4, C])
        oT = sb(st, "oT", [P, 2, KT, P])
        x2 = sb(st, "x2", [P, 4, C])
        bn = sb(st, "bn", [P, 4, 6])
        mv = sb(st, "mv", [P, 4, 2])
        h2 = sb(st, "h2", [P, 4, C])
        h2T = sb(st, "h2T", [P, 2, KT, P])
        pO = ps(st, "pO", [P, 2, 512])
        pW = ps(st, "pW", [P, 2, 512])
        pH2 = ps(st, "pH2", [P, 2, 512])
        pg = ps(st, "pg", [P, 2, 512])
        p = sems.loop(1)
        s_w, s_wo = p.dma(2), p.step()
        s_w.by(sp.dma_start(wo[:, :, :], a["Wo"].rearrange("(k p) n -> p k n", p=P)))
        s_w.by(sp.dma_start(gw[:, :, :], a["gate_w"].rearrange("(k p) n -> p k n", p=P)))
        s_w.wait(dve)
        s_w.wait(pe)
        s_wo.by(dve.tensor_scalar(wo[:, :, :], wo[:, :, :], onorm[:, 0:1], None, ALU.mult))
        s_wo.wait(pe)

        q = sems.loop(TILES)
        s_ld, s_xt, s_x2o, s_h2o = [Ring(sems, TILES, n) for n in (NBR, 1, 1, 1)]
        s_pr, s_mx, s_ms, s_r, s_rt, s_rc, s_on = q.step(), q.step(), q.step(), q.step(2), q.step(), q.step(), q.step()
        s_to, s_eo, s_wm, s_ga, s_x2, s_b, s_sr, s_ri, s_n, s_h, s_th, s_eh, s_gm, s_g = (
            q.step(), q.step(), q.step(), q.step(), q.step(), q.step(3), q.step(), q.step(), q.step(), q.step(),
            q.step(), q.step(), q.step(), q.step())

        def row(n, t):
            return rows[:, n, bass.ds(t // (TILES // B), 1), :].rearrange("p o c -> p (o c)")

        def load_branches(t, slot, round):
            s_pr.back(sp, t, 4)
            for n in range(NBR):
                s_ld.by(sp.dma_start(br[:, slot, n, :], branch(n, t)), slot)

        def weigh(t, slot, round):
            s_ld.wait(pool, slot, round)
            s_mx.back(pool, t, 4)
            w = weight[:, bass.ds(t, 1), :, :].rearrange("p o h n -> p n (o h)")
            s_pr.by(pool.tensor_tensor(pr[:, slot, :, :].rearrange("p n (h d) -> p n h d", h=H),
                                       br[:, slot, :, :].rearrange("p n (h d) -> p n h d", h=H),
                                       w.unsqueeze(3).broadcast_to([P, NBR, H, D]), ALU.mult))

        def mix_branches(t, slot, round):
            s_pr.wait(dve, t=t)
            s_on.back(dve, t, 4)
            s_mx.by(dve.tensor_reduce(mix[:, slot, :], pr[:, slot, :, :].rearrange("p n c -> p c n"), AX, ALU.add))
            s_mx.wait(act, t=t)
            s_r.back(act, t, 4)
            s_ms.by(act.activation(msq[:, slot, :], mix[:, slot, :], ACT.Square))

        def mean_square(t, slot, round):
            s_ms.wait(dve, t=t)
            s_r.by(dve.tensor_reduce(rr[:, slot, :], msq[:, slot, :].rearrange("p (h d) -> p h d", h=H), AX, ALU.add))

        def mean_square_root(t, slot, round):
            s_r.wait(dve, 1, t=t)
            s_r.by(dve.tensor_scalar(rr[:, slot, :], rr[:, slot, :], 1.0 / D, EPS_RMS, ALU.mult, ALU.add))
            s_r.wait(act, t=t)
            s_rt.by(act.activation(rr[:, slot, :], rr[:, slot, :], ACT.Sqrt))

        def inverse_root(t, slot, round):
            s_rt.wait(dve, t=t)
            s_rc.by(dve.reciprocal(rr[:, slot, :], rr[:, slot, :]))

        def normalise(t, slot, round):
            s_rc.wait(dve, t=t)
            s_to.back(dve, t, 4)
            s_on.by(dve.tensor_tensor(on[:, slot, :].rearrange("p (h d) -> p h d", h=H),
                                      mix[:, slot, :].rearrange("p (h d) -> p h d", h=H),
                                      rr[:, slot, :].unsqueeze(2).broadcast_to([P, H, D]), ALU.mult))
            s_on.wait(pe, t=t)
            s_eo.back(pe, t, 2)
            for k in range(KT):
                i = pe.transpose(pO[:, slot % 2, k * P:(k + 1) * P], on[:, slot, k * P:(k + 1) * P], ident[:, :])
            s_to.by(i)
            s_x2.back(sp, t, 4)
            s_xt.by(sp.dma_start(xt[:, slot, :], a["x"][bass.ds(t * P, P), :]), slot)

        def project_out(t, slot, round):
            s_to.wait(act, t=t)
            s_wm.back(act, t, 2)
            s_eo.by(act.activation(oT[:, slot % 2, :, :].rearrange("p k t -> p (k t)"), pO[:, slot % 2, 0:C], ACT.Copy))
            s_eo.wait(pe, t=t)
            s_ga.back(pe, t, 2)
            for k in range(KT):
                i = pe.matmul(pW[:, slot % 2, 0:C], oT[:, slot % 2, k, :], wo[:, k, :], start=(k == 0), stop=(k == KT - 1))
            s_wm.by(i)

        def residual(t, slot, round):
            s_wm.wait(dve, t=t)
            s_x2o.free(dve, slot, round)
            s_n.back(dve, t, 4)
            s_ga.by(dve.tensor_tensor(x2[:, slot, :], pW[:, slot % 2, 0:C], row(0, t), ALU.mult))
            s_ga.wait(pool, t=t)
            s_xt.wait(pool, slot, round)
            s_x2.by(pool.tensor_tensor(x2[:, slot, :], x2[:, slot, :], xt[:, slot, :], ALU.add))
            s_x2.wait(sp, t=t)
            s_x2o.by(sp.dma_start(x2_d[bass.ds(t * P, P), :], x2[:, slot, :]), slot)

        def second_stats(t, slot, round):
            s_x2.wait(dve, t=t)
            s_b.by(dve.bn_stats(bn[:, slot, :], x2[:, slot, :]))

        def second_variance(t, slot, round):
            s_b.wait(dve, 1, t=t, alone=True)
            s_b.by(dve.bn_aggr(mv[:, slot, :], bn[:, slot, :]))

        def second_root(t, slot, round):
            s_b.wait(dve, 2, t=t)
            s_b.by(dve.tensor_scalar(mv[:, slot, 1:2], mv[:, slot, 1:2], EPS_LN, None, ALU.add))
            s_b.wait(act, 3, t=t)
            s_sr.by(act.activation(mv[:, slot, 1:2], mv[:, slot, 1:2], ACT.Sqrt))

        def second_inverse(t, slot, round):
            s_sr.wait(dve, t=t)
            s_ri.by(dve.reciprocal(mv[:, slot, 1:2], mv[:, slot, 1:2]))

        def second_norm(t, slot, round):
            s_th.back(dve, t, 4)
            s_h2o.free(dve, slot, round)
            s_n.by(dve.scalar_tensor_tensor(h2[:, slot, :], x2[:, slot, :], mv[:, slot, 0:1], row(2, t), ALU.subtract, ALU.mult))

        def second_modulate(t, slot, round):
            s_ri.wait(dve, t=t)
            s_n.wait(dve, t=t)
            s_h.by(dve.scalar_tensor_tensor(h2[:, slot, :], h2[:, slot, :], mv[:, slot, 1:2], row(1, t), ALU.mult, ALU.add))
            s_h.wait(sp, t=t)
            s_h2o.by(sp.dma_start(h2_d[bass.ds(t * P, P), :], h2[:, slot, :]), slot)

        def router(t, slot, round):
            s_h.wait(pe, t=t)
            s_eh.back(pe, t, 2)
            for k in range(KT):
                i = pe.transpose(pH2[:, slot % 2, k * P:(k + 1) * P], h2[:, slot, k * P:(k + 1) * P], ident[:, :])
            s_th.by(i)
            s_th.wait(act, t=t)
            s_gm.back(act, t, 2)
            s_eh.by(act.activation(h2T[:, slot % 2, :, :].rearrange("p k t -> p (k t)"), pH2[:, slot % 2, 0:C], ACT.Copy))
            s_eh.wait(pe, t=t)
            s_g.back(pe, t, 2)
            for k in range(KT):
                i = pe.matmul(pg[:, slot % 2, 0:NE], h2T[:, slot % 2, k, :], gw[:, k, :], start=(k == 0), stop=(k == KT - 1))
            s_gm.by(i)

        def keep_router(t, slot, round):
            s_gm.wait(dve, t=t)
            s_g.by(dve.tensor_scalar(gates[:, bass.ds(t % TPB, 1), bass.ds(t // TPB, 1), :].rearrange("p o b e -> p (o b e)"),
                                     pg[:, slot % 2, 0:NE], 1e-6, None, ALU.max))

        flow(nc, TILES, [(keep_router, 10), (second_inverse, 8), (inverse_root, 4), (second_norm, 8), (second_stats, 7),
                         (normalise, 4), (second_variance, 7), (second_modulate, 8), (router, 9), (second_root, 7),
                         (residual, 6), (mean_square, 3), (project_out, 5), (mix_branches, 2), (mean_square_root, 3),
                         (weigh, 1), (load_branches, 0)], 3)
        for s in (s_x2o, s_h2o):
            s.wait_all(sp)
        barrier()
        for s in (s_ld, s_xt, s_x2o, s_h2o):
            s.close()
        q.close()
        p.close()
    gate.close()

    R = B * NE
    route = ExitStack()
    top = sb(route, "top", [R, CAP])
    topi = sb(route, "topi", [R, CAP])
    G = sb(route, "G", [R, L])
    m8 = sb(route, "m8", [R, 8])
    i8 = sb(route, "i8", [R, 8], U32)
    with ExitStack() as st:
        cs7 = sb(st, "cs7", [P, R])
        rs7 = sb(st, "rs7", [P, TILES])
        zero = sb(st, "zero", [P, TOK * NE // P])
        pc = ps(st, "pc", [P, R])
        pgt = ps(st, "pgt", [R, 4, 4, P])
        p = sems.loop(1)
        s_z, s_zo = p.step(), p.pool_dma()
        s_z.by(pool.memset(zero[:, :], 0.0))
        s_z.wait(pool)
        s_zo.by(pool.dma_start(key_d.rearrange("(p x) o -> p (x o)", p=P), zero[:, :]))
        q = sems.loop(8)
        s_s, s_cm = q.step(6), q.step()
        g3 = gates[:, :, :, :].rearrange("p t b e -> p t (b e)")
        gr7 = gates[:, :, :, :].rearrange("p t b e -> p (t b) e")
        with nc.Fori(0, 8, engines=[ENG.DVE, ENG.PE]) as i:
            q.it = i
            s_s.by(dve.tensor_reduce(cs7[:, :], g3.rearrange("p t r -> p r t"), AX, ALU.add))
            s_s.wait(pe, 1)
            s_cm.by(pe.matmul(pc[:, :], ones[:, :], cs7[:, :], start=True, stop=True))
            s_cm.wait(dve)
            s_s.by(dve.reciprocal(cs7[:, :], pc[:, :]))
            s_s.wait(dve, 2)
            s_s.by(dve.tensor_tensor(g3, g3, cs7[:, :].unsqueeze(1).broadcast_to([P, TPB, R]), ALU.mult))
            s_s.wait(dve, 3)
            s_s.by(dve.tensor_reduce(rs7[:, :], gr7, AX, ALU.add))
            s_s.wait(dve, 4)
            s_s.by(dve.reciprocal(rs7[:, :], rs7[:, :]))
            s_s.wait(dve, 5)
            s_s.by(dve.tensor_tensor(gr7, gr7, rs7[:, :].unsqueeze(2).broadcast_to([P, TILES, NE]), ALU.mult))
            s_s.wait(dve, 6)
        s_s.wait_all(pe)
        s_t, s_e = p.step(4), p.step(4)
        for j in range(TPB):
            i = pe.transpose(pgt[:, j // 4, j % 4, :], g3[:, j, :], ident[:, :])
            if j % 4 == 3:
                s_t.by(i)
        for w in range(4):
            s_t.wait(dve, w + 1)
            s_e.by(dve.tensor_copy(G[:, w * 512:(w + 1) * 512], pgt[:, w, :, :].rearrange("r t p -> r (t p)")))
        s_e.wait(dve)
        s_zo.wait(pool)
        barrier()
        q.close()
        p.close()

    with ExitStack() as st:
        NH = CAP // P
        exw = sb(st, "exw", [P, KT, NE, C])
        hot = sb(st, "hot", [P, NH, R])
        tokf = sb(st, "tokf", [P, NH, R])
        keyf = sb(st, "keyf", [P, NH, R])
        toku = sb(st, "toku", [P, NH, R], U32)
        keyu = sb(st, "keyu", [P, NH, R], U32)
        keyv = sb(st, "keyv", [P, NH, NE])
        keyi = sb(st, "keyi", [P, NH, NE], mybir.dt.int32)
        cur = sb(st, "cur8", [P, 2, NE], U32)
        idx = sb(st, "idx", [P, 4], U32)
        hc = sb(st, "hc", [P, 4])
        hg = sb(st, "hg", [P, 4, C])
        hgT = sb(st, "hgT", [P, 4, C])
        eo = sb(st, "eo", [P, 4, C])
        pt = ps(st, "pt", [P, 2, NH, R])
        pT8 = ps(st, "pT8", [P, 2, 512])
        pE8 = ps(st, "pE8", [P, 2, 512])
        p = sems.loop(1)
        s_w, s_i, s_kv = p.dma(KT), p.step(), p.step()
        for k in range(KT):
            s_w.by(sp.dma_start(exw[:, k, :, :], a["experts"].rearrange("(e k p) n -> k p e n", k=KT, p=P)[k]))
        s_i.by(pool.iota(keyi[:, :, :], pattern=[[P * NE, NH], [1, NE]], base=1, channel_multiplier=NE))
        s_i.wait(dve)
        s_kv.by(dve.tensor_copy(keyv[:, :, :], keyi[:, :, :]))
        s_kv.wait(pool)
        s_w.wait(pe)
        HT = P // 8
        q2 = sems.loop(NH * HT)
        s_k = q2.step(5)
        s_t = p.step(NH)
        NV = B + NE + 3
        s_v = p.step(NH * NV)
        q5 = sems.loop(NH * B)
        s_cu = q5.step()
        s_sc = Ring(sems, NH * B, NE, 2, pool=True)
        q3 = sems.loop(NH * R)
        s_id, s_hc, s_tr, s_ev, s_mm, s_oe = [q3.step() for _ in range(6)]
        s_ga, s_eo = Ring(sems, NH * R, pool=True), Ring(sems, NH * R)

        def largest(w):
            with nc.Fori(w * HT, (w + 1) * HT, engines=[ENG.DVE]) as i:
                q2.it = i
                s_k.by(dve.max(m8[:, :], G[:, :]))
                s_k.wait(dve, 1, alone=True)
                s_k.by(dve.max_index(i8[:, :], m8[:, :], G[:, :]))
                s_k.wait(dve, 2, alone=True)
                s_k.by(dve.match_replace(G[:, :], m8[:, :], G[:, :], -1.0))
                s_k.by(dve.tensor_copy(top[:, bass.ds(i * 8, 8)], m8[:, :]))
                s_k.by(dve.tensor_copy(topi[:, bass.ds(i * 8, 8)], i8[:, :]))
                s_k.wait(dve, 5)

        def tokens_and_keys(w):
            s_k.wait(pe, t=(w + 1) * HT - 1)
            pe.transpose(pt[:, 0, w, :], topi[:, w * P:(w + 1) * P], ident[0:R, 0:R])
            s_t.by(pe.transpose(pt[:, 1, w, :], top[:, w * P:(w + 1) * P], ident[0:R, 0:R]))
            s_t.wait(dve, w + 1)
            for b in range(B):
                r = slice(b * NE, (b + 1) * NE)
                s_v.by(dve.tensor_scalar(tokf[:, w, r], pt[:, 0, w, r], float(b * L), None, ALU.add))
            s_v.by(dve.tensor_scalar(hot[:, w, :], pt[:, 1, w, :], 0.5, None, ALU.is_gt))
            s_v.wait(dve, w * NV + B + 1)
            for e in range(NE):
                by_e = lambda x: x[:, w, :].rearrange("p (b e) -> p b e", b=B)[:, :, e]
                s_v.by(dve.tensor_scalar(by_e(keyf), by_e(tokf), float(NE), float(e), ALU.mult, ALU.add))
            s_v.by(dve.tensor_copy(toku[:, w, :], tokf[:, w, :]))
            s_v.wait(dve, w * NV + NV - 1)
            s_v.by(dve.tensor_copy(keyu[:, w, :], keyf[:, w, :]))
            s_v.wait(pool, (w + 1) * NV)

        def ranks_out(w):
            def scatter(b, slot, round):
                b, b0, round = b + w * B, b, round + w * B // 2
                s_sc.free(pool, slot, round)
                s_cu.by(pool.tensor_copy(cur[:, slot, :], keyu[:, w, bass.ds(b0 * NE, NE)]))
                s_cu.wait(pool, t=b)
                for e in range(NE):
                    s_sc.by(pool.indirect_dma_start(key_d, bass.IndirectOffsetOnAxis(ap=cur[:, slot, e:e + 1], axis=0),
                                                    keyv[:, w, e:e + 1], None), slot)

            flow(nc, B, oldest_first(scatter), 1, 2, [ENG.Pool])

        def experts(w):
            T0 = w * R

            def gather(t, slot, round):
                round = round + T0 // 4
                s_ga.free(pool, slot, round)
                s_id.by(pool.tensor_copy(idx[:, slot:slot + 1], toku[:, w, bass.ds(t, 1)]))
                s_oe.back(pool, t + T0, 4)
                s_hc.by(pool.tensor_copy(hc[:, slot:slot + 1], hot[:, w, bass.ds(t, 1)]))
                s_id.wait(pool, t=t + T0)
                s_tr.back(pool, t + T0, 4)
                s_ga.by(pool.indirect_dma_start(hg[:, slot, :], None, h2_d,
                                                bass.IndirectOffsetOnAxis(ap=idx[:, slot:slot + 1], axis=0)), slot)

            def turn_gathered(t, slot, round):
                s_ga.wait(pe, slot, round + T0 // 4)
                s_ev.back(pe, t + T0, 2)
                for k in range(KT):
                    i = pe.transpose(pT8[:, slot % 2, k * P:(k + 1) * P], hg[:, slot, k * P:(k + 1) * P], ident[:, :])
                s_tr.by(i)

            def keep_gathered(t, slot, round):
                s_tr.wait(act, t=t + T0)
                s_mm.back(act, t + T0, 4)
                s_ev.by(act.activation(hgT[:, slot, :], pT8[:, slot % 2, 0:C], ACT.Copy))

            def expert(t, slot, round):
                s_ev.wait(pe, t=t + T0)
                s_oe.back(pe, t + T0, 2)
                for k in range(KT):
                    i = pe.matmul(pE8[:, slot % 2, 0:C], hgT[:, slot, k * P:(k + 1) * P],
                                  exw[:, k, bass.ds(t % NE, 1), :].rearrange("p o n -> p (o n)"), start=(k == 0), stop=(k == KT - 1))
                s_mm.by(i)

            def keep_expert(t, slot, round):
                s_mm.wait(act, t=t + T0)
                s_hc.wait(act, t=t + T0)
                s_eo.free(act, slot, round + T0 // 4)
                s_oe.by(act.activation(eo[:, slot, :], pE8[:, slot % 2, 0:C], ACT.Copy, scale=hc[:, slot:slot + 1]))
                s_oe.wait(sp, t=t + T0)
                dst = bass.AP(routed_d.tensor, ((t // NE) * (CAP * NE) + (t % NE) + w * P * NE) * C, [[NE * C, P], [1, C]])
                s_eo.by(sp.dma_start(dst, eo[:, slot, :]), slot)

            flow(nc, R, [(keep_expert, 4), (keep_gathered, 3), (expert, 3), (turn_gathered, 2), (gather, 0)], 2,
                 engines=[ENG.Pool, ENG.PE, ENG.Activation, ENG.SP])

        for w in range(NH):
            if w == 0:
                largest(0)
            tokens_and_keys(w)
            if w == 0:
                largest(1)
            ranks_out(w)
            experts(w)
        s_sc.wait_all(sp)
        s_eo.wait_all(pool)
        keys = sb(st, "keys", [P, TILES, NE])
        won = sb(st, "won", [P, TILES])
        mask = sb(st, "mask", [P, TILES])
        rowu = sb(st, "rowu", [P, TILES], U32)
        s_kl = p.dma()
        s_kl.by(sp.dma_start(keys[:, :, :], key_d.rearrange("(t p e) o -> p t (e o)", p=P, e=NE)))
        s_kl.wait(dve)
        s_n = p.step(2 + B + 1)
        s_n.by(dve.tensor_reduce(won[:, :], keys[:, :, :], AX, ALU.max))
        s_n.wait(dve, 1)
        s_n.by(dve.tensor_scalar(mask[:, :], won[:, :], 1.0, None, ALU.min))
        s_n.wait(dve, 2)
        for b in range(B):
            r = slice(b * TILES // B, (b + 1) * TILES // B)
            s_n.by(dve.tensor_scalar(won[:, r], won[:, r], 1.0, float(b * L + 1), ALU.max, ALU.add))
        s_n.wait(dve, 2 + B)
        s_n.by(dve.tensor_scalar(rowu[:, :], won[:, :], -2.0, None, ALU.add))
        s_n.wait(dve)

        ix = sb(st, "ix", [P, 4], U32)
        og = sb(st, "og", [P, 4, C])
        xr = sb(st, "xr", [P, 4, C])
        y = sb(st, "y9", [P, 4, C])
        q4 = sems.loop(TILES)
        s_ix, s_o, s_fy = q4.step(), q4.step(), q4.step()
        s_og, s_xr, s_y = Ring(sems, TILES, pool=True), Ring(sems, TILES), Ring(sems, TILES)

        def fetch(t, slot, round):
            s_og.free(dve, slot, round)
            s_ix.by(dve.tensor_copy(ix[:, slot:slot + 1], rowu[:, bass.ds(t, 1)]))
            s_ix.wait(pool, t=t)
            s_o.back(pool, t, 4)
            s_og.by(pool.indirect_dma_start(og[:, slot, :], None, routed_d,
                                            bass.IndirectOffsetOnAxis(ap=ix[:, slot:slot + 1], axis=0)), slot)
            s_fy.back(sp, t, 4)
            s_xr.by(sp.dma_start(xr[:, slot, :], x2_d[bass.ds(t * P, P), :]), slot)

        def finish(t, slot, round):
            s_og.wait(dve, slot, round)
            s_y.free(dve, slot, round)
            s_o.by(dve.scalar_tensor_tensor(y[:, slot, :], og[:, slot, :], mask[:, bass.ds(t, 1)], row(3, t), ALU.mult, ALU.mult))
            s_xr.wait(dve, slot, round)
            s_o.wait(dve, t=t)
            s_fy.by(dve.tensor_tensor(y[:, slot, :], y[:, slot, :], xr[:, slot, :], ALU.add))
            s_fy.wait(act, t=t)
            s_y.by(act.dma_start(out[bass.ds(t * P, P), :], y[:, slot, :]), slot)

        flow(nc, TILES, oldest_first(fetch, None, None, finish), 2)
        s_y.wait_all(sp)
        barrier()
    route.close()
    whole.close()



INS = {"x": "L0_attn_x", "Wq": "L0_attn_Wq", "Wk": "L0_attn_Wk", "Wv": "L0_attn_Wv", "Wb": "L0_attn_Wb",
       "qc": "L0_attn_qc_w", "kc": "L0_attn_kc_w", "vc": "L0_attn_vc_w", "fir_s": "L0_attn_fir_s",
       "fir_l": "L0_attn_fir_l", "gW1": "L0_attn_gW1", "gb1": "L0_attn_gb1", "gW2": "L0_attn_gW2",
       "gb2": "L0_attn_gb2", "temp": "L0_attn_temp", "floor": "L0_attn_eps_floor",
       "onorm": "L0_attn_onorm_w", "Wo": "L0_attn_Wo", "gate_w": "L0_ffn_gate_w",
       "experts": "L0_ffn_experts", "cT": "L0_c", "wmod": "L0_wmod"}


def lay_out(inputs):
    import numpy as np
    shape = {"x": (TOK, C), "fir_s": (C, FIRS), "fir_l": (C, FIRL), "gb1": (P, 1), "gb2": (1, 4), "temp": (1, H),
             "floor": (1, 16), "onorm": (1, D), "gate_w": (C, NE), "experts": (NE * C, C)}
    got = {}
    for name, full in INS.items():
        v = np.asarray(inputs[full])
        if name in shape:
            v = v.reshape(shape[name])
        if name == "cT":
            v = v.T
        got[name] = np.ascontiguousarray(v)
    return got


def kernel(**inputs):
    import concourse.bacc as bacc
    from concourse.bass_utils import run_bass_kernel_spmd

    nc = bacc.Bacc("TRN2", target_bir_lowering=False, num_devices=1)
    arrays = lay_out(inputs)
    a = {n: nc.dram_tensor(f"in_{n}", list(v.shape), F32, kind="ExternalInput").ap() for n, v in arrays.items()}
    out = nc.dram_tensor("y", [TOK, C], F32, kind="ExternalOutput").ap()
    build(nc, a, out)
    r = run_bass_kernel_spmd(nc, [{f"in_{n}": v for n, v in arrays.items()}], core_ids=[0])
    return r.results[0]["y"].reshape(B, L, C)
```
